# Optimizing a Trainium2 kernel written in Bass

```python
import numpy as np
import jax
import jax.numpy as jnp

def _softmax(x, axis=-1):
    return jax.nn.softmax(x, axis=axis)

def _gelu(x):
    return jax.nn.gelu(x, approximate=True)

def _silu(x):
    return jax.nn.silu(x)

def _sigmoid(x):
    return jax.nn.sigmoid(x)

def _layernorm(x, axis=-1, eps=1e-05):
    m = jnp.mean(x, axis=axis, keepdims=True)
    v = jnp.var(x, axis=axis, keepdims=True)
    return (x - m) / jnp.sqrt(v + eps)

def _scatter_add(tgt, idx, src, axis=0):
    return tgt.at[idx].add(src)

def _segment_sum(src, seg, n):
    return jax.ops.segment_sum(src, seg, n)
kernel_name = 'mk_lm_tower_d1_tok_ids256_r4_1c4cf9'

def setup_inputs(seed: int=0):
    np.random.seed(seed)
    _w = jnp.asarray

    def _rec_inputs():
        import jax
        import jax.numpy as jnp
        _rk = jax.random.key(seed)
        x = jax.random.randint(jax.random.fold_in(_rk, 1), (8, 256), 0, 64, jnp.int32)
        return x
    x = _rec_inputs()

    def _L0_tok_setup():
        import jax, jax.numpy as jnp
        import numpy as np
        from jax import lax
        E, H, NL, K, NCH, V = (32, 64, 6, 3, 4, 64)
        B, L = (16, 4096)

        def _causal_conv(x, w, b, dilation):
            k = w.shape[2]
            out = lax.conv_general_dilated(x, w, window_strides=(1,), padding=[((k - 1) * dilation, 0)], rhs_dilation=(dilation,), dimension_numbers=('NCH', 'OIH', 'NCH'))
            return out + b[None, :, None]
        key = jax.random.key(seed)
        ks = jax.random.split(key, 16)
        s_e = 1.0 / np.sqrt(E)
        s_h = 1.0 / np.sqrt(H)
        s_c = 1.0 / np.sqrt(H * K)
        return {'byte_sequence': jax.random.randint(ks[0], (B, L), 0, V, dtype=jnp.int64), 'channel_id': 0, 'byte_embed': jax.random.normal(ks[1], (V, E), jnp.float32), 'channel_embed': jax.random.normal(ks[2], (NCH, E), jnp.float32), 'start_token': jax.random.normal(ks[3], (E,), jnp.float32), 'in_w': jax.random.normal(ks[4], (H, E), jnp.float32) * s_e, 'in_b': jnp.zeros((H,), jnp.float32), 'conv_w': jax.random.normal(ks[5], (NL, H, H, K), jnp.float32) * s_c, 'conv_b': jnp.zeros((NL, H), jnp.float32), 'pw_w': jax.random.normal(ks[6], (NL, H, H), jnp.float32) * s_h, 'pw_b': jnp.zeros((NL, H), jnp.float32), 'out1_w': jax.random.normal(ks[7], (H, H), jnp.float32) * s_h, 'out1_b': jnp.zeros((H,), jnp.float32), 'out2_w': jax.random.normal(ks[8], (V, H), jnp.float32) * s_h, 'out2_b': jnp.zeros((V,), jnp.float32)}
    _L0_tok_all = _L0_tok_setup()
    _L0_tok_in = {k: v for k, v in _L0_tok_all.items() if k in ('byte_embed', 'channel_embed', 'start_token', 'in_w', 'in_b', 'conv_w', 'conv_b', 'pw_w', 'pw_b', 'out1_w', 'out1_b', 'out2_w', 'out2_b')}
    del _L0_tok_all

    def _L0_attn_setup():
        import jax, jax.numpy as jnp
        import numpy as np
        key = jax.random.key(seed)
        k1, k2, k3 = jax.random.split(key, 3)
        b, n_t, n, n_h = (8, 256, 64, 8)
        s = jax.random.normal(k1, (b, n_t, n), dtype=jnp.float32)
        Q = jax.random.normal(k2, (n_h, n, n), dtype=jnp.float32) * 0.02
        E = jax.random.normal(k3, (n_h, n, n), dtype=jnp.float32) * 0.02
        return {'s': s, 'Q': Q, 'E': E}
    _L0_attn_all = _L0_attn_setup()
    _L0_attn_in = {k: v for k, v in _L0_attn_all.items() if k in ('Q', 'E')}
    del _L0_attn_all

    def _L0_ffn_setup():
        import jax, jax.numpy as jnp
        import numpy as np
        B, T, C = (64, 96, 64)
        NH, NKV = (4, 2)
        HD = C // NH
        NREP = NH // NKV
        NE, TOPK = (8, 2)
        HID = int(8 / 3 * C)
        EPS_RMS = 1e-06

        def _rope_tables(t_len):
            inv_freq = 1.0 / 10000.0 ** (np.arange(0, HD, 2, dtype=np.float32) / HD)
            t = np.arange(t_len, dtype=np.float32)
            freqs = np.outer(t, inv_freq)
            emb = np.concatenate([freqs, freqs], axis=-1)
            return (jnp.asarray(np.cos(emb)), jnp.asarray(np.sin(emb)))

        def _rotate_half(x):
            h = x.shape[-1] // 2
            return jnp.concatenate([-x[..., h:], x[..., :h]], axis=-1)

        def _rmsnorm(v, w):
            return v * jax.lax.rsqrt(jnp.mean(v * v, axis=-1, keepdims=True) + EPS_RMS) * w
        key = jax.random.key(seed)
        ks = jax.random.split(key, 10)
        s = lambda k, shape: jax.random.normal(k, shape, jnp.float32) * 0.02
        return {'x': jax.random.normal(ks[0], (B, T, C), jnp.float32), 'ln1_w': jnp.ones((C,), jnp.float32), 'ln2_w': jnp.ones((C,), jnp.float32), 'wq': s(ks[1], (NH * HD, C)), 'wk': s(ks[2], (NKV * HD, C)), 'wv': s(ks[3], (NKV * HD, C)), 'wo': s(ks[4], (C, C)), 'router_w': s(ks[5], (NE, C)), 'w1': s(ks[6], (NE, HID, C)), 'w2': s(ks[7], (NE, C, HID)), 'w3': s(ks[8], (NE, HID, C))}
    _L0_ffn_all = _L0_ffn_setup()
    _L0_ffn_in = {k: v for k, v in _L0_ffn_all.items() if k in ('ln1_w', 'ln2_w', 'wq', 'wk', 'wv', 'wo', 'router_w', 'w1', 'w2', 'w3')}
    del _L0_ffn_all
    return {'x': x, 'L0_tok_byte_embed': _L0_tok_in['byte_embed'], 'L0_tok_channel_embed': _L0_tok_in['channel_embed'], 'L0_tok_start_token': _L0_tok_in['start_token'], 'L0_tok_in_w': _L0_tok_in['in_w'], 'L0_tok_in_b': _L0_tok_in['in_b'], 'L0_tok_conv_w': _L0_tok_in['conv_w'], 'L0_tok_conv_b': _L0_tok_in['conv_b'], 'L0_tok_pw_w': _L0_tok_in['pw_w'], 'L0_tok_pw_b': _L0_tok_in['pw_b'], 'L0_tok_out1_w': _L0_tok_in['out1_w'], 'L0_tok_out1_b': _L0_tok_in['out1_b'], 'L0_tok_out2_w': _L0_tok_in['out2_w'], 'L0_tok_out2_b': _L0_tok_in['out2_b'], 'L0_attn_Q': _L0_attn_in['Q'], 'L0_attn_E': _L0_attn_in['E'], 'L0_ffn_ln1_w': _L0_ffn_in['ln1_w'], 'L0_ffn_ln2_w': _L0_ffn_in['ln2_w'], 'L0_ffn_wq': _L0_ffn_in['wq'], 'L0_ffn_wk': _L0_ffn_in['wk'], 'L0_ffn_wv': _L0_ffn_in['wv'], 'L0_ffn_wo': _L0_ffn_in['wo'], 'L0_ffn_router_w': _L0_ffn_in['router_w'], 'L0_ffn_w1': _L0_ffn_in['w1'], 'L0_ffn_w2': _L0_ffn_in['w2'], 'L0_ffn_w3': _L0_ffn_in['w3']}

def reference(x, L0_tok_byte_embed, L0_tok_channel_embed, L0_tok_start_token, L0_tok_in_w, L0_tok_in_b, L0_tok_conv_w, L0_tok_conv_b, L0_tok_pw_w, L0_tok_pw_b, L0_tok_out1_w, L0_tok_out1_b, L0_tok_out2_w, L0_tok_out2_b, L0_attn_Q, L0_attn_E, L0_ffn_ln1_w, L0_ffn_ln2_w, L0_ffn_wq, L0_ffn_wk, L0_ffn_wv, L0_ffn_wo, L0_ffn_router_w, L0_ffn_w1, L0_ffn_w2, L0_ffn_w3):
    import jax
    import jax.numpy as jnp

    def _L0_tok_ref(byte_sequence, channel_id, byte_embed, channel_embed, start_token, in_w, in_b, conv_w, conv_b, pw_w, pw_b, out1_w, out1_b, out2_w, out2_b):
        import jax, jax.numpy as jnp
        import numpy as np
        from jax import lax
        E, H, NL, K, NCH, V = (32, 64, 6, 3, 4, 64)
        B, L = (16, 4096)

        def _causal_conv(x, w, b, dilation):
            k = w.shape[2]
            out = lax.conv_general_dilated(x, w, window_strides=(1,), padding=[((k - 1) * dilation, 0)], rhs_dilation=(dilation,), dimension_numbers=('NCH', 'OIH', 'NCH'))
            return out + b[None, :, None]
        Bb, Ll = byte_sequence.shape
        emb = byte_embed[byte_sequence]
        start = jnp.broadcast_to(start_token[None, None, :], (Bb, 1, emb.shape[-1]))
        shifted = jnp.concatenate([start, emb[:, :-1]], axis=1)
        xin = shifted + channel_embed[channel_id][None, None, :]
        x = jnp.einsum('ble,he->bhl', xin, in_w) + in_b[None, :, None]
        n_layers = conv_w.shape[0]
        for i in range(n_layers):
            h = jax.nn.gelu(_causal_conv(x, conv_w[i], conv_b[i], 2 ** i), approximate=False)
            h = jax.nn.gelu(jnp.einsum('bhl,oh->bol', h, pw_w[i]) + pw_b[i][None, :, None], approximate=False)
            x = x + h
        h = jax.nn.gelu(jnp.einsum('bhl,oh->bol', x, out1_w) + out1_b[None, :, None], approximate=False)
        logits = jnp.einsum('bhl,oh->bol', h, out2_w) + out2_b[None, :, None]
        logits = jnp.transpose(logits, (0, 2, 1))
        return jax.nn.log_softmax(logits, axis=-1)

    def _L0_attn_ref(s, Q, E):
        import jax, jax.numpy as jnp
        import numpy as np
        n_t = s.shape[1]
        qs = jnp.einsum('bti,hij->bhtj', s, Q)
        Omega = jnp.einsum('bhtj,buj->bhtu', qs, s)
        mask = jnp.tril(jnp.ones((n_t, n_t), dtype=s.dtype))
        Omega = Omega * mask
        es = jnp.einsum('hij,buj->bhui', E, s)
        r = jnp.einsum('bhtu,bhui->bti', Omega, es)
        return r

    def _L0_ffn_ref(x, ln1_w, ln2_w, wq, wk, wv, wo, router_w, w1, w2, w3):
        import jax, jax.numpy as jnp
        import numpy as np
        B, T, C = (64, 96, 64)
        NH, NKV = (4, 2)
        HD = C // NH
        NREP = NH // NKV
        NE, TOPK = (8, 2)
        HID = int(8 / 3 * C)
        EPS_RMS = 1e-06

        def _rope_tables(t_len):
            inv_freq = 1.0 / 10000.0 ** (np.arange(0, HD, 2, dtype=np.float32) / HD)
            t = np.arange(t_len, dtype=np.float32)
            freqs = np.outer(t, inv_freq)
            emb = np.concatenate([freqs, freqs], axis=-1)
            return (jnp.asarray(np.cos(emb)), jnp.asarray(np.sin(emb)))

        def _rotate_half(x):
            h = x.shape[-1] // 2
            return jnp.concatenate([-x[..., h:], x[..., :h]], axis=-1)

        def _rmsnorm(v, w):
            return v * jax.lax.rsqrt(jnp.mean(v * v, axis=-1, keepdims=True) + EPS_RMS) * w
        Bx, Tx, Cx = x.shape
        h = _rmsnorm(x, ln1_w)
        q = (h @ wq.T).reshape(Bx, Tx, NH, HD).transpose(0, 2, 1, 3)
        k = (h @ wk.T).reshape(Bx, Tx, NKV, HD).transpose(0, 2, 1, 3)
        v = (h @ wv.T).reshape(Bx, Tx, NKV, HD).transpose(0, 2, 1, 3)
        cos, sin = _rope_tables(Tx)
        cos, sin = (cos[None, None], sin[None, None])
        q = q * cos + _rotate_half(q) * sin
        k = k * cos + _rotate_half(k) * sin
        k = jnp.repeat(k, NREP, axis=1)
        v = jnp.repeat(v, NREP, axis=1)
        scores = jnp.einsum('bhtd,bhsd->bhts', q, k) / jnp.sqrt(jnp.float32(HD))
        causal = jnp.tril(jnp.ones((Tx, Tx), dtype=bool))
        scores = jnp.where(causal[None, None], scores, jnp.float32(-1e+30))
        att = jax.nn.softmax(scores, axis=-1)
        y = jnp.einsum('bhts,bhsd->bhtd', att, v).transpose(0, 2, 1, 3).reshape(Bx, Tx, Cx)
        x = x + y @ wo.T
        flat = _rmsnorm(x, ln2_w).reshape(-1, Cx)
        probs = jax.nn.softmax(flat @ router_w.T, axis=-1)
        tp, ti = jax.lax.top_k(probs, TOPK)
        tp = tp / (jnp.sum(tp, axis=-1, keepdims=True) + 1e-09)
        weights = jnp.sum(tp[..., None] * jax.nn.one_hot(ti, NE, dtype=flat.dtype), axis=1)
        out = jnp.zeros_like(flat)
        for e in range(NE):
            hh = jax.nn.silu(flat @ w1[e].T) * (flat @ w3[e].T)
            out = out + weights[:, e:e + 1] * (hh @ w2[e].T)
        return x + out.reshape(Bx, Tx, Cx)
    h = _L0_tok_ref(x, 0, L0_tok_byte_embed, L0_tok_channel_embed, L0_tok_start_token, L0_tok_in_w, L0_tok_in_b, L0_tok_conv_w, L0_tok_conv_b, L0_tok_pw_w, L0_tok_pw_b, L0_tok_out1_w, L0_tok_out1_b, L0_tok_out2_w, L0_tok_out2_b)
    h = h + _L0_attn_ref(_layernorm(h, axis=-1), L0_attn_Q, L0_attn_E)
    h = h + _L0_ffn_ref(_layernorm(h, axis=-1), L0_ffn_ln1_w, L0_ffn_ln2_w, L0_ffn_wq, L0_ffn_wk, L0_ffn_wv, L0_ffn_wo, L0_ffn_router_w, L0_ffn_w1, L0_ffn_w2, L0_ffn_w3)
    return h

_drawn_inputs = setup_inputs


def setup_inputs(seed=0):
    import zlib

    import numpy as np

    out = dict(_drawn_inputs(seed))
    spreads = {'L0_tok_in_b': (0.0, 0.1),
     'L0_tok_conv_b': (0.0, 0.1),
     'L0_tok_pw_b': (0.0, 0.1),
     'L0_tok_out1_b': (0.0, 0.1),
     'L0_tok_out2_b': (0.0, 0.1),
     'L0_ffn_ln1_w': (1.0, 0.6),
     'L0_ffn_ln2_w': (1.0, 0.6)}
    factors = {'L0_tok_start_token': 4.532,
     'L0_ffn_wq': 8.0,
     'L0_ffn_wk': 8.0,
     'L0_ffn_wv': 8.0,
     'L0_ffn_wo': 8.0,
     'L0_ffn_router_w': 8.0,
     'L0_ffn_w1': 8.0,
     'L0_ffn_w2': 8.0,
     'L0_ffn_w3': 8.0}
    for name, (base, spread) in spreads.items():
        noise = np.random.default_rng([zlib.crc32(name.encode()), seed]).standard_normal(out[name].shape)
        drawn = base * np.exp(spread * noise) if base else spread * noise
        out[name] = jnp.asarray(drawn.astype(out[name].dtype))
    for name, factor in factors.items():
        out[name] = (out[name] * factor).astype(out[name].dtype)
    return out
```

```python
import concourse.bass as bass
from concourse import mybir
from contextlib import ExitStack
import numpy as np

B, T, C, V, EMB = 8, 256, 64, 64, 32
LAYERS, TAPS, PAD = 6, 3, 64
HEADS = 8
NH, NKV, HD = 4, 2, 16
NE, HID, MAIN = 8, 170, 128
REM = HID - MAIN
PAIRS, TILES, P = 4, 16, 128
CH = NE + NE // 2
NEG = -1e30
ATT_SCALE, FFN_SCALE = 64.0, 16.0


def tower(nc, x, tcn_w, tcn_b, out2_b, emb, in_b, attn_q, attn_e, qkv_w, wo_t, ln1, ln2, router,
          w1m, w1r, w3m, w3r, w2m, w2r, cos_t, sin_t, out):
    f32, f16, bf16, i32 = mybir.dt.float32, mybir.dt.float16, mybir.dt.bfloat16, mybir.dt.int32
    ALU = mybir.AluOpType
    ACT = mybir.ActivationFunctionType
    AX = mybir.AxisListType.X
    NBLK = 3 * LAYERS + LAYERS + 2

    ctx = ExitStack()
    with ctx:
        def sb(name, shape, dt=f32):
            return ctx.enter_context(nc.sbuf_tensor(name, shape, dt))

        def sem(name):
            return ctx.enter_context(nc.semaphore(name))

        bank = [ctx.enter_context(nc.psum_tensor(f"bank{i}", [P, 512], f32)) for i in range(8)]

        NW, NX = NBLK * P, 4 * (PAD + T)
        early = sb("early", [P, NW + NX + 2048])
        Wt = early[:, 0:NW].rearrange("p (n o) -> p n o", o=P)
        Xp = early[:, NW:NW + NX].rearrange("p (b t) -> p b t", b=4)
        hid1 = early[:, NW + NX:NW + NX + 1024].rearrange("p (a c) -> p a c", a=2)
        hid2 = early[:, NW + NX + 1024:NW + NX + 2048].rearrange("p (a c) -> p a c", a=2)
        qkT = early[0:96, 0:TILES * 6 * P // 2].bitcast(bf16).rearrange("p (g n t) -> p g n t", n=6, t=P)
        bt = sb("bt", [P, 2 * LAYERS + 1])
        b2bc = sb("b2bc", [P, V])
        idx = sb("idx", [P, 4, T], i32)
        onehot = sb("onehot", [P, 4, T])
        vcol_i = sb("vcol_i", [P, 1], i32)
        vcol = sb("vcol", [P, 1])
        embp = sb("embp", [EMB + 1, 2 * V + 2])
        embc = sb("embc", [EMB + 1, 2, V])
        inw2 = sb("inw2", [EMB + 1, 2, C])
        startc = sb("startc", [EMB + 1, 1])
        table = sb("table", [P, P])
        identf = sb("identf", [P, P])
        ident16 = sb("ident16", [P, P], f16)
        identb = sb("identb", [P, P], bf16)
        trimul = sb("trimul", [P, 64])
        mask_t = sb("mask_t", [P, 4, P], bf16)
        mask_t2 = sb("mask_t2", [P, 2, T], bf16)
        mask_s = sb("mask_s", [P, 4, P], bf16)
        mask_s2 = sb("mask_s2", [P, 2, T], bf16)
        selh = sb("selh", [3 * NH, NH, P], bf16)
        neghalf = sb("neghalf", [P, 4])
        L = sb("L", [P, TILES, V])
        h = sb("h", [P, TILES, V])
        cen = sb("cen", [P, 2, 4, V])
        sqr = sb("sqr", [P, 2, 4, V])
        ex = sb("ex", [P, 2, 4, V])
        stat = sb("stat", [P, 12, TILES])
        s2 = sb("s2", [P, 2, 4, 2, V])
        shl = sb("shl", [P, 2, 4, 2, V], f16)
        qw = sb("qw", [P, 4, P])
        qwh = sb("qwh", [P, 2, 4, P], f16)
        ew = sb("ew", [P, 4, C])
        sTs = sb("sTs", [P, TILES, P], f16)
        shared = sb("shared", [P, 2 * CH * 512])
        bdT = shared[:, 0:4096].rearrange("p (n u) -> p n u", u=P)
        bdS = shared[:, 4096:8192].rearrange("p (n u) -> p n u", u=P)
        bdM = shared[:, 8192:11264].rearrange("p (b k u) -> p b k u", k=3, u=P)
        om = shared[:, 11264:12288].rearrange("p (a c) -> p a c", a=2)
        hh = shared[:, :].rearrange("p (a j c) -> p a j c", a=2, j=CH)
        qT = sb("qT", [P, 2, 4, 512])
        oT = sb("oT", [P, 2, 4, P])
        xf = sb("xf", [P, TILES, C])
        hx = sb("hx", [P, TILES, C])
        qkvw = sb("qkvw", [P, P])
        qkvh = sb("qkvh", [P, 2, P], f16)
        lns = sb("lns", [P, 2])
        wo_sb = sb("wo_sb", [C, C])
        cos4 = sb("cos4", [P, 4, 96])
        sin4 = sb("sin4", [P, 4, 96])
        hTs = sb("hTs", [P, TILES, P], f16)
        rope = sb("rope", [P, 4, 96])
        rot = sb("rot", [P, 4, 96])
        qst = sb("qst", [P, 2, 4, 6, 6, HD], bf16)
        vaug = sb("vaug", [P, TILES, NKV, HD + 1])
        nmx = sb("nmx", [P, TILES, NH])
        nmr = sb("nmr", [P, 2, 2, NH])
        nms = sb("nms", [P, 2, 2, NH, 3], bf16)
        nmT = sb("nmT", [3 * NH, 2, 2, P], bf16)
        pT = qT[:, :, 0:3, :]
        rec = sb("rec", [P, 2, 2, NH])
        y = sb("y", [P, 2, 2, NH, HD])
        yT = sb("yT", [C, 2, 2, P])
        rw = sb("rw", [P, NE])
        rwh = sb("rwh", [P, 2, NE], f16)
        w1s = sb("w1s", [P, CH, P])
        w1h = sb("w1h", [P, 2, CH, P], f16)
        w3h = sb("w3h", [P, 2, CH, P], f16)
        w2s = sb("w2s", [P, NE, C])
        w2x = sb("w2x", [P, NE // 2, P])
        x2 = idx[:, :, :].rearrange("p a b -> p (a b)").bitcast(f32).rearrange("p (g c) -> p g c", c=C)
        fTs = onehot[:, :, :].rearrange("p a b -> p (a b)").bitcast(f16).rearrange("p (g c) -> p g c", c=P)
        lg = sb("lg", [P, 4, NE])
        ge = sb("ge", [P, 4, NE, NE])
        gt = sb("gt", [P, 4, NE, NE])
        lowidx = sb("lowidx", [P, NE, NE])
        gate = sb("gate", [P, TILES, NE])
        sil = qT[:, :, 3, :]
        moe = sb("moe", [P, 2, NE, C])
        fin = L

        names = ["ld_tok", "ld_emb", "ld_tcn0", "ld_tcn1", "ld_attn", "ld_ffn", "ld_w1", "ld_w3", "ld_w2", "stored",
                 "gchain", "consts", "memz", "bd_zero", "vchain", "achain", "embc_ready", "table_ps", "table_ready",
                 "onehot_ready", "emb_ps", "x_ready", "conv_ps", "hid_ready", "pw_ps", "pw_gelu", "out1_ps",
                 "logits_ps", "logits_read", "lsub_ready", "exp_ready", "lsum_ready", "ln_ready", "var_ready", "rstd_ready",
                 "s_ready", "shl_ready", "h_ready", "tr32_ps", "tr16_ps", "sTs_ready", "bdT_ready", "bdS_ready",
                 "M_ps", "M_ready", "q_ps", "q_ready", "om_ps", "om_ready", "o_ps", "o_ready", "e_ps", "h2_ready",
                 "var2_ready", "rstd2_ready", "q1_ready", "rinv_ready", "hr_ready", "hsplit_ready", "trh_ps", "hTs_ready",
                 "qkv_ps", "rope_ready", "v_ready", "split_ready", "stk_ps", "stk_ready", "p1_ps", "max_ready",
                 "nms_ready", "nmT_ps", "nmT_ready", "p2_ps", "exp2_ready", "y_ps", "y_ready", "yT_ps", "yT_ready",
                 "wo_ps", "x2_ready", "ss_ready", "r2_ready", "fs_ready", "fsplit_ready", "trf_ps", "fTs_ready",
                 "rt_ps", "rexp_in", "rexp_ready", "gate_ready", "a_ps", "b_ps", "sil_ready", "hh_ready", "w2_ps",
                 "mix_ready", "fin_ready", "wts_ready", "wts2_ready", "w1cast", "emb_w"]
        S = {n: sem(n) for n in names}

        block = ctx.enter_context(nc.Block())

        def xrows(half):
            return x[4 * half:4 * half + 4, 0:T - 1]

        @block.sync
        def _(sp):
            for half in range(2):
                sp.dma_start(idx[64 * half:64 * half + 64, :, 1:T],
                             xrows(half).unsqueeze(0).to_broadcast([64, 4, T - 1])).then_inc(S["ld_tok"], 16)
            sp.dma_start(embp[0:EMB, :], emb[:, :]).then_inc(S["ld_emb"], 16)
            sp.dma_start(embp[EMB:EMB + 1, V:2 * V], in_b[:, :]).then_inc(S["ld_emb"], 16)
            sp.wait_ge(S["bd_zero"], 1)
            tw = tcn_w.rearrange("c (n o) -> c n o", o=C)
            for lo, hi, s in ((0, 3, "ld_tcn0"), (3, NBLK, "ld_tcn1")):
                for half in range(2):
                    q = slice(64 * half, 64 * half + 64)
                    sp.dma_start(Wt[q, lo:hi, q], tw[:, lo:hi, :]).then_inc(S[s], 16)
                if lo == 0:
                    for half in range(2):
                        sp.dma_start(bt[64 * half:64 * half + 64, :], tcn_b[:, :]).then_inc(S[s], 16)
            sp.dma_start(b2bc[:, :], out2_b[:, :].to_broadcast([P, V])).then_inc(S["ld_tcn1"], 16)
            for half in range(2):
                q = slice(64 * half, 64 * half + 64)
                sp.dma_start(qw[q, :, :], attn_q.rearrange("c (a m) -> c a m", m=P)).then_inc(S["ld_attn"], 16)
            sp.dma_start(ew[:, :, :], attn_e.rearrange("(a two) j i -> (two j) a i", two=2)).then_inc(S["ld_attn"], 16)
            for half in range(2):
                q = slice(64 * half, 64 * half + 64)
                sp.dma_start(qkvw[q, :], qkv_w[:, :]).then_inc(S["ld_ffn"], 16)
                sp.dma_start(lns[q, 0:1], ln1[:, :]).then_inc(S["ld_ffn"], 16)
                sp.dma_start(lns[q, 1:2], ln2[:, :]).then_inc(S["ld_ffn"], 16)
                sp.dma_start(rw[q, :], router[:, :]).then_inc(S["ld_ffn"], 16)
                tt = cos_t.rearrange("(a p) c -> p a c", a=2)
                sp.dma_start(cos4[:, 2 * half:2 * half + 2, :], tt).then_inc(S["ld_ffn"], 16)
                tt = sin_t.rearrange("(a p) c -> p a c", a=2)
                sp.dma_start(sin4[:, 2 * half:2 * half + 2, :], tt).then_inc(S["ld_ffn"], 16)
            sp.dma_start(wo_sb[:, :], wo_t[:, :]).then_inc(S["ld_ffn"], 16)
            sp.dma_start(w2s[:, :, :], w2m[:, :, :]).then_inc(S["ld_w2"], 16)
            w2v = w2r.rearrange("r (k two) c -> r k two c", two=2)
            for half in range(2):
                sp.dma_start(w2x[64 * half:64 * half + REM, :, 64 * half:64 * half + 64],
                             w2v[:, :, half, :]).then_inc(S["ld_w2"], 16)
            for n, (wm, wr, s) in enumerate(((w1m, w1r, "ld_w1"), (w3m, w3r, "ld_w3"))):
                if n:
                    sp.wait_ge(S["w1cast"], 1)
                for half in range(2):
                    q = slice(64 * half, 64 * half + 64)
                    sp.dma_start(w1s[q, 0:NE, :], wm[:, :, :]).then_inc(S[s], 16)
                    sp.dma_start(w1s[q, NE:CH, :].rearrange("c k (two r) -> c (k two) r", two=2)[:, :, 0:REM],
                                 wr[:, :, :]).then_inc(S[s], 16)
            ov = out.rearrange("(hf p) (tt q) c -> q p hf tt c", hf=2, tt=2)
            for g in range(TILES):
                p_, hf, tt = g // 4, (g // 2) % 2, g % 2
                sp.wait_ge(S["fin_ready"], g + 1)
                sp.dma_start(ov[:, p_, hf, tt, :], fin[:, g, :]).then_inc(S["stored"], 16)
            sp.wait_ge(S["stored"], 16 * TILES)

        @block.gpsimd
        def _(pool):
            n = [0]

            def link(ins):
                n[0] += 1
                ins.then_inc(S["gchain"], 1)
                pool.wait_ge(S["gchain"], n[0])

            made = [0]

            def const(ins):
                made[0] += 1
                ins.then_inc(S["consts"], 1)
                pool.wait_ge(S["consts"], made[0])

            link(nc.gpsimd.memset(Wt[:, :, :], 0.0))
            nc.gpsimd.memset(w2x[:, :, :], 0.0).then_inc(S["memz"], 1)
            nc.gpsimd.memset(w1s[:, NE:CH, :], 0.0).then_inc(S["memz"], 1)
            pool.wait_ge(S["memz"], 2)
            nc.gpsimd.iota(vcol_i[0:64, :], [[0, 1]], base=0, channel_multiplier=1).then_inc(S["bd_zero"], 1)
            link(nc.gpsimd.iota(vcol_i[64:P, :], [[0, 1]], base=0, channel_multiplier=1))
            pool.wait_ge(S["bd_zero"], 1)
            const(nc.gpsimd.tensor_copy(vcol[:, :], vcol_i[:, :]))
            link(nc.gpsimd.memset(identf[:, :], 0.0))
            link(nc.gpsimd.affine_select(out=identf[:, :], in_=identf[:, :], compare_op=ALU.not_equal, fill=1.0,
                                         base=0, pattern=[[-1, P]], channel_multiplier=1))
            const(nc.gpsimd.tensor_copy(ident16[:, :], identf[:, :]))
            const(nc.gpsimd.tensor_copy(identb[:, :], identf[:, :]))
            link(nc.gpsimd.memset(trimul[:, :], 1.0))
            for half in range(2):
                q = slice(64 * half, 64 * half + 64)
                const(nc.gpsimd.affine_select(out=trimul[q, :], in_=trimul[q, :], compare_op=ALU.is_ge, fill=0.0, base=0,
                                        pattern=[[1, 64]], channel_multiplier=-1))
            const(nc.gpsimd.memset(neghalf[:, :], -0.5))
            const(nc.gpsimd.memset(bdT[:, :, :], 0.0))
            const(nc.gpsimd.memset(bdS[:, :, :], 0.0))
            const(nc.gpsimd.memset(bdM[:, :, :, :], 0.0))
            for m in (mask_t, mask_t2, mask_s, mask_s2):
                link(nc.gpsimd.memset(m[:, :, :], 0.0))
            for m, w, rep, sgn in ((mask_t, 0, 4, -1), (mask_t2, P, 2, -1), (mask_s, 0, 4, 1), (mask_s2, 0, 2, 1)):
                const(nc.gpsimd.affine_select(out=m[:, :, w:w + P], in_=m[:, :, w:w + P], compare_op=ALU.is_ge, fill=NEG,
                                        base=0, pattern=[[0, rep], [sgn, P]],
                                        channel_multiplier=-sgn))
            link(nc.gpsimd.memset(selh[:, :, :], 1.0))
            link(nc.gpsimd.affine_select(out=selh[:, :, :], in_=selh[:, :, :], compare_op=ALU.is_ge, fill=0.0, base=0,
                                         pattern=[[-3, NH], [0, P]], channel_multiplier=1))
            const(nc.gpsimd.affine_select(out=selh[:, :, :], in_=selh[:, :, :], compare_op=ALU.is_ge, fill=0.0, base=2,
                                    pattern=[[3, NH], [0, P]], channel_multiplier=-1))
            const(nc.gpsimd.memset(vaug[:, :, :, :], 1.0))
            link(nc.gpsimd.memset(lowidx[:, :, :], 1.0))
            const(nc.gpsimd.affine_select(out=lowidx[:, :, :], in_=lowidx[:, :, :], compare_op=ALU.is_gt, fill=0.0, base=0,
                                    pattern=[[1, NE], [-1, NE]], channel_multiplier=0))

            def first_norm(p):
                g4 = slice(4 * p, 4 * p + 4)
                pool.wait_ge(S["var_ready"], p + 1)
                nc.gpsimd.tensor_tensor(stat[:, 4, g4], stat[:, 3, g4], neghalf[:, 0:4], ALU.pow) \
                    .then_inc(S["rstd_ready"], 1)
                pool.wait_ge(S["s_ready"], p + 1)
                if p >= 2:
                    pool.wait_ge(S["tr16_ps"], p - 1)
                link(nc.gpsimd.tensor_copy(shl[:, p % 2, :, 0, :], s2[:, p % 2, :, 0, :]))
                nc.gpsimd.tensor_tensor(shl[:, p % 2, :, 1, :], s2[:, p % 2, :, 0, :], shl[:, p % 2, :, 0, :],
                                        ALU.subtract).then_inc(S["shl_ready"], 1)

            def second_norm(p):
                g4 = slice(4 * p, 4 * p + 4)
                pool.wait_ge(S["var2_ready"], p + 1)
                nc.gpsimd.tensor_tensor(stat[:, 4, g4], stat[:, 3, g4], neghalf[:, 0:4], ALU.pow) \
                    .then_inc(S["rstd2_ready"], 1)
                pool.wait_ge(S["q1_ready"], p + 1)
                nc.gpsimd.tensor_tensor(stat[:, 6, g4], stat[:, 5, g4], neghalf[:, 0:4], ALU.pow) \
                    .then_inc(S["rinv_ready"], 1)
                pool.wait_ge(S["hr_ready"], p + 1)
                if p >= 2:
                    pool.wait_ge(S["trh_ps"], p - 1)
                link(nc.gpsimd.tensor_copy(shl[:, p % 2, :, 0, :], s2[:, p % 2, :, 0, :]))
                nc.gpsimd.tensor_tensor(shl[:, p % 2, :, 1, :], s2[:, p % 2, :, 0, :], shl[:, p % 2, :, 0, :],
                                        ALU.subtract).then_inc(S["hsplit_ready"], 1)

            def third_norm(p):
                g4 = slice(4 * p, 4 * p + 4)
                pool.wait_ge(S["ss_ready"], p + 1)
                nc.gpsimd.tensor_tensor(stat[:, 8, g4], stat[:, 7, g4], neghalf[:, 0:4], ALU.pow) \
                    .then_inc(S["r2_ready"], 1)
                pool.wait_ge(S["fs_ready"], p + 1)
                if p >= 2:
                    pool.wait_ge(S["trf_ps"], p - 1)
                link(nc.gpsimd.tensor_copy(shl[:, p % 2, :, 0, :], s2[:, p % 2, :, 0, :]))
                nc.gpsimd.tensor_tensor(shl[:, p % 2, :, 1, :], s2[:, p % 2, :, 0, :], shl[:, p % 2, :, 0, :],
                                        ALU.subtract).then_inc(S["fsplit_ready"], 1)

            for p in range(PAIRS):
                first_norm(p)
                if p >= 1:
                    pass
            for p in range(PAIRS):
                second_norm(p)
            for p in range(PAIRS):
                pool.wait_ge(S["x2_ready"], 2 * p + 2)
                g4 = slice(4 * p, 4 * p + 4)
                link(nc.gpsimd.tensor_tensor(hx[:, g4, :], h[:, g4, :], x2[:, g4, :], ALU.add))
                third_norm(p)
            for g in range(TILES):
                pool.wait_ge(S["mix_ready"], g + 1)
                m = moe[:, g % 2, :, :]
                link(nc.gpsimd.tensor_tensor(m[:, 0:4, :], m[:, 0:4, :], m[:, 4:8, :], ALU.add))
                link(nc.gpsimd.tensor_tensor(m[:, 0:2, :], m[:, 0:2, :], m[:, 2:4, :], ALU.add))
                link(nc.gpsimd.tensor_tensor(m[:, 0, :], m[:, 0, :], m[:, 1, :], ALU.add))
                nc.gpsimd.tensor_tensor(fin[:, g, :], m[:, 0, :], hx[:, g, :], ALU.add).then_inc(S["fin_ready"], 1)

        @block.scalar
        def _(act):
            def conv_gelu(l, gm):
                act.wait_ge(S["conv_ps"], 2 * l + gm + 1)
                if l:
                    act.wait_ge(S["pw_ps"], 2 * (l - 1) + gm + 1)
                nc.scalar.activation(hid1[:, gm, :], bank[gm][:, :], ACT.Gelu,
                                     bias=bt[:, l:l + 1]).then_inc(S["hid_ready"], 1)

            def pw_gelu(l, gm):
                act.wait_ge(S["pw_ps"], 2 * l + gm + 1)
                if l:
                    act.wait_ge(S["x_ready"], 2 + 2 * (l - 1) + gm + 1)
                nc.scalar.activation(hid2[:, gm, :], bank[2 + gm][:, :], ACT.Gelu,
                                     bias=bt[:, LAYERS + l:LAYERS + l + 1]).then_inc(S["pw_gelu"], 1)

            act.wait_ge(S["ld_tcn0"], 64)
            act.wait_ge(S["ld_tcn1"], 48)
            for l in range(LAYERS):
                for gm in range(2):
                    conv_gelu(l, gm)
                for gm in range(2):
                    pw_gelu(l, gm)
            for gm in range(2):
                act.wait_ge(S["out1_ps"], gm + 1)
                nc.scalar.activation(hid1[:, gm, :], bank[gm][:, :], ACT.Gelu,
                                     bias=bt[:, 2 * LAYERS:2 * LAYERS + 1]).then_inc(S["hid_ready"], 1)

            def softmax_parts(p):
                g4 = slice(4 * p, 4 * p + 4)
                act.wait_ge(S["lsub_ready"], p + 1)
                nc.scalar.activation(ex[:, p % 2, :, :], L[:, g4, :], ACT.Exp).then_inc(S["exp_ready"], 1)
                act.wait_ge(S["lsum_ready"], p + 1)
                nc.scalar.activation(stat[:, 1, g4], stat[:, 0, g4], ACT.Ln).then_inc(S["ln_ready"], 1)

            def transposed_rows(p):
                g4 = slice(4 * p, 4 * p + 4)
                act.wait_ge(S["tr16_ps"], p + 1)
                nc.scalar.copy(sTs[:, g4, :].rearrange("p a b -> p (a b)"),
                               bank[1][:, 0:256].bitcast(f16)).then_inc(S["sTs_ready"], 1)

            def q_out(p, a):
                act.wait_ge(S["q_ps"], 4 * p + a + 1)
                if p >= 2:
                    act.wait_ge(S["o_ps"], 4 * (p - 1))
                nc.scalar.mul(qT[:, p % 2, a, :], bank[2 + a % 2][:, :], 1.0 / ATT_SCALE).then_inc(S["q_ready"], 1)

            def o_out(g):
                act.wait_ge(S["o_ps"], g + 1)
                if g >= 2:
                    act.wait_ge(S["e_ps"], g - 1)
                nc.scalar.copy(oT[:, g % 2, :, :].rearrange("p a (cc t) -> p cc a t", cc=2),
                               bank[6][:, :].rearrange("p (cc a t) -> p cc a t", cc=2, a=4)) \
                    .then_inc(S["o_ready"], 1)

            for p in (0,):
                softmax_parts(p)
                transposed_rows(p)
                for a in range(4):
                    q_out(p, a)
            for g in range(TILES):
                p = g // 4 + 1
                if g % 4 == 0 and p < PAIRS:
                    softmax_parts(p)
                o_out(g)
                if g % 4 == 2 and p < PAIRS:
                    transposed_rows(p)
                    for a in range(4):
                        q_out(p, a)

            def h_rows(p):
                g4 = slice(4 * p, 4 * p + 4)
                act.wait_ge(S["trh_ps"], p + 1)
                nc.scalar.copy(hTs[:, g4, :].rearrange("p a b -> p (a b)"),
                               bank[7][:, 0:256].bitcast(f16)).then_inc(S["hTs_ready"], 1)

            def stacked(g):
                act.wait_ge(S["stk_ps"], g + 1)
                nc.scalar.copy(qkT[:, g, :, :].rearrange("p a b -> p (a b)"),
                               bank[1 + g % 2][0:96, 0:384].bitcast(bf16)).then_inc(S["stk_ready"], 1)

            def probs(b):
                for u in range(3):
                    act.wait_ge(S["p2_ps"], 3 * b + u + 1)
                    if b >= 2:
                        act.wait_ge(S["y_ps"], b - 1)
                    nc.scalar.activation(pT[:, b % 2, u, :], bank[5 + (3 * b + u) % 2][:, :],
                                         ACT.Exp).then_inc(S["exp2_ready"], 1)

            def y_rows(b):
                act.wait_ge(S["yT_ps"], b + 1)
                nc.scalar.copy(yT[:, b % 2, :, :].rearrange("p a b -> p (a b)"),
                               bank[7][0:C, 0:2 * P]).then_inc(S["yT_ready"], 1)

            for p in range(PAIRS):
                h_rows(p)
            for g in range(4):
                stacked(g)
            for b in range(B):
                if b % 2 == 0 and b // 2 + 1 < PAIRS:
                    for g in range(4 * (b // 2 + 1), 4 * (b // 2 + 2)):
                        stacked(g)
                probs(b)
                y_rows(b)
            for p in range(PAIRS):
                g4 = slice(4 * p, 4 * p + 4)
                act.wait_ge(S["trf_ps"], p + 1)
                nc.scalar.copy(fTs[:, g4, :].rearrange("p a b -> p (a b)"),
                               bank[6][:, 0:256].bitcast(f16)).then_inc(S["fTs_ready"], 1)
                act.wait_ge(S["rexp_in"], p + 1)
                nc.scalar.activation(lg[:, :, :], lg[:, :, :], ACT.Exp).then_inc(S["rexp_ready"], 1)
            for n in range(PAIRS):
                for j in range(CH):
                    u = CH * n + j
                    act.wait_ge(S["a_ps"], u + 1)
                    if u >= 2:
                        act.wait_ge(S["hh_ready"], u - 1)
                    nc.scalar.activation(sil[:, u % 2, :], bank[u % 2][:, :], ACT.Silu,
                                         scale=1.0 / FFN_SCALE).then_inc(S["sil_ready"], 1)

        @block.vector
        def _(dve):
            n = [0]

            def link(ins):
                n[0] += 1
                ins.then_inc(S["vchain"], 1)
                dve.wait_ge(S["vchain"], n[0])

            V_ = nc.vector

            link(V_.memset(embc[:, :, :], 1.0))
            link(V_.memset(startc[:, :], 1.0))
            link(V_.memset(table[:, :], 0.0))
            link(V_.memset(Xp[:, :, 0:PAD], 0.0))
            dve.wait_ge(S["ld_emb"], 32)
            for d in range(2):
                link(V_.tensor_scalar(embc[0:EMB, d, :], embp[0:EMB, 0:V], embp[0:EMB, 2 * V:2 * V + 1], None,
                                      ALU.add))
                link(V_.tensor_copy(inw2[:, d, :], embp[:, V:2 * V]))
            V_.tensor_tensor(startc[0:EMB, :], embp[0:EMB, 2 * V + 1:2 * V + 2], embp[0:EMB, 2 * V:2 * V + 1],
                             ALU.add).then_inc(S["embc_ready"], 1)
            dve.wait_ge(S["consts"], 1)
            dve.wait_ge(S["ld_tok"], 32)
            for gm in range(2):
                V_.tensor_scalar(onehot[:, 2 * gm:2 * gm + 2, 1:T], idx[:, 2 * gm:2 * gm + 2, 1:T], vcol[:, 0:1],
                                 None, ALU.is_equal).then_inc(S["onehot_ready"], 1)
            dve.wait_ge(S["table_ps"], 1)
            link(V_.tensor_copy(table[0:64, 0:64], bank[4][0:64, 0:64]))
            link(V_.tensor_copy(Xp[:, :, PAD:PAD + 1], bank[4][:, 64:65].unsqueeze(1).to_broadcast([P, 4, 1])))
            V_.tensor_copy(table[64:P, 64:P], bank[4][64:P, 0:64]).then_inc(S["table_ready"], 1)
            for gm in range(2):
                dve.wait_ge(S["emb_ps"], gm + 1)
                V_.tensor_copy(Xp[:, 2 * gm:2 * gm + 2, PAD + 1:PAD + T],
                               bank[gm][:, :].rearrange("p (b t) -> p b t", b=2)[:, :, 1:T]) \
                    .then_inc(S["x_ready"], 1)

            def residual(l, gm):
                dve.wait_ge(S["pw_gelu"], 2 * l + gm + 1)
                if l == LAYERS - 1 or True:
                    dve.wait_ge(S["conv_ps"], 2 * l + gm + 1)
                V_.tensor_tensor(Xp[:, 2 * gm:2 * gm + 2, PAD:PAD + T], Xp[:, 2 * gm:2 * gm + 2, PAD:PAD + T],
                                 hid2[:, gm, :].rearrange("p (b t) -> p b t", b=2), ALU.add) \
                    .then_inc(S["x_ready"], 1)

            def split16(hi, lo, src, scale, scratch):
                link(V_.tensor_scalar(scratch, src, scale, None, ALU.mult))
                link(V_.tensor_copy(hi, scratch))
                link(V_.tensor_tensor(lo, scratch, hi, ALU.subtract))

            def weights_setup(stage):
                if stage == 0:
                    dve.wait_ge(S["ld_attn"], 48)
                    split16(qwh[:, 0, :, :], qwh[:, 1, :, :], qw[:, :, :], ATT_SCALE, qw[:, :, :])
                    V_.tensor_copy(stat[0:1, 11, 0:1], vcol[0:1, :]).then_inc(S["wts_ready"], 1)
                elif stage == 1:
                    dve.wait_ge(S["ld_ffn"], 13 * 16)
                    link(V_.tensor_scalar(qkvw[:, :], qkvw[:, :], lns[:, 0:1], None, ALU.mult))
                    split16(qkvh[:, 0, :], qkvh[:, 1, :], qkvw[:, :], FFN_SCALE, qkvw[:, :])
                    link(V_.tensor_scalar(rw[:, :], rw[:, :], lns[:, 1:2], None, ALU.mult))
                    split16(rwh[:, 0, :], rwh[:, 1, :], rw[:, :], FFN_SCALE, rw[:, :])
                elif stage in (2, 3):
                    dve.wait_ge(S["ld_w1" if stage == 2 else "ld_w3"], 64)
                    dst = w1h if stage == 2 else w3h
                    link(V_.tensor_scalar(w1s[:, :, :], w1s[:, :, :], lns[:, 1:2], FFN_SCALE, ALU.mult, ALU.mult))
                    link(V_.tensor_copy(dst[:, 0, :, :], w1s[:, :, :]))
                    V_.tensor_tensor(dst[:, 1, :, :], w1s[:, :, :], dst[:, 0, :, :], ALU.subtract) \
                        .then_inc(S["w1cast"], 1)
                    dve.wait_ge(S["w1cast"], stage - 1)

            for l in range(LAYERS):
                for gm in range(2):
                    residual(l, gm)
                if 1 <= l <= 4:
                    weights_setup(l - 1)

            def bc4(ap):
                return ap.unsqueeze(2).to_broadcast([P, 4, V])

            def logits_out(p):
                g4 = slice(4 * p, 4 * p + 4)
                dve.wait_ge(S["logits_ps"], p + 1)
                (V_.tensor_tensor(L[:, g4, :].rearrange("p (hf tt) v -> p tt hf v", hf=2),
                                      bank[4 + p][:, 0:256].rearrange("p (tt hf v) -> p tt hf v", tt=2, hf=2),
                                      b2bc[:, :].unsqueeze(1).unsqueeze(1).to_broadcast([P, 2, 2, V]), ALU.add)
                 .then_inc(S["logits_read"], 1))

            def ln0_a(p):
                g4 = slice(4 * p, 4 * p + 4)
                dve.wait_ge(S["logits_read"], p + 1)
                link(V_.tensor_reduce(stat[:, 2, g4], L[:, g4, :], AX, ALU.max))
                V_.tensor_tensor(L[:, g4, :], L[:, g4, :], bc4(stat[:, 2, g4]), ALU.subtract) \
                    .then_inc(S["lsub_ready"], 1)
                dve.wait_ge(S["lsub_ready"], p + 1)

            def centre(p, src, ready):
                g4 = slice(4 * p, 4 * p + 4)
                c_, q_ = cen[:, p % 2, :, :], sqr[:, p % 2, :, :]
                link(V_.tensor_reduce(stat[:, 2, g4], src, AX, ALU.add))
                link(V_.scalar_tensor_tensor(c_, bc4(stat[:, 2, g4]), -1.0 / V, src, ALU.mult, ALU.add))
                link(V_.tensor_tensor(q_, c_, c_, ALU.mult))
                link(V_.tensor_reduce(stat[:, 9, g4], q_, AX, ALU.add))
                V_.tensor_scalar(stat[:, 3, g4], stat[:, 9, g4], 1.0 / V, 1e-5, ALU.mult, ALU.add) \
                    .then_inc(S[ready], 1)

            def ln0_b(p):
                g4 = slice(4 * p, 4 * p + 4)
                centre(p, L[:, g4, :], "var_ready")
                dve.wait_ge(S["exp_ready"], p + 1)
                V_.tensor_reduce(stat[:, 0, g4], ex[:, p % 2, :, :], AX, ALU.add).then_inc(S["lsum_ready"], 1)

            def ln0_c(p):
                g4 = slice(4 * p, 4 * p + 4)
                dve.wait_ge(S["rstd_ready"], p + 1)
                if p >= 2:
                    dve.wait_ge(S["shl_ready"], p - 1)
                    dve.wait_ge(S["M_ps"], p - 1)
                    dve.wait_ge(S["bdS_ready"], p - 1)
                for d in range(2):
                    r = V_.tensor_tensor(s2[:, p % 2, :, d, :], cen[:, p % 2, :, :], bc4(stat[:, 4, g4]), ALU.mult)
                    if d:
                        r.then_inc(S["s_ready"], 1)
                    else:
                        link(r)
                dve.wait_ge(S["ln_ready"], p + 1)
                V_.tensor_tensor(h[:, g4, :], L[:, g4, :], bc4(stat[:, 1, g4]), ALU.subtract) \
                    .then_inc(S["h_ready"], 1)
                dve.wait_ge(S["s_ready"], p + 1)
                dve.wait_ge(S["consts"], 9)
                for src in range(2):
                    for dst in range(2):
                        sq = slice(64 * src, 64 * src + 64)
                        dq = slice(64 * dst, 64 * dst + 64)
                        o = bdS[dq, 8 * p:8 * p + 8, dq].rearrange("p (a cc) i -> p a cc i", cc=2)[:, :, src, :]
                        r = V_.tensor_copy(o, s2[sq, p % 2, :, dst, :])
                r.then_inc(S["bdS_ready"], 1)

            def ln0_d(p):
                dve.wait_ge(S["tr32_ps"], p + 1)
                for hf in range(2):
                    q = slice(64 * hf, 64 * hf + 64)
                    r = V_.tensor_copy(bdT[q, 8 * p:8 * p + 8, q],
                                       bank[0][q, :].rearrange("p (a u) -> p a u", u=64))
                r.then_inc(S["bdT_ready"], 1)

            def ln0_e(p):
                dve.wait_ge(S["M_ps"], p + 1)
                for hf in range(2):
                    q = slice(64 * hf, 64 * hf + 64)
                    r = V_.tensor_copy(bdM[q, 2 * p:2 * p + 2, :, q],
                                       bank[1][q, 0:384].rearrange("p (b k j) -> p b k j", b=2, k=3))
                r.then_inc(S["M_ready"], 1)

            def mask_omega(g):
                dve.wait_ge(S["om_ps"], g + 1)
                if g >= 2:
                    dve.wait_ge(S["o_ps"], g - 1)
                V_.tensor_tensor(om[:, g % 2, :].rearrange("p (a t) -> p a t", t=64),
                                 bank[4 + g % 2][:, :].rearrange("p (a t) -> p a t", t=64),
                                 trimul[:, :].unsqueeze(1).to_broadcast([P, 8, 64]), ALU.mult) \
                    .then_inc(S["om_ready"], 1)

            def ln2_a(p):
                g4 = slice(4 * p, 4 * p + 4)
                dve.wait_ge(S["e_ps"], 4 * p + 4)
                dve.wait_ge(S["h_ready"], p + 1)
                V_.tensor_tensor(h[:, g4, :], h[:, g4, :], bank[7][:, 0:256].rearrange("p (a c) -> p a c", a=4),
                                 ALU.add).then_inc(S["h2_ready"], 1)
                dve.wait_ge(S["h2_ready"], p + 1)

            def ln2_b(p):
                g4 = slice(4 * p, 4 * p + 4)
                centre(p, h[:, g4, :], "var2_ready")
                dve.wait_ge(S["rstd2_ready"], p + 1)
                link(V_.tensor_tensor(xf[:, g4, :], cen[:, p % 2, :, :], bc4(stat[:, 4, g4]), ALU.mult))
                link(V_.tensor_tensor(stat[:, 10, g4], stat[:, 4, g4], stat[:, 4, g4], ALU.mult))
                link(V_.tensor_tensor(stat[:, 10, g4], stat[:, 10, g4], stat[:, 9, g4], ALU.mult))
                V_.tensor_scalar(stat[:, 5, g4], stat[:, 10, g4], 1.0 / V, 1e-6, ALU.mult, ALU.add) \
                    .then_inc(S["q1_ready"], 1)
                dve.wait_ge(S["rinv_ready"], p + 1)
                if p >= 2:
                    dve.wait_ge(S["hsplit_ready"], p - 1)
                V_.tensor_tensor(s2[:, p % 2, :, 0, :], xf[:, g4, :], bc4(stat[:, 6, g4]), ALU.mult) \
                    .then_inc(S["hr_ready"], 1)

            dve.wait_ge(S["ld_tcn1"], 48)
            for p in range(PAIRS):
                logits_out(p)
            ln0_a(0)
            ln0_b(0)
            ln0_c(0)
            ln0_d(0)
            ln0_e(0)
            dve.wait_ge(S["consts"], 6)
            for g in range(TILES):
                p = g // 4 + 1
                mask_omega(g)
                if p < PAIRS:
                    if g % 4 == 0:
                        ln0_a(p)
                        ln0_b(p)
                    elif g % 4 == 1:
                        ln0_c(p)
                    elif g % 4 == 2:
                        ln0_d(p)
                    else:
                        ln0_e(p)
                if g % 4 == 0 and g:
                    ln2_a(p - 2)
            ln2_a(PAIRS - 1)
            for p in range(PAIRS):
                ln2_b(p)

            def rotary(p):
                dve.wait_ge(S["qkv_ps"], p + 1)
                src = bank[0][:, :].rearrange("p (a c) -> p a c", a=4)
                qk = src[:, :, 0:96]
                link(V_.tensor_tensor(rope[:, :, :], qk, cos4[:, :, :], ALU.mult))
                for d in range(2):
                    def half(ap, k):
                        return ap.rearrange("p a (n two e) -> p a n two e", two=2, e=8)[:, :, :, k, :]
                    link(V_.tensor_tensor(half(rot[:, :, :], d), half(qk, 1 - d), half(sin4[:, :, :], d), ALU.mult))
                dve.wait_ge(S["consts"], 15)
                V_.tensor_scalar(vaug[:, 4 * p:4 * p + 4, :, 0:HD],
                                 src[:, :, 96:128].rearrange("p a (n e) -> p a n e", e=HD), 1.0 / FFN_SCALE, None,
                                 ALU.mult).then_inc(S["v_ready"], 1)
                link(V_.tensor_tensor(rope[:, :, :], rope[:, :, :], rot[:, :, :], ALU.add))
                if p >= 2:
                    dve.wait_ge(S["stk_ps"], 4 * (p - 1))
                r6 = rope[:, :, :].rearrange("p a (n e) -> p a n e", e=HD)
                t6 = rot[:, :, :].rearrange("p a (n e) -> p a n e", e=HD)
                d_ = qst[:, p % 2, :, :, :, :]
                link(V_.tensor_copy(d_[:, :, :, 0, :], r6))
                link(V_.tensor_tensor(t6, r6, d_[:, :, :, 0, :], ALU.subtract))
                link(V_.tensor_copy(d_[:, :, 0:4, 3, :], t6[:, :, 0:4, :]))
                link(V_.tensor_copy(d_[:, :, 4:6, 1, :], t6[:, :, 4:6, :]))
                V_.tensor_tensor(d_[:, :, 0:4, 5, :], t6[:, :, 0:4, :], d_[:, :, 0:4, 3, :], ALU.subtract)
                V_.tensor_tensor(d_[:, :, 4:6, 2, :], t6[:, :, 4:6, :], d_[:, :, 4:6, 1, :], ALU.subtract)
                V_.tensor_copy(d_[:, :, 0:4, 1, :], d_[:, :, 0:4, 0, :])
                V_.tensor_copy(d_[:, :, 0:4, 2, :], d_[:, :, 0:4, 0, :])
                V_.tensor_copy(d_[:, :, 0:4, 4, :], d_[:, :, 0:4, 3, :])
                V_.tensor_copy(d_[:, :, 4:6, 3, :], d_[:, :, 4:6, 0, :])
                V_.tensor_copy(d_[:, :, 4:6, 5, :], d_[:, :, 4:6, 0, :])
                V_.tensor_copy(d_[:, :, 4:6, 4, :], d_[:, :, 4:6, 1, :]).then_inc(S["split_ready"], 1)
                dve.wait_ge(S["split_ready"], p + 1)

            def row_max(b):
                for u in range(3):
                    dve.wait_ge(S["p1_ps"], 3 * b + u + 1)
                    g, h0, nh = (2 * b, 0, 4) if u == 0 else (2 * b + 1, 2 * (u - 1), 2)
                    V_.tensor_reduce(nmx[:, g, h0:h0 + nh],
                                     bank[3 + (3 * b + u) % 2][:, :].rearrange("p (n s) -> p n s", n=nh),
                                     AX, ALU.max, negate=True).then_inc(S["max_ready"], 1)
                dve.wait_ge(S["max_ready"], 3 * b + 3)
                src, d_, r_ = nmx[:, 2 * b:2 * b + 2, :], nms[:, b % 2, :, :, :], nmr[:, b % 2, :, :]
                if b >= 2:
                    dve.wait_ge(S["nmT_ps"], b - 1)
                link(V_.tensor_copy(d_[:, :, :, 0], src))
                link(V_.tensor_tensor(r_, src, d_[:, :, :, 0], ALU.subtract))
                link(V_.tensor_copy(d_[:, :, :, 1], r_))
                V_.tensor_tensor(d_[:, :, :, 2], r_, d_[:, :, :, 1], ALU.subtract).then_inc(S["nms_ready"], 1)
                dve.wait_ge(S["nmT_ps"], b + 1)
                if b >= 2:
                    dve.wait_ge(S["p2_ps"], 3 * b - 3)
                V_.tensor_copy(nmT[:, b % 2, :, :].rearrange("p a b -> p (a b)"),
                               bank[0][0:3 * NH, 0:P].bitcast(bf16)).then_inc(S["nmT_ready"], 1)

            def attended(b):
                dve.wait_ge(S["y_ps"], b + 1)
                ps = bank[7][:, 0:2 * NH * (HD + 1)].rearrange("p (a n e) -> p a n e", a=2, n=NH)
                link(V_.reciprocal(rec[:, b % 2, :, :], ps[:, :, :, HD]))
                if b >= 2:
                    dve.wait_ge(S["yT_ps"], b - 1)
                V_.tensor_tensor(y[:, b % 2, :, :, :], ps[:, :, :, 0:HD],
                                 rec[:, b % 2, :, :].unsqueeze(3).to_broadcast([P, 2, NH, HD]), ALU.mult) \
                    .then_inc(S["y_ready"], 1)

            def add_wo(b):
                dve.wait_ge(S["wo_ps"], b + 1)
                V_.tensor_tensor(x2[:, 2 * b:2 * b + 2, :], xf[:, 2 * b:2 * b + 2, :],
                                 bank[0][:, 0:2 * C].rearrange("p (a c) -> p a c", a=2), ALU.add) \
                    .then_inc(S["x2_ready"], 1)

            rotary(0)
            row_max(0)
            for b in range(B):
                if b % 2 == 0 and b // 2 + 1 < PAIRS:
                    rotary(b // 2 + 1)
                if b + 1 < B:
                    row_max(b + 1)
                attended(b)
                add_wo(b)

            def rms(p):
                g4 = slice(4 * p, 4 * p + 4)
                dve.wait_ge(S["x2_ready"], 2 * p + 2)
                link(V_.tensor_tensor(sqr[:, p % 2, :, :], x2[:, g4, :], x2[:, g4, :], ALU.mult))
                link(V_.tensor_reduce(stat[:, 10, g4], sqr[:, p % 2, :, :], AX, ALU.add))
                V_.tensor_scalar(stat[:, 7, g4], stat[:, 10, g4], 1.0 / C, 1e-6, ALU.mult, ALU.add) \
                    .then_inc(S["ss_ready"], 1)
                dve.wait_ge(S["r2_ready"], p + 1)
                if p >= 2:
                    dve.wait_ge(S["fsplit_ready"], p - 1)
                V_.tensor_tensor(s2[:, p % 2, :, 0, :], x2[:, g4, :], bc4(stat[:, 8, g4]), ALU.mult) \
                    .then_inc(S["fs_ready"], 1)

            def gates(p):
                g4 = slice(4 * p, 4 * p + 4)

                def b8(ap):
                    return ap.unsqueeze(2).to_broadcast([P, 4, NE])
                dve.wait_ge(S["rt_ps"], p + 1)
                ps = bank[7][:, 0:4 * NE].rearrange("p (a e) -> p a e", a=4)
                link(V_.tensor_reduce(stat[:, 10, g4], ps, AX, ALU.max))
                link(V_.tensor_tensor(lg[:, :, :], ps, b8(stat[:, 10, g4]), ALU.subtract))
                V_.tensor_scalar(lg[:, :, :], lg[:, :, :], 1.0 / FFN_SCALE, None, ALU.mult).then_inc(S["rexp_in"], 1)
                dve.wait_ge(S["rexp_ready"], p + 1)
                e_i = lg[:, :, :].unsqueeze(3).to_broadcast([P, 4, NE, NE])
                e_j = lg[:, :, :].unsqueeze(2).to_broadcast([P, 4, NE, NE])
                low = lowidx[:, :, :].unsqueeze(1).to_broadcast([P, 4, NE, NE])
                link(V_.tensor_tensor(gt[:, :, :, :], e_j, e_i, ALU.is_gt))
                link(V_.tensor_tensor(ge[:, :, :, :], e_j, e_i, ALU.is_ge))
                link(V_.tensor_tensor(ge[:, :, :, :], ge[:, :, :, :], low, ALU.mult))
                link(V_.tensor_tensor(ge[:, :, :, :], ge[:, :, :, :], gt[:, :, :, :], ALU.max))
                link(V_.tensor_reduce(gate[:, g4, :], ge[:, :, :, :], AX, ALU.add))
                link(V_.scalar_tensor_tensor(gate[:, g4, :], gate[:, g4, :], 1.5, lg[:, :, :], ALU.is_lt, ALU.mult))
                link(V_.tensor_reduce(stat[:, 10, g4], lg[:, :, :], AX, ALU.add))
                link(V_.tensor_reduce(stat[:, 9, g4], gate[:, g4, :], AX, ALU.add))
                link(V_.scalar_tensor_tensor(stat[:, 9, g4], stat[:, 10, g4], 1e-9, stat[:, 9, g4], ALU.mult, ALU.add))
                link(V_.reciprocal(stat[:, 10, g4], stat[:, 9, g4]))
                V_.tensor_tensor(gate[:, g4, :], gate[:, g4, :], b8(stat[:, 10, g4]), ALU.mult) \
                    .then_inc(S["gate_ready"], 1)
                dve.wait_ge(S["gate_ready"], p + 1)

            for p in range(PAIRS):
                rms(p)
            for p in range(PAIRS):
                gates(p)

            def mix(g):
                dve.wait_ge(S["w2_ps"], g + 1)
                if g >= 2:
                    dve.wait_ge(S["fin_ready"], g - 1)
                V_.tensor_tensor(moe[:, g % 2, :, :], bank[4 + g % 2][:, :].rearrange("p (e c) -> p e c", e=NE),
                                 gate[:, g, :].unsqueeze(2).to_broadcast([P, NE, C]), ALU.mult) \
                    .then_inc(S["mix_ready"], 1)

            for n_ in range(PAIRS + 1):
                for j in range(CH):
                    u = CH * n_ + j
                    if n_ < PAIRS:
                        dve.wait_ge(S["sil_ready"], u + 1)
                        dve.wait_ge(S["b_ps"], u + 1)
                        if n_ >= 2:
                            dve.wait_ge(S["w2_ps"], 4 * (n_ - 1))
                        V_.scalar_tensor_tensor(hh[:, n_ % 2, j, :], bank[2 + u % 2][:, :], 1.0 / FFN_SCALE,
                                                sil[:, u % 2, :], ALU.mult, ALU.mult).then_inc(S["hh_ready"], 1)
                    if n_ and j % 3 == 2:
                        mix(4 * (n_ - 1) + j // 3)

        @block.tensor
        def _(pe):
            def mm(out_, l_, r_, a, z, skip=False):
                return nc.tensor.matmul(out_, l_, r_, start=a, stop=z, skip_group_check=skip)

            pe.wait_ge(S["embc_ready"], 1)
            mm(bank[4][:, 0:64], embc[:, :, :].rearrange("p a b -> p (a b)"), embp[:, V:2 * V], True, True)
            mm(bank[4][:, 64:65], inw2[:, :, :].rearrange("p a b -> p (a b)"), startc[:, :], True, True) \
                .then_inc(S["table_ps"], 1)
            pe.wait_ge(S["table_ready"], 1)
            for gm in range(2):
                pe.wait_ge(S["onehot_ready"], gm + 1)
                mm(bank[gm][:, :].rearrange("p (b t) -> p b t", b=2)[:, :, 1:T], table[:, :],
                   onehot[:, 2 * gm:2 * gm + 2, 1:T], True, True).then_inc(S["emb_ps"], 1)
            for l in range(LAYERS):
                d = 2 ** l
                if l == 0:
                    pe.wait_ge(S["ld_tcn0"], 64)
                    pe.wait_ge(S["ld_tcn1"], 48)
                for gm in range(2):
                    pe.wait_ge(S["x_ready"], 2 * l + gm + 1)
                    if l:
                        pe.wait_ge(S["hid_ready"], 2 * (l - 1) + gm + 1)
                    for k in range(TAPS):
                        at = PAD - (TAPS - 1 - k) * d
                        r = mm(bank[gm][:, :].rearrange("p (b t) -> p b t", b=2), Wt[:, TAPS * l + k, :],
                               Xp[:, 2 * gm:2 * gm + 2, at:at + T], k == 0, k == TAPS - 1)
                    r.then_inc(S["conv_ps"], 1)
                for gm in range(2):
                    pe.wait_ge(S["hid_ready"], 2 * l + gm + 1)
                    if l:
                        pe.wait_ge(S["pw_gelu"], 2 * (l - 1) + gm + 1)
                    mm(bank[2 + gm][:, :], Wt[:, TAPS * LAYERS + l, :], hid1[:, gm, :], True, True) \
                        .then_inc(S["pw_ps"], 1)
            for gm in range(2):
                pe.wait_ge(S["x_ready"], 2 * LAYERS + gm + 1)
                mm(bank[gm][:, :].rearrange("p (b t) -> p b t", b=2), Wt[:, NBLK - 2, :],
                   Xp[:, 2 * gm:2 * gm + 2, PAD:PAD + T], True, True).then_inc(S["out1_ps"], 1)
            for p in range(PAIRS):
                pe.wait_ge(S["hid_ready"], 2 * LAYERS + p // 2 + 1)
                if p == 0:
                    pe.wait_ge(S["table_ready"], 1)
                for tt in range(2):
                    at = (p % 2) * T + tt * P
                    r = mm(bank[4 + p][:, P * tt:P * tt + P], hid1[:, p // 2, at:at + P], Wt[:, NBLK - 1, :],
                           True, True)
                r.then_inc(S["logits_ps"], 1)

            def prep(p):
                pe.wait_ge(S["s_ready"], p + 1)
                pe.wait_ge(S["consts"], 3)
                if p == 0:
                    pe.wait_ge(S["hid_ready"], 2 * LAYERS + 2)
                else:
                    pe.wait_ge(S["bdT_ready"], p)
                    pe.wait_ge(S["M_ready"], p)
                for a in range(4):
                    r = nc.tensor.transpose(bank[0][:, P * a:P * a + P],
                                            s2[:, p % 2, a, :, :].rearrange("p a b -> p (a b)"), identf[:, :])
                r.then_inc(S["tr32_ps"], 1)
                pe.wait_ge(S["shl_ready"], p + 1)
                for a in range(4):
                    r = nc.tensor.transpose(bank[1][:, 64 * a:64 * a + 64].bitcast(f16),
                                            shl[:, p % 2, a, :, :].rearrange("p a b -> p (a b)"), ident16[:, :])
                r.then_inc(S["tr16_ps"], 1)

            def outer_sums(p):
                pe.wait_ge(S["sTs_ready"], p + 1)
                for hf in range(2):
                    for k in range(3):
                        o = bank[1][:, 64 * (3 * hf + k):64 * (3 * hf + k) + 64]
                        parts = [(2 * hf, 64 if k == 0 else P)] + ([(2 * hf + 1, 64)] if k == 2 else [])
                        for i, (a, rows) in enumerate(parts):
                            r = mm(o, s2[0:rows, p % 2, a, :, :].rearrange("p a b -> p (a b)"),
                                   s2[0:rows, p % 2, a, 0, :], i == 0, i == len(parts) - 1)
                r.then_inc(S["M_ps"], 1)

            def queries(p):
                if p == 0:
                    pe.wait_ge(S["wts_ready"], 1)
                    pe.wait_ge(S["pw_gelu"], 2 * LAYERS)
                for a in range(4):
                    if 4 * p + a >= 2:
                        pe.wait_ge(S["q_ready"], 4 * p + a - 1)
                    rhs = sTs[:, 4 * p:4 * p + 4, :].rearrange("p a b -> p (a b)")
                    for w in range(2):
                        r = mm(bank[2 + a % 2][:, :], qwh[:, w, a, :], rhs, w == 0, w == 1)
                    r.then_inc(S["q_ps"], 1)

            def omega(g):
                p = g // 4
                pe.wait_ge(S["q_ready"], 4 * p + 4)
                pe.wait_ge(S["bdT_ready"], p + 1)
                if g < 2:
                    pe.wait_ge(S["logits_read"], g + 1)
                if g >= 2:
                    pe.wait_ge(S["om_ready"], g - 1)
                for cc in range(2):
                    t0 = P * (g % 4) + 64 * cc
                    r = mm(bank[4 + g % 2][:, 256 * cc:256 * cc + 256].rearrange("p (a t) -> p a t", a=4),
                           bdT[:, 2 * g + cc, :], qT[:, p % 2, :, t0:t0 + 64], True, True)
                r.then_inc(S["om_ps"], 1)

            def attend(g):
                p = g // 4
                pe.wait_ge(S["om_ready"], g + 1)
                pe.wait_ge(S["bdS_ready"], p + 1)
                pe.wait_ge(S["M_ready"], p + 1)
                if g == 0:
                    pe.wait_ge(S["logits_read"], 3)
                if g >= 1:
                    pe.wait_ge(S["o_ready"], g)
                for cc in range(2):
                    k = 2 * (g % 2) + cc
                    o = bank[6][:, 256 * cc:256 * cc + 256]
                    t0 = P * (g % 4) + 64 * cc
                    r = mm(o, bdS[:, 2 * g + cc, :], om[:, g % 2, 256 * cc:256 * cc + 256], True, k == 0)
                    if k:
                        r = mm(o.rearrange("p (a t) -> p a t", a=4), bdM[:, g // 2, k - 1, :],
                               qT[:, p % 2, :, t0:t0 + 64], False, True)
                r.then_inc(S["o_ps"], 1)

            def project(g):
                pe.wait_ge(S["o_ready"], g + 1)
                if g == 0:
                    pe.wait_ge(S["logits_read"], 4)
                if g % 4 == 0 and g:
                    pe.wait_ge(S["h2_ready"], g // 4)
                for a in range(4):
                    r = mm(bank[7][:, 64 * (g % 4):64 * (g % 4) + 64], oT[:, g % 2, a, :], ew[:, a, :],
                           a == 0, a == 3)
                r.then_inc(S["e_ps"], 1)

            prep(0)
            outer_sums(0)
            queries(0)
            omega(0)
            pe.wait_ge(S["ld_attn"], 48)
            for g in range(TILES):
                p = g // 4 + 1
                if g + 1 < TILES and (g + 1) % 4:
                    omega(g + 1)
                attend(g)
                if g:
                    project(g - 1)
                if p < PAIRS:
                    if g % 4 == 1:
                        prep(p)
                    if g % 4 == 2:
                        outer_sums(p)
                        queries(p)
                    if g % 4 == 3:
                        omega(g + 1)
            project(TILES - 1)

            def rows(p):
                pe.wait_ge(S["hsplit_ready"], p + 1)
                if p == 0:
                    pe.wait_ge(S["h2_ready"], PAIRS)
                else:
                    pe.wait_ge(S["hTs_ready"], p)
                for a in range(4):
                    r = nc.tensor.transpose(bank[7][:, 64 * a:64 * a + 64].bitcast(f16),
                                            shl[:, p % 2, a, :, :].rearrange("p a b -> p (a b)"), ident16[:, :])
                r.then_inc(S["trh_ps"], 1)

            def qkv(p):
                pe.wait_ge(S["hTs_ready"], p + 1)
                if p == 0:
                    pe.wait_ge(S["w1cast"], 1)
                for a in range(4):
                    for w in range(2):
                        r = mm(bank[0][:, P * a:P * a + P], hTs[:, 4 * p + a, :], qkvh[:, w, :], w == 0, w == 1)
                r.then_inc(S["qkv_ps"], 1)

            def stack(g):
                p = g // 4
                pe.wait_ge(S["split_ready"], p + 1)
                if g >= 2:
                    pe.wait_ge(S["stk_ready"], g - 1)
                for n_ in range(6):
                    r = nc.tensor.transpose(bank[1 + g % 2][0:96, 64 * n_:64 * n_ + 64].bitcast(bf16),
                                            qst[:, p % 2, g % 4, n_, :, :].rearrange("p a b -> p (a b)"),
                                            identb[:, :])
                r.then_inc(S["stk_ps"], 1)

            def scores_for_max(b):
                pe.wait_ge(S["stk_ready"], 2 * b + 2)
                for u in range(3):
                    U = 3 * b + u
                    if U == 0:
                        pe.wait_ge(S["consts"], 16)
                        pe.wait_ge(S["om_ready"], TILES)
                    if U >= 2:
                        pe.wait_ge(S["max_ready"], U - 1)
                    o = bank[3 + U % 2]
                    if u == 0:
                        mm(o[:, :], identb[:, :], mask_t[:, :, :].rearrange("p a b -> p (a b)"), True, False)
                        for n_ in range(NH):
                            r = mm(o[:, P * n_:P * n_ + P], qkT[:, 2 * b, n_, :], qkT[:, 2 * b, NH + n_ // 2, :],
                                   False, n_ == NH - 1)
                    else:
                        mm(o[:, :], identb[:, :], mask_t2[:, :, :].rearrange("p a b -> p (a b)"), True, False)
                        for i in range(2):
                            n_ = 2 * (u - 1) + i
                            r = mm(o[:, T * i:T * i + T].rearrange("p (a s) -> p a s", a=2),
                                   qkT[:, 2 * b + 1, n_, :], qkT[:, 2 * b:2 * b + 2, NH + n_ // 2, :],
                                   False, i == 1)
                    r.then_inc(S["p1_ps"], 1)

            def max_rows(b):
                pe.wait_ge(S["nms_ready"], b + 1)
                if b >= 2:
                    pe.wait_ge(S["x2_ready"], b - 1)
                for a in range(2):
                    r = nc.tensor.transpose(bank[0][0:3 * NH, 64 * a:64 * a + 64].bitcast(bf16),
                                            nms[:, b % 2, a, :, :].rearrange("p a b -> p (a b)"), identb[:, :])
                r.then_inc(S["nmT_ps"], 1)

            def scores_shifted(b):
                pe.wait_ge(S["nmT_ready"], b + 1)
                for u in range(3):
                    U = 3 * b + u
                    if U == 0:
                        pe.wait_ge(S["o_ready"], TILES)
                    if U >= 2:
                        pe.wait_ge(S["exp2_ready"], U - 1)
                    o = bank[5 + U % 2]
                    if u < 2:
                        mm(o[:, :], identb[:, :], mask_s2[:, :, :].rearrange("p a b -> p (a b)"), True, False)
                        for i in range(2):
                            n_ = 2 * u + i
                            ov_ = o[:, T * i:T * i + T].rearrange("p (a s) -> p a s", a=2)
                            mm(ov_, selh[:, n_, :], nmT[:, b % 2, :, :], False, False)
                            r = mm(ov_, qkT[:, 2 * b, NH + n_ // 2, :], qkT[:, 2 * b:2 * b + 2, n_, :], False, i == 1)
                    else:
                        mm(o[:, :], identb[:, :], mask_s[:, :, :].rearrange("p a b -> p (a b)"), True, False)
                        for n_ in range(NH):
                            ov_ = o[:, P * n_:P * n_ + P]
                            mm(ov_, selh[:, n_, :], nmT[:, b % 2, 1, :], False, False)
                            r = mm(ov_, qkT[:, 2 * b + 1, NH + n_ // 2, :], qkT[:, 2 * b + 1, n_, :],
                                   False, n_ == NH - 1)
                    r.then_inc(S["p2_ps"], 1)

            def values(b):
                pe.wait_ge(S["exp2_ready"], 3 * b + 3)
                pe.wait_ge(S["v_ready"], b // 2 + 1)
                if b == 0:
                    pe.wait_ge(S["hTs_ready"], PAIRS)
                else:
                    pe.wait_ge(S["yT_ready"], b)
                for tt in range(2):
                    for n_ in range(NH):
                        at = (NH * tt + n_) * (HD + 1)
                        o = bank[7][:, at:at + HD + 1]
                        c0 = T * (n_ % 2) + P * tt
                        r = mm(o, pT[:, b % 2, n_ // 2, c0:c0 + P], vaug[:, 2 * b, n_ // 2, :], True, tt == 0)
                        if tt:
                            r = mm(o, pT[:, b % 2, 2, P * n_:P * n_ + P], vaug[:, 2 * b + 1, n_ // 2, :], False, True)
                r.then_inc(S["y_ps"], 1)

            def out_rows(b):
                pe.wait_ge(S["y_ready"], b + 1)
                for a in range(2):
                    r = nc.tensor.transpose(bank[7][0:C, P * a:P * a + P],
                                            y[:, b % 2, a, :, :].rearrange("p a b -> p (a b)"), identf[:, :])
                r.then_inc(S["yT_ps"], 1)
                pe.wait_ge(S["yT_ready"], b + 1)
                pe.wait_ge(S["nmT_ready"], min(b + 2, B))
                for a in range(2):
                    r = mm(bank[0][:, C * a:C * a + C], yT[:, b % 2, a, :], wo_sb[:, :], True, True)
                r.then_inc(S["wo_ps"], 1)

            for p in range(PAIRS):
                rows(p)
            pe.wait_ge(S["M_ready"], PAIRS)
            pe.wait_ge(S["q_ready"], 4 * PAIRS)
            qkv(0)
            for g in range(4):
                stack(g)
            scores_for_max(0)
            max_rows(0)
            for b in range(B):
                if b % 2 == 0 and b // 2 + 1 < PAIRS:
                    pe.wait_ge(S["nmT_ready"], b + 1)
                    if b:
                        pe.wait_ge(S["x2_ready"], b)
                    qkv(b // 2 + 1)
                    for g in range(4 * (b // 2 + 1), 4 * (b // 2 + 2)):
                        stack(g)
                if b + 1 < B:
                    scores_for_max(b + 1)
                scores_shifted(b)
                if b + 1 < B:
                    max_rows(b + 1)
                values(b)
                out_rows(b)

            for p in range(PAIRS):
                pe.wait_ge(S["fsplit_ready"], p + 1)
                if p == 0:
                    pe.wait_ge(S["exp2_ready"], 3 * B)
                else:
                    pe.wait_ge(S["fTs_ready"], p)
                for a in range(4):
                    r = nc.tensor.transpose(bank[6][:, 64 * a:64 * a + 64].bitcast(f16),
                                            shl[:, p % 2, a, :, :].rearrange("p a b -> p (a b)"), ident16[:, :])
                r.then_inc(S["trf_ps"], 1)
                pe.wait_ge(S["fTs_ready"], p + 1)
                if p == 0:
                    pe.wait_ge(S["x2_ready"], B)
                    pe.wait_ge(S["w1cast"], 2)
                else:
                    pe.wait_ge(S["rexp_in"], p)
                for a in range(4):
                    for w in range(2):
                        r = mm(bank[7][:, NE * a:NE * a + NE], fTs[:, 4 * p + a, :], rwh[:, w, :], w == 0, w == 1)
                r.then_inc(S["rt_ps"], 1)

            def down(g):
                n_ = g // 4
                if g % 4 == 0:
                    pe.wait_ge(S["hh_ready"], CH * (n_ + 1))
                if g == 0:
                    pe.wait_ge(S["ld_w2"], 48)
                if g >= 2:
                    pe.wait_ge(S["mix_ready"], g - 1)
                o = bank[4 + g % 2]
                c = slice(P * (g % 4), P * (g % 4) + P)
                for k in range(NE // 2):
                    mm(o[:, P * k:P * k + P], hh[:, n_ % 2, NE + k, c], w2x[:, k, :], True, False)
                    for i in range(2):
                        e = 2 * k + i
                        r = mm(o[:, C * e:C * e + C], hh[:, n_ % 2, e, c], w2s[:, e, :], False, i == 1)
                r.then_inc(S["w2_ps"], 1)

            for n_ in range(PAIRS + 1):
                for j in range(CH):
                    u = CH * n_ + j
                    if n_ < PAIRS:
                        rhs = fTs[:, 4 * n_:4 * n_ + 4, :].rearrange("p a b -> p (a b)")
                        for w_, b0, read, done in ((w1h, 0, "sil_ready", "a_ps"), (w3h, 2, "hh_ready", "b_ps")):
                            if u == 0:
                                pe.wait_ge(S["max_ready"], 3 * B)
                            if u >= 2:
                                pe.wait_ge(S[read], u - 1)
                            for w in range(2):
                                r = mm(bank[b0 + u % 2][:, :], w_[:, w, j, :], rhs, w == 0, w == 1)
                            r.then_inc(S[done], 1)
                    if n_ and j % 3 == 1:
                        down(4 * (n_ - 1) + j // 3)


def kernel(**inputs):
    import numpy as _np
    import concourse.bacc as _bacc
    from concourse import mybir as _mybir
    from concourse.bass_utils import run_bass_kernel_spmd as _run

    a = {k: _np.asarray(v) for k, v in inputs.items()}
    t = {k[3:]: v for k, v in a.items() if k != "x"}

    def cat(*xs):
        return _np.concatenate(xs, axis=1)

    tcn_w = cat(t["tok_conv_w"].transpose(2, 0, 3, 1).reshape(C, -1),
                t["tok_pw_w"].transpose(2, 0, 1).reshape(C, -1),
                t["tok_out1_w"].T, t["tok_out2_w"].T)
    tcn_b = cat(t["tok_conv_b"].T, t["tok_pw_b"].T, t["tok_out1_b"][:, None])
    emb = cat(t["tok_byte_embed"].T, t["tok_in_w"].T, t["tok_channel_embed"][0][:, None],
              t["tok_start_token"][:, None])
    inv = 1.0 / 10000.0 ** (_np.arange(0, HD, 2, dtype=_np.float32) / HD)
    ang = _np.outer(_np.arange(T, dtype=_np.float32), inv)
    ang = _np.concatenate([ang, ang], axis=-1)
    sign = _np.repeat(_np.array([-1.0, 1.0], _np.float32), HD // 2)
    scale = _np.repeat(_np.array([0.25] * NH + [1.0] * NKV, _np.float32), HD)[None] / FFN_SCALE
    cos_t = (_np.tile(_np.cos(ang), (1, NH + NKV)) * scale).astype(_np.float32)
    sin_t = (_np.tile(_np.sin(ang) * sign, (1, NH + NKV)) * scale).astype(_np.float32)
    arrs = {
        "x": a["x"], "tcn_w": tcn_w, "tcn_b": tcn_b, "out2_b": t["tok_out2_b"][None, :], "emb": emb,
        "in_b": t["tok_in_b"][None, :],
        "attn_q": t["attn_Q"].transpose(1, 0, 2).reshape(C, HEADS * C),
        "attn_e": t["attn_E"].transpose(0, 2, 1),
        "qkv_w": cat(t["ffn_wq"].T, t["ffn_wk"].T, t["ffn_wv"].T),
        "wo_t": t["ffn_wo"].T, "ln1": t["ffn_ln1_w"][:, None], "ln2": t["ffn_ln2_w"][:, None],
        "router": t["ffn_router_w"].T,
        "w1m": t["ffn_w1"][:, :MAIN].transpose(2, 0, 1), "w1r": t["ffn_w1"][:, MAIN:].transpose(2, 0, 1),
        "w3m": t["ffn_w3"][:, :MAIN].transpose(2, 0, 1), "w3r": t["ffn_w3"][:, MAIN:].transpose(2, 0, 1),
        "w2m": t["ffn_w2"][:, :, :MAIN].transpose(2, 0, 1), "w2r": t["ffn_w2"][:, :, MAIN:].transpose(2, 0, 1),
        "cos_t": cos_t, "sin_t": sin_t,
    }
    nc = _bacc.Bacc("TRN2", target_bir_lowering=False, num_devices=1)
    arrays, args = {}, []
    for name, v in arrs.items():
        v = _np.ascontiguousarray(v)
        arrays[f"in_{name}_dram"] = v
        args.append(nc.dram_tensor(f"in_{name}_dram", v.shape, _mybir.dt.from_np(v.dtype), kind="ExternalInput").ap())
    args.append(nc.dram_tensor("out_0_dram", (B, T, C), _mybir.dt.float32, kind="ExternalOutput").ap())
    tower(nc, *args)
    r = _run(nc, [arrays], core_ids=[0])
    return r.results[0]["out_0_dram"]
```

```python
import concourse.bass as bass
from concourse import mybir
from contextlib import ExitStack
import numpy as np

B, T, C, V, EMB = 8, 256, 64, 64, 32
LAYERS, TAPS, PAD = 6, 3, 64
HEADS = 8
NH, NKV, HD = 4, 2, 16
NE, HID, MAIN = 8, 170, 128
REM = HID - MAIN
PAIRS, TILES, P = 4, 16, 128
CH = NE + NE // 2
NEG = -1e30
ATT_SCALE, FFN_SCALE = 64.0, 16.0


def tower(nc, x, tcn_w, tcn_b, out2_b, emb, in_b, attn_q, attn_e, qkv_w, wo_t, ln1, ln2, router,
          w1m, w1r, w3m, w3r, w2m, w2r, cos_t, sin_t, out):
    f32, f16, bf16, i32 = mybir.dt.float32, mybir.dt.float16, mybir.dt.bfloat16, mybir.dt.int32
    ALU = mybir.AluOpType
    ACT = mybir.ActivationFunctionType
    AX = mybir.AxisListType.X
    NBLK = 3 * LAYERS + LAYERS + 2

    ctx = ExitStack()
    with ctx:
        def sb(name, shape, dt=f32):
            return ctx.enter_context(nc.sbuf_tensor(name, shape, dt))

        def sem(name):
            return ctx.enter_context(nc.semaphore(name))

        bank = [ctx.enter_context(nc.psum_tensor(f"bank{i}", [P, 512], f32)) for i in range(8)]

        NW, NX = NBLK * P, 4 * (PAD + T)
        early = sb("early", [P, NW + NX + 2048])
        Wt = early[:, 0:NW].rearrange("p (n o) -> p n o", o=P)
        Xp = early[:, NW:NW + NX].rearrange("p (b t) -> p b t", b=4)
        hid1 = early[:, NW + NX:NW + NX + 1024].rearrange("p (a c) -> p a c", a=2)
        hid2 = early[:, NW + NX + 1024:NW + NX + 2048].rearrange("p (a c) -> p a c", a=2)
        qkT = early[0:96, 0:TILES * 6 * P // 2].bitcast(bf16).rearrange("p (g n t) -> p g n t", n=6, t=P)
        bt = sb("bt", [P, 2 * LAYERS + 1])
        b2bc = sb("b2bc", [P, V])
        idx = sb("idx", [P, 4, T], i32)
        onehot = sb("onehot", [P, 4, T])
        vcol_i = sb("vcol_i", [P, 1], i32)
        vcol = sb("vcol", [P, 1])
        embp = sb("embp", [EMB + 1, 2 * V + 2])
        embc = sb("embc", [EMB + 1, 2, V])
        inw2 = sb("inw2", [EMB + 1, 2, C])
        startc = sb("startc", [EMB + 1, 1])
        table = sb("table", [P, P])
        identf = sb("identf", [P, P])
        ident16 = sb("ident16", [P, P], f16)
        identb = sb("identb", [P, P], bf16)
        trimul = sb("trimul", [P, 64])
        mask_t = sb("mask_t", [P, 4, P], bf16)
        mask_s = sb("mask_s", [P, 4, P], bf16)
        selh = sb("selh", [3 * NH, NH, P], bf16)
        neghalf = sb("neghalf", [P, 4])
        L = sb("L", [P, TILES, V])
        h = sb("h", [P, TILES, V])
        cen = sb("cen", [P, 2, 4, V])
        sqr = sb("sqr", [P, 2, 4, V])
        ex = sb("ex", [P, 2, 4, V])
        stat = sb("stat", [P, 16, TILES])
        s2 = sb("s2", [P, 2, 4, 2, V])
        shl = sb("shl", [P, 2, 4, 2, V], f16)
        qw = sb("qw", [P, 4, P])
        qwh = sb("qwh", [P, 2, 4, P], f16)
        ew = sb("ew", [P, 4, C])
        sTs = sb("sTs", [P, TILES, P], f16)
        shared = sb("shared", [P, 2 * CH * 512])
        bdT = shared[:, 0:4096].rearrange("p (n u) -> p n u", u=P)
        bdS = shared[:, 4096:8192].rearrange("p (n u) -> p n u", u=P)
        bdM = shared[:, 8192:11264].rearrange("p (b k u) -> p b k u", k=3, u=P)
        om = shared[:, 11264:12288].rearrange("p (a c) -> p a c", a=2)
        hh = shared[:, :].rearrange("p (a j c) -> p a j c", a=2, j=CH)
        qT = sb("qT", [P, 2, 4, 512])
        oT = sb("oT", [P, 2, 4, P])
        xf = sb("xf", [P, TILES, C])
        hx = sb("hx", [P, TILES, C])
        qkvw = sb("qkvw", [P, P])
        qkvh = sb("qkvh", [P, 2, P], f16)
        lns = sb("lns", [P, 2])
        NWO = NH * C + NH
        wo_sb = sb("wo_sb", [P, NWO])
        cos4 = sb("cos4", [P, 4, 96])
        sin4 = sb("sin4", [P, 4, 96])
        hTs = sb("hTs", [P, TILES, P], f16)
        rope = sb("rope", [P, 4, 96])
        rot = sb("rot", [P, 4, 96])
        qst = sb("qst", [P, 2, 4, 6, 6, HD], bf16)
        vaug = sb("vaug", [P, TILES, NKV, 32])
        nmx = sb("nmx", [P, TILES, NH])
        nmr = sb("nmr", [P, 2, 2, NH])
        nms = sb("nms", [P, 2, 2, NH, 3], bf16)
        nmT = sb("nmT", [3 * NH, 2, 2, P], bf16)
        pT = qT[:, :, 0:3, :]
        rec = sb("rec", [P, TILES, NH])
        yT = sb("yT", [P, 2, T])
        ym = sb("ym", [P, 2, 2, NH, C])
        cenB = sb("cenB", [P, 4, V])
        sqrB = sb("sqrB", [P, 4, V])
        hrB = sb("hrB", [P, 4, V])
        shlB = sb("shlB", [P, 4, 2, V], f16)
        rw = sb("rw", [P, NE])
        rwh = sb("rwh", [P, 2, NE], f16)
        w1s = sb("w1s", [P, CH, P])
        w1h = sb("w1h", [P, 2, CH, P], f16)
        w3h = sb("w3h", [P, 2, CH, P], f16)
        w2s = sb("w2s", [P, NE, C])
        w2x = sb("w2x", [P, NE // 2, P])
        x2 = idx[:, :, :].rearrange("p a b -> p (a b)").bitcast(f32).rearrange("p (g c) -> p g c", c=C)
        fTs = onehot[:, :, :].rearrange("p a b -> p (a b)").bitcast(f16).rearrange("p (g c) -> p g c", c=P)
        lg = sb("lg", [P, 2, 4, NE])
        ge = sqr[:, 0, :, :].rearrange("p a (i j) -> p a i j", j=NE)
        gt = sqr[:, 1, :, :].rearrange("p a (i j) -> p a i j", j=NE)
        lowidx = sb("lowidx", [P, NE, NE])
        gate = sb("gate", [P, TILES, NE])
        sil = qT[:, :, 3, :]
        moe = qst[:, :, :, :, :, :].rearrange("p a b c d e -> p (a b c d e)")[:, 0:2 * 2 * NE * C].bitcast(f32) \
            .rearrange("p (a e c) -> p a e c", a=2, e=NE)
        fin = L

        names = ["ld_tok", "ld_emb", "ld_tcn0", "ld_tcn1", "ld_attn", "ld_ffn", "ld_w1", "ld_w3", "ld_w2", "stored",
                 "gchain", "consts", "memz", "bd_zero", "vchain", "embc_ready", "table_ps", "table_ready",
                 "onehot_ready", "emb_ps", "x_ready", "conv_ps", "hid_ready", "pw_ps", "pw_gelu", "out1_ps",
                 "logits_ps", "logits_read", "lsub_ready", "exp_ready", "lsum_ready", "ln_ready", "var_ready", "rstd_ready",
                 "s_ready", "shl_ready", "h_ready", "tr32_ps", "tr16_ps", "sTs_ready", "bdT_ready", "bdS_ready",
                 "M_ps", "M_ready", "q_ps", "q_ready", "om_ps", "om_ready", "o_ps", "o_ready", "e_ps", "h2_ready",
                 "var2_ready", "rstd2_ready", "q1_ready", "rinv_ready", "hr_ready", "hsplit_ready", "trh_ps", "hTs_ready",
                 "qkv_ps", "rope_ready", "v_ready", "split_ready", "stk_ps", "stk_ready", "p1_ps", "max_ready",
                 "nms_ready", "nmT_ps", "nmT_ready", "p2_ps", "exp2_ready", "y_ps", "y_ready", "yT_ps", "yT_ready",
                 "wo_ps", "x2_ready", "ym_ready", "ss_ready", "r2_ready", "fs_ready", "fsplit_ready", "trf_ps", "fTs_ready",
                 "rt_ps", "rexp_in", "rexp_ready", "gate_ready", "a_ps", "b_ps", "sil_ready", "hh_ready", "w2_ps",
                 "mix_ready", "fin_ready", "wts_ready", "w1cast", "wt_zero_low", "wt_zero_high"]
        S = {n: sem(n) for n in names}

        QKV_BANK = (5, 5, 2, 0)

        STACK_B = {0: (6, 7), 1: (8, 9), 2: (10, 11), 4: (12, 13), 5: (14, 15)}

        def stack_bank(g):
            return g % 2 if g < 6 else 1

        block = ctx.enter_context(nc.Block())

        def xrows(half):
            return x[4 * half:4 * half + 4, 0:T - 1]

        @block.sync
        def _(sp):
            for half in range(2):
                sp.dma_start(idx[64 * half:64 * half + 64, :, 1:T],
                             xrows(half).unsqueeze(0).to_broadcast([64, 4, T - 1])).then_inc(S["ld_tok"], 16)
            sp.dma_start(embp[0:EMB, :], emb[:, :]).then_inc(S["ld_emb"], 16)
            sp.dma_start(embp[EMB:EMB + 1, V:2 * V], in_b[:, :]).then_inc(S["ld_emb"], 16)
            tw = tcn_w.rearrange("c (n o) -> c n o", o=C)
            for lo, hi, s in ((0, TAPS + 1, "ld_tcn0"), (TAPS + 1, NBLK, "ld_tcn1")):
                for half in range(2):
                    q = slice(64 * half, 64 * half + 64)
                    sp.dma_start(Wt[q, lo:hi, q], tw[:, lo:hi, :]).then_inc(S[s], 16)
                if lo == 0:
                    for half in range(2):
                        sp.dma_start(bt[64 * half:64 * half + 64, :], tcn_b[:, :]).then_inc(S[s], 16)
            sp.dma_start(b2bc[:, :], out2_b[:, :].to_broadcast([P, V])).then_inc(S["ld_tcn1"], 16)
            for half in range(2):
                q = slice(64 * half, 64 * half + 64)
                sp.dma_start(qw[q, :, :], attn_q.rearrange("c (a m) -> c a m", m=P)).then_inc(S["ld_attn"], 16)
            sp.dma_start(ew[:, :, :], attn_e.rearrange("(a two) j i -> (two j) a i", two=2)).then_inc(S["ld_attn"], 16)
            for half in range(2):
                q = slice(64 * half, 64 * half + 64)
                sp.dma_start(qkvw[q, :], qkv_w[:, :]).then_inc(S["ld_ffn"], 16)
                sp.dma_start(lns[q, 0:1], ln1[:, :]).then_inc(S["ld_ffn"], 16)
                sp.dma_start(lns[q, 1:2], ln2[:, :]).then_inc(S["ld_ffn"], 16)
                sp.dma_start(rw[q, :], router[:, :]).then_inc(S["ld_ffn"], 16)
                tt = cos_t.rearrange("(a p) c -> p a c", a=2)
                sp.dma_start(cos4[:, 2 * half:2 * half + 2, :], tt).then_inc(S["ld_ffn"], 16)
                tt = sin_t.rearrange("(a p) c -> p a c", a=2)
                sp.dma_start(sin4[:, 2 * half:2 * half + 2, :], tt).then_inc(S["ld_ffn"], 16)
            sp.wait_ge(S["bd_zero"], 2)
            for n_ in range(NH):
                sp.dma_start(wo_sb[32 * n_:32 * n_ + HD, C * n_:C * n_ + C],
                             wo_t[HD * n_:HD * n_ + HD, :]).then_inc(S["ld_ffn"], 16)
            sp.dma_start(w2s[:, :, :], w2m[:, :, :]).then_inc(S["ld_w2"], 16)
            w2v = w2r.rearrange("r (k two) c -> r k two c", two=2)
            for half in range(2):
                sp.dma_start(w2x[64 * half:64 * half + REM, :, 64 * half:64 * half + 64],
                             w2v[:, :, half, :]).then_inc(S["ld_w2"], 16)
            for n, (wm, wr, s) in enumerate(((w1m, w1r, "ld_w1"), (w3m, w3r, "ld_w3"))):
                if n:
                    sp.wait_ge(S["w1cast"], 1)
                for half in range(2):
                    q = slice(64 * half, 64 * half + 64)
                    sp.dma_start(w1s[q, 0:NE, :], wm[:, :, :]).then_inc(S[s], 16)
                    sp.dma_start(w1s[q, NE:CH, :].rearrange("c k (two r) -> c (k two) r", two=2)[:, :, 0:REM],
                                 wr[:, :, :]).then_inc(S[s], 16)
            ov = out.rearrange("(hf p) (tt q) c -> q p hf tt c", hf=2, tt=2)
            for g in range(TILES):
                p_, hf, tt = g // 4, (g // 2) % 2, g % 2
                sp.wait_ge(S["fin_ready"], g + 1)
                sp.dma_start(ov[:, p_, hf, tt, :], fin[:, g, :]).then_inc(S["stored"], 16)
            sp.wait_ge(S["stored"], 16 * TILES)

        @block.gpsimd
        def _(pool):
            n = [0]

            def link(ins):
                n[0] += 1
                ins.then_inc(S["gchain"], 1)
                pool.wait_ge(S["gchain"], n[0])

            made = [0]

            def const(ins):
                made[0] += 1
                ins.then_inc(S["consts"], 1)
                pool.wait_ge(S["consts"], made[0])

            nc.gpsimd.iota(vcol_i[0:64, :], [[0, 1]], base=0, channel_multiplier=1).then_inc(S["bd_zero"], 1)
            link(nc.gpsimd.iota(vcol_i[64:P, :], [[0, 1]], base=0, channel_multiplier=1))
            pool.wait_ge(S["bd_zero"], 1)
            const(nc.gpsimd.tensor_copy(vcol[:, :], vcol_i[:, :]))
            nc.gpsimd.memset(Wt[64:P, :, 0:64], 0.0).then_inc(S["wt_zero_low"], 1)
            pool.wait_ge(S["wt_zero_low"], 1)
            nc.gpsimd.memset(w2x[:, :, :], 0.0).then_inc(S["memz"], 1)
            nc.gpsimd.memset(w1s[:, NE:CH, :], 0.0).then_inc(S["memz"], 1)
            pool.wait_ge(S["memz"], 2)
            link(nc.gpsimd.memset(wo_sb[:, :], 0.0))
            nc.gpsimd.affine_select(out=wo_sb[:, NH * C:NWO], in_=wo_sb[:, NH * C:NWO],
                                    compare_op=ALU.not_equal, fill=1.0, base=-HD, pattern=[[-32, NH]],
                                    channel_multiplier=1).then_inc(S["bd_zero"], 1)
            pool.wait_ge(S["bd_zero"], 2)
            link(nc.gpsimd.memset(identf[:, :], 0.0))
            link(nc.gpsimd.affine_select(out=identf[:, :], in_=identf[:, :], compare_op=ALU.not_equal, fill=1.0,
                                         base=0, pattern=[[-1, P]], channel_multiplier=1))
            const(nc.gpsimd.tensor_copy(ident16[:, :], identf[:, :]))
            const(nc.gpsimd.tensor_copy(identb[:, :], identf[:, :]))
            link(nc.gpsimd.memset(trimul[:, :], 1.0))
            for half in range(2):
                q = slice(64 * half, 64 * half + 64)
                const(nc.gpsimd.affine_select(out=trimul[q, :], in_=trimul[q, :], compare_op=ALU.is_ge, fill=0.0, base=0,
                                        pattern=[[1, 64]], channel_multiplier=-1))
            const(nc.gpsimd.memset(neghalf[:, :], -0.5))
            const(nc.gpsimd.memset(bdT[:, :, :], 0.0))
            const(nc.gpsimd.memset(bdS[:, :, :], 0.0))
            const(nc.gpsimd.memset(bdM[:, :, :, :], 0.0))
            for m in (mask_t, mask_s):
                link(nc.gpsimd.memset(m[:, :, :], 0.0))
            for m, sgn in ((mask_t, -1), (mask_s, 1)):
                const(nc.gpsimd.affine_select(out=m[:, :, :], in_=m[:, :, :], compare_op=ALU.is_ge, fill=NEG, base=0,
                                              pattern=[[0, NH], [sgn, P]], channel_multiplier=-sgn))
            link(nc.gpsimd.memset(selh[:, :, :], 1.0))
            link(nc.gpsimd.affine_select(out=selh[:, :, :], in_=selh[:, :, :], compare_op=ALU.is_ge, fill=0.0, base=0,
                                         pattern=[[-3, NH], [0, P]], channel_multiplier=1))
            const(nc.gpsimd.affine_select(out=selh[:, :, :], in_=selh[:, :, :], compare_op=ALU.is_ge, fill=0.0, base=2,
                                    pattern=[[3, NH], [0, P]], channel_multiplier=-1))
            const(nc.gpsimd.memset(vaug[:, :, :, :], 1.0))
            link(nc.gpsimd.memset(lowidx[:, :, :], 1.0))
            const(nc.gpsimd.affine_select(out=lowidx[:, :, :], in_=lowidx[:, :, :], compare_op=ALU.is_gt, fill=0.0, base=0,
                                    pattern=[[1, NE], [-1, NE]], channel_multiplier=0))

            def split(dst, src, ready):
                link(nc.gpsimd.tensor_copy(dst[:, :, 0, :], src))
                nc.gpsimd.tensor_tensor(dst[:, :, 1, :], src, dst[:, :, 0, :], ALU.subtract).then_inc(S[ready], 1)

            def inverse_root(dst, src, p, before, ready):
                g4 = slice(4 * p, 4 * p + 4)
                pool.wait_ge(S[before], p + 1)
                nc.gpsimd.tensor_tensor(stat[:, dst, g4], stat[:, src, g4], neghalf[:, 0:4], ALU.pow) \
                    .then_inc(S[ready], 1)

            def variance_root(p):
                inverse_root(4, 3, p, "var_ready", "rstd_ready")

            def first_split(p):
                pool.wait_ge(S["s_ready"], p + 1)
                if p >= 2:
                    pool.wait_ge(S["tr16_ps"], p - 1)
                split(shl[:, p % 2], s2[:, p % 2, :, 0, :], "shl_ready")

            def first_h(p):
                g4 = slice(4 * p, 4 * p + 4)
                pool.wait_ge(S["ln_ready"], 1)
                nc.gpsimd.tensor_tensor(h[:, g4, :], L[:, g4, :], stat[:, 1, g4].unsqueeze(2)
                                        .to_broadcast([P, 4, V]), ALU.subtract).then_inc(S["h_ready"], 1)

            def variance2_root(p):
                inverse_root(12, 11, p, "var2_ready", "rstd2_ready")

            def square2_root(p):
                inverse_root(6, 5, p, "q1_ready", "rinv_ready")

            def second_split(p):
                pool.wait_ge(S["hr_ready"], p + 1)
                if p:
                    pool.wait_ge(S["trh_ps"], p)
                split(shlB[:, :, :, :], hrB[:, :, :], "hsplit_ready")

            def third_root(p):
                inverse_root(8, 7, p, "ss_ready", "r2_ready")

            def third_split(p):
                pool.wait_ge(S["fs_ready"], p + 1)
                if p >= 2:
                    pool.wait_ge(S["trf_ps"], p - 1)
                split(shl[:, p % 2], s2[:, p % 2, :, 0, :], "fsplit_ready")

            def head_sum(b):
                pool.wait_ge(S["ym_ready"], 2 * b + 2)
                m = ym[:, b % 2, :, :, :]
                link(nc.gpsimd.tensor_tensor(m[:, :, 0:2, :], m[:, :, 0:2, :], m[:, :, 2:4, :], ALU.add))
                link(nc.gpsimd.tensor_tensor(m[:, :, 0, :], m[:, :, 0, :], m[:, :, 1, :], ALU.add))
                nc.gpsimd.tensor_tensor(x2[:, 2 * b:2 * b + 2, :], m[:, :, 0, :], xf[:, 2 * b:2 * b + 2, :],
                                        ALU.add).then_inc(S["x2_ready"], 1)
                pool.wait_ge(S["x2_ready"], b + 1)

            variance_root(0)
            first_split(0)
            variance_root(1)
            for g in range(TILES):
                p, s = g // 4, g % 4
                if s == 0 and p + 1 < PAIRS:
                    first_split(p + 1)
                if s == 1:
                    first_h(p)
                    if p:
                        variance2_root(p - 1)
                if s == 2 and p:
                    square2_root(p - 1)
                if s == 3:
                    if p:
                        second_split(p - 1)
                    if p + 2 < PAIRS:
                        variance_root(p + 2)
            variance2_root(PAIRS - 1)
            square2_root(PAIRS - 1)
            second_split(PAIRS - 1)
            for b in range(1, B + 1):
                if b in (3, 5, 7):
                    third_root((b - 3) // 2)
                if b in (4, 6, 8):
                    third_split((b - 4) // 2)
                head_sum(b - 1)
            third_root(PAIRS - 1)
            third_split(PAIRS - 1)
            for p in range(PAIRS):
                g4 = slice(4 * p, 4 * p + 4)
                link(nc.gpsimd.tensor_tensor(hx[:, g4, :], h[:, g4, :], x2[:, g4, :], ALU.add))
            for g in range(TILES):
                pool.wait_ge(S["mix_ready"], g + 1)
                m = moe[:, g % 2, :, :]
                link(nc.gpsimd.tensor_tensor(m[:, 0:4, :], m[:, 0:4, :], m[:, 4:8, :], ALU.add))
                link(nc.gpsimd.tensor_tensor(m[:, 0:2, :], m[:, 0:2, :], m[:, 2:4, :], ALU.add))
                link(nc.gpsimd.tensor_tensor(m[:, 0, :], m[:, 0, :], m[:, 1, :], ALU.add))
                nc.gpsimd.tensor_tensor(fin[:, g, :], m[:, 0, :], hx[:, g, :], ALU.add).then_inc(S["fin_ready"], 1)

        @block.scalar
        def _(act):
            def conv_gelu(l, gm):
                act.wait_ge(S["conv_ps"], 2 * l + gm + 1)
                if l:
                    act.wait_ge(S["pw_ps"], 2 * (l - 1) + gm + 1)
                nc.scalar.activation(hid1[:, gm, :], bank[gm][:, :], ACT.Gelu,
                                     bias=bt[:, l:l + 1]).then_inc(S["hid_ready"], 1)

            def pw_gelu(l, gm):
                act.wait_ge(S["pw_ps"], 2 * l + gm + 1)
                if l:
                    act.wait_ge(S["x_ready"], 2 + 2 * (l - 1) + gm + 1)
                nc.scalar.activation(hid2[:, gm, :], bank[2 + gm][:, :], ACT.Gelu,
                                     bias=bt[:, LAYERS + l:LAYERS + l + 1]).then_inc(S["pw_gelu"], 1)

            act.wait_ge(S["ld_tcn0"], 64)
            for l in range(LAYERS):
                for gm in range(2):
                    conv_gelu(l, gm)
                for gm in range(2):
                    pw_gelu(l, gm)
            for gm in range(2):
                act.wait_ge(S["out1_ps"], gm + 1)
                nc.scalar.activation(hid1[:, gm, :], bank[gm][:, :], ACT.Gelu,
                                     bias=bt[:, 2 * LAYERS:2 * LAYERS + 1]).then_inc(S["hid_ready"], 1)

            def exponentials(p):
                act.wait_ge(S["lsub_ready"], p + 1)
                if p >= 2:
                    act.wait_ge(S["lsum_ready"], p - 1)
                nc.scalar.activation(ex[:, p % 2, :, :], L[:, 4 * p:4 * p + 4, :], ACT.Exp) \
                    .then_inc(S["exp_ready"], 1)

            def chunk_rows(p):
                act.wait_ge(S["s_ready"], p + 1)
                act.wait_ge(S["consts"], 9)
                for src in range(2):
                    for dst in range(2):
                        sq = slice(64 * src, 64 * src + 64)
                        dq = slice(64 * dst, 64 * dst + 64)
                        o = bdS[dq, 8 * p:8 * p + 8, dq].rearrange("p (a cc) i -> p a cc i", cc=2)[:, :, src, :]
                        r = nc.scalar.copy(o, s2[sq, p % 2, :, dst, :])
                r.then_inc(S["bdS_ready"], 1)

            def turned_rows(p):
                act.wait_ge(S["tr32_ps"], p + 1)
                for hf in range(2):
                    q = slice(64 * hf, 64 * hf + 64)
                    r = nc.scalar.copy(bdT[q, 8 * p:8 * p + 8, q], bank[0][q, :].rearrange("p (a u) -> p a u", u=64))
                r.then_inc(S["bdT_ready"], 1)
                act.wait_ge(S["tr16_ps"], p + 1)
                nc.scalar.copy(sTs[:, 4 * p:4 * p + 4, :].rearrange("p a b -> p (a b)"),
                               bank[1][:, 0:256].bitcast(f16)).then_inc(S["sTs_ready"], 1)

            def outer_out(p):
                act.wait_ge(S["M_ps"], p + 1)
                for hf in range(2):
                    q = slice(64 * hf, 64 * hf + 64)
                    r = nc.scalar.copy(bdM[q, 2 * p:2 * p + 2, :, q],
                                       bank[1][q, 0:384].rearrange("p (b k j) -> p b k j", b=2, k=3))
                r.then_inc(S["M_ready"], 1)

            def q_out(p, a):
                act.wait_ge(S["q_ps"], 4 * p + a + 1)
                if p >= 2:
                    act.wait_ge(S["o_ps"], 4 * (p - 1))
                nc.scalar.mul(qT[:, p % 2, a, :], bank[2 + a % 2][:, :], 1.0 / ATT_SCALE).then_inc(S["q_ready"], 1)

            def o_out(g):
                act.wait_ge(S["o_ps"], g + 1)
                if g >= 2:
                    act.wait_ge(S["e_ps"], g - 1)
                nc.scalar.copy(oT[:, g % 2, :, :].rearrange("p a (cc t) -> p cc a t", cc=2),
                               bank[6][:, :].rearrange("p (cc a t) -> p cc a t", cc=2, a=4)) \
                    .then_inc(S["o_ready"], 1)

            def h_rows(p):
                act.wait_ge(S["trh_ps"], p + 1)
                nc.scalar.copy(hTs[:, 4 * p:4 * p + 4, :].rearrange("p a b -> p (a b)"),
                               bank[QKV_BANK[p]][:, 0:256].bitcast(f16)).then_inc(S["hTs_ready"], 1)

            def stacked(g):
                act.wait_ge(S["stk_ps"], g + 1)
                nc.scalar.copy(qkT[:, g, :, :].rearrange("p a b -> p (a b)"),
                               bank[stack_bank(g)][0:96, 0:384].bitcast(bf16)).then_inc(S["stk_ready"], 1)

            exponentials(0)
            chunk_rows(0)
            turned_rows(0)
            outer_out(0)
            for a in range(4):
                q_out(0, a)
            for p in range(1, PAIRS):
                exponentials(p)
            act.wait_ge(S["lsum_ready"], PAIRS)
            nc.scalar.activation(stat[:, 1, :], stat[:, 0, :], ACT.Ln).then_inc(S["ln_ready"], 1)
            for g in range(TILES):
                p, s = g // 4, g % 4
                o_out(g)
                if s == 0 and p + 1 < PAIRS:
                    chunk_rows(p + 1)
                if s == 0 and p >= 2:
                    h_rows(p - 2)
                if s == 1 and p + 1 < PAIRS:
                    turned_rows(p + 1)
                if s == 2 and p + 1 < PAIRS:
                    outer_out(p + 1)
                    for a in range(4):
                        q_out(p + 1, a)
                if p == PAIRS - 1:
                    stacked(s)

            def probs(b, u):
                act.wait_ge(S["p2_ps"], 3 * b + u + 1)
                if b >= 2:
                    act.wait_ge(S["y_ps"], b - 1)
                nc.scalar.activation(pT[:, b % 2, u, :], bank[5 + (3 * b + u) % 2][:, :],
                                     ACT.Exp).then_inc(S["exp2_ready"], 1)

            def y_rows(b):
                act.wait_ge(S["y_ps"], b + 1)
                if b >= 2:
                    act.wait_ge(S["wo_ps"], 2 * b - 2)
                nc.scalar.copy(yT[:, b % 2, :], bank[7][:, 0:T]).then_inc(S["yT_ready"], 1)

            def f_rows(p, b_):
                act.wait_ge(S["trf_ps"], p + 1)
                nc.scalar.copy(fTs[:, 4 * p:4 * p + 4, :].rearrange("p a b -> p (a b)"),
                               bank[b_][:, 0:256].bitcast(f16)).then_inc(S["fTs_ready"], 1)

            def router_exp(p):
                act.wait_ge(S["rexp_in"], p + 1)
                nc.scalar.activation(lg[:, p % 2, :, :], lg[:, p % 2, :, :], ACT.Exp).then_inc(S["rexp_ready"], 1)

            h_rows(2)
            stacked(4)
            stacked(5)
            for b in range(B + 1):
                if b >= 1:
                    y_rows(b - 1)
                if b in (6, 7):
                    f_rows(b - 6, 1)
                if b in (7, 8):
                    router_exp(b - 7)
                for u in range(3):
                    if u == 1 and b in STACK_B:
                        stacked(STACK_B[b][0])
                    if b < B:
                        probs(b, u)
                if b in STACK_B:
                    stacked(STACK_B[b][1])
                if b == 1:
                    h_rows(3)
            for n in range(PAIRS):
                for j in range(CH):
                    u = CH * n + j
                    if n == 0 and j == 2:
                        f_rows(2, 6)
                    if n == 0 and j == 9:
                        f_rows(3, 6)
                    if n == 1 and j == 3:
                        router_exp(2)
                        router_exp(3)
                    act.wait_ge(S["a_ps"], u + 1)
                    if u >= 2:
                        act.wait_ge(S["hh_ready"], u - 1)
                    nc.scalar.activation(sil[:, u % 2, :], bank[u % 2][:, :], ACT.Silu,
                                         scale=1.0 / FFN_SCALE).then_inc(S["sil_ready"], 1)

        @block.vector
        def _(dve):
            n = [0]

            def link(ins):
                n[0] += 1
                ins.then_inc(S["vchain"], 1)
                dve.wait_ge(S["vchain"], n[0])

            V_ = nc.vector

            V_.memset(Wt[0:64, :, 64:P], 0.0).then_inc(S["wt_zero_high"], 1)
            link(V_.memset(embc[:, :, :], 1.0))
            link(V_.memset(startc[:, :], 1.0))
            link(V_.memset(table[:, :], 0.0))
            link(V_.memset(Xp[:, :, 0:PAD], 0.0))
            dve.wait_ge(S["ld_emb"], 32)
            for d in range(2):
                link(V_.tensor_scalar(embc[0:EMB, d, :], embp[0:EMB, 0:V], embp[0:EMB, 2 * V:2 * V + 1], None,
                                      ALU.add))
                link(V_.tensor_copy(inw2[:, d, :], embp[:, V:2 * V]))
            V_.tensor_tensor(startc[0:EMB, :], embp[0:EMB, 2 * V + 1:2 * V + 2], embp[0:EMB, 2 * V:2 * V + 1],
                             ALU.add).then_inc(S["embc_ready"], 1)
            dve.wait_ge(S["consts"], 1)
            dve.wait_ge(S["ld_tok"], 32)
            for gm in range(2):
                V_.tensor_scalar(onehot[:, 2 * gm:2 * gm + 2, 1:T], idx[:, 2 * gm:2 * gm + 2, 1:T], vcol[:, 0:1],
                                 None, ALU.is_equal).then_inc(S["onehot_ready"], 1)
            dve.wait_ge(S["table_ps"], 1)
            link(V_.tensor_copy(table[0:64, 0:64], bank[4][0:64, 0:64]))
            link(V_.tensor_copy(Xp[:, :, PAD:PAD + 1], bank[4][:, 64:65].unsqueeze(1).to_broadcast([P, 4, 1])))
            V_.tensor_copy(table[64:P, 64:P], bank[4][64:P, 0:64]).then_inc(S["table_ready"], 1)
            for gm in range(2):
                dve.wait_ge(S["emb_ps"], gm + 1)
                V_.tensor_copy(Xp[:, 2 * gm:2 * gm + 2, PAD + 1:PAD + T],
                               bank[gm][:, :].rearrange("p (b t) -> p b t", b=2)[:, :, 1:T]) \
                    .then_inc(S["x_ready"], 1)

            def residual(l, gm):
                dve.wait_ge(S["pw_gelu"], 2 * l + gm + 1)
                dve.wait_ge(S["conv_ps"], 2 * l + gm + 1)
                V_.tensor_tensor(Xp[:, 2 * gm:2 * gm + 2, PAD:PAD + T], Xp[:, 2 * gm:2 * gm + 2, PAD:PAD + T],
                                 hid2[:, gm, :].rearrange("p (b t) -> p b t", b=2), ALU.add) \
                    .then_inc(S["x_ready"], 1)

            def split16(hi, lo, src, scale, scratch):
                link(V_.tensor_scalar(scratch, src, scale, None, ALU.mult))
                link(V_.tensor_copy(hi, scratch))
                link(V_.tensor_tensor(lo, scratch, hi, ALU.subtract))

            def weights_setup(stage):
                if stage == 0:
                    dve.wait_ge(S["ld_attn"], 48)
                    split16(qwh[:, 0, :, :], qwh[:, 1, :, :], qw[:, :, :], ATT_SCALE, qw[:, :, :])
                    V_.tensor_copy(stat[0:1, 11, 0:1], vcol[0:1, :]).then_inc(S["wts_ready"], 1)
                elif stage == 1:
                    dve.wait_ge(S["ld_ffn"], 16 * 16)
                    link(V_.tensor_scalar(qkvw[:, :], qkvw[:, :], lns[:, 0:1], None, ALU.mult))
                    split16(qkvh[:, 0, :], qkvh[:, 1, :], qkvw[:, :], FFN_SCALE, qkvw[:, :])
                    link(V_.tensor_scalar(rw[:, :], rw[:, :], lns[:, 1:2], None, ALU.mult))
                    split16(rwh[:, 0, :], rwh[:, 1, :], rw[:, :], FFN_SCALE, rw[:, :])
                elif stage in (2, 3):
                    dve.wait_ge(S["ld_w1" if stage == 2 else "ld_w3"], 64)
                    dst = w1h if stage == 2 else w3h
                    link(V_.tensor_scalar(w1s[:, :, :], w1s[:, :, :], lns[:, 1:2], FFN_SCALE, ALU.mult, ALU.mult))
                    link(V_.tensor_copy(dst[:, 0, :, :], w1s[:, :, :]))
                    V_.tensor_tensor(dst[:, 1, :, :], w1s[:, :, :], dst[:, 0, :, :], ALU.subtract) \
                        .then_inc(S["w1cast"], 1)
                    dve.wait_ge(S["w1cast"], stage - 1)

            for l in range(LAYERS):
                for gm in range(2):
                    residual(l, gm)
                if 1 <= l <= 4:
                    weights_setup(l - 1)

            def bc4(ap):
                return ap.unsqueeze(2).to_broadcast([P, 4, V])

            def logits_out(p):
                g4 = slice(4 * p, 4 * p + 4)
                dve.wait_ge(S["logits_ps"], p + 1)
                (V_.tensor_tensor(L[:, g4, :].rearrange("p (hf tt) v -> p tt hf v", hf=2),
                                      bank[4 + p][:, 0:256].rearrange("p (tt hf v) -> p tt hf v", tt=2, hf=2),
                                      b2bc[:, :].unsqueeze(1).unsqueeze(1).to_broadcast([P, 2, 2, V]), ALU.add)
                 .then_inc(S["logits_read"], 1))

            def ln0_a(p):
                g4 = slice(4 * p, 4 * p + 4)
                dve.wait_ge(S["logits_read"], p + 1)
                link(V_.tensor_reduce(stat[:, 2, g4], L[:, g4, :], AX, ALU.max))
                V_.tensor_tensor(L[:, g4, :], L[:, g4, :], bc4(stat[:, 2, g4]), ALU.subtract) \
                    .then_inc(S["lsub_ready"], 1)
                dve.wait_ge(S["lsub_ready"], p + 1)

            def centre(p, src, c_, q_, at, ready):
                g4 = slice(4 * p, 4 * p + 4)
                link(V_.tensor_reduce(stat[:, 2, g4], src, AX, ALU.add))
                link(V_.scalar_tensor_tensor(c_, bc4(stat[:, 2, g4]), -1.0 / V, src, ALU.mult, ALU.add))
                link(V_.tensor_tensor(q_, c_, c_, ALU.mult))
                link(V_.tensor_reduce(stat[:, 9, g4], q_, AX, ALU.add))
                V_.tensor_scalar(stat[:, at, g4], stat[:, 9, g4], 1.0 / V, 1e-5, ALU.mult, ALU.add) \
                    .then_inc(S[ready], 1)

            def ln0_b(p):
                centre(p, L[:, 4 * p:4 * p + 4, :], cen[:, p % 2], sqr[:, p % 2], 3, "var_ready")

            def exp_sum(p):
                dve.wait_ge(S["exp_ready"], p + 1)
                V_.tensor_reduce(stat[:, 0, 4 * p:4 * p + 4], ex[:, p % 2, :, :], AX, ALU.add) \
                    .then_inc(S["lsum_ready"], 1)

            def ln0_c(p):
                g4 = slice(4 * p, 4 * p + 4)
                dve.wait_ge(S["rstd_ready"], p + 1)
                if p >= 2:
                    dve.wait_ge(S["shl_ready"], p - 1)
                    dve.wait_ge(S["M_ps"], p - 1)
                    dve.wait_ge(S["bdS_ready"], p - 1)
                V_.tensor_tensor(s2[:, p % 2, :, :, :], cen[:, p % 2, :, :].unsqueeze(2).to_broadcast([P, 4, 2, V]),
                                 stat[:, 4, g4].unsqueeze(2).unsqueeze(2).to_broadcast([P, 4, 2, V]), ALU.mult) \
                    .then_inc(S["s_ready"], 1)

            def mask_omega(g):
                dve.wait_ge(S["om_ps"], g + 1)
                if g >= 2:
                    dve.wait_ge(S["o_ps"], g - 1)
                V_.tensor_tensor(om[:, g % 2, :].rearrange("p (a t) -> p a t", t=64),
                                 bank[4][:, :].rearrange("p (a t) -> p a t", t=64),
                                 trimul[:, :].unsqueeze(1).to_broadcast([P, 8, 64]), ALU.mult) \
                    .then_inc(S["om_ready"], 1)

            def ln2_a(p):
                g4 = slice(4 * p, 4 * p + 4)
                dve.wait_ge(S["e_ps"], 4 * p + 4)
                dve.wait_ge(S["h_ready"], p + 1)
                V_.tensor_tensor(h[:, g4, :], h[:, g4, :], bank[7][:, 0:256].rearrange("p (a c) -> p a c", a=4),
                                 ALU.add).then_inc(S["h2_ready"], 1)
                dve.wait_ge(S["h2_ready"], p + 1)

            def ln2_b(p):
                if p:
                    dve.wait_ge(S["hr_ready"], p)
                centre(p, h[:, 4 * p:4 * p + 4, :], cenB[:, :, :], sqrB[:, :, :], 11, "var2_ready")

            def ln2_c(p):
                g4 = slice(4 * p, 4 * p + 4)
                dve.wait_ge(S["rstd2_ready"], p + 1)
                link(V_.tensor_tensor(xf[:, g4, :], cenB[:, :, :], bc4(stat[:, 12, g4]), ALU.mult))
                link(V_.tensor_tensor(stat[:, 10, g4], stat[:, 12, g4], stat[:, 12, g4], ALU.mult))
                link(V_.tensor_tensor(stat[:, 10, g4], stat[:, 10, g4], stat[:, 9, g4], ALU.mult))
                V_.tensor_scalar(stat[:, 5, g4], stat[:, 10, g4], 1.0 / V, 1e-6, ALU.mult, ALU.add) \
                    .then_inc(S["q1_ready"], 1)

            def ln2_d(p):
                g4 = slice(4 * p, 4 * p + 4)
                dve.wait_ge(S["rinv_ready"], p + 1)
                if p:
                    dve.wait_ge(S["hsplit_ready"], p)
                V_.tensor_tensor(hrB[:, :, :], xf[:, g4, :], bc4(stat[:, 6, g4]), ALU.mult) \
                    .then_inc(S["hr_ready"], 1)

            def rotary(p):
                dve.wait_ge(S["qkv_ps"], p + 1)
                src = bank[QKV_BANK[p]][:, :].rearrange("p (a c) -> p a c", a=4)
                qk = src[:, :, 0:96]
                link(V_.tensor_tensor(rope[:, :, :], qk, cos4[:, :, :], ALU.mult))
                for d in range(2):
                    def half(ap, k):
                        return ap.rearrange("p a (n two e) -> p a n two e", two=2, e=8)[:, :, :, k, :]
                    link(V_.tensor_tensor(half(rot[:, :, :], d), half(qk, 1 - d), half(sin4[:, :, :], d), ALU.mult))
                dve.wait_ge(S["consts"], 13)
                V_.tensor_scalar(vaug[:, 4 * p:4 * p + 4, :, 0:HD],
                                 src[:, :, 96:128].rearrange("p a (n e) -> p a n e", e=HD), 1.0 / FFN_SCALE, None,
                                 ALU.mult).then_inc(S["v_ready"], 1)
                link(V_.tensor_tensor(rope[:, :, :], rope[:, :, :], rot[:, :, :], ALU.add))

            def exact_parts(p):
                if p >= 2:
                    dve.wait_ge(S["stk_ps"], 4 * (p - 1))
                r6 = rope[:, :, :].rearrange("p a (n e) -> p a n e", e=HD)
                t6 = rot[:, :, :].rearrange("p a (n e) -> p a n e", e=HD)
                d_ = qst[:, p % 2, :, :, :, :]
                link(V_.tensor_copy(d_[:, :, :, 0, :], r6))
                link(V_.tensor_tensor(t6, r6, d_[:, :, :, 0, :], ALU.subtract))
                link(V_.tensor_copy(d_[:, :, 0:4, 3, :], t6[:, :, 0:4, :]))
                link(V_.tensor_copy(d_[:, :, 4:6, 1, :], t6[:, :, 4:6, :]))
                V_.tensor_tensor(d_[:, :, 0:4, 5, :], t6[:, :, 0:4, :], d_[:, :, 0:4, 3, :], ALU.subtract)
                V_.tensor_tensor(d_[:, :, 4:6, 2, :], t6[:, :, 4:6, :], d_[:, :, 4:6, 1, :], ALU.subtract)
                V_.tensor_copy(d_[:, :, 0:4, 1, :], d_[:, :, 0:4, 0, :])
                V_.tensor_copy(d_[:, :, 0:4, 2, :], d_[:, :, 0:4, 0, :])
                V_.tensor_copy(d_[:, :, 0:4, 4, :], d_[:, :, 0:4, 3, :])
                V_.tensor_copy(d_[:, :, 4:6, 3, :], d_[:, :, 4:6, 0, :])
                V_.tensor_copy(d_[:, :, 4:6, 5, :], d_[:, :, 4:6, 0, :])
                V_.tensor_copy(d_[:, :, 4:6, 4, :], d_[:, :, 4:6, 1, :]).then_inc(S["split_ready"], 1)
                dve.wait_ge(S["split_ready"], p + 1)

            dve.wait_ge(S["ld_tcn1"], 48)
            logits_out(0)
            ln0_a(0)
            ln0_b(0)
            for p in range(1, PAIRS):
                logits_out(p)
            ln0_c(0)
            exp_sum(0)
            ln0_a(1)
            ln0_b(1)
            ln0_a(2)
            exp_sum(1)
            ln0_a(3)
            exp_sum(2)
            exp_sum(3)
            dve.wait_ge(S["consts"], 6)
            for g in range(TILES):
                p, s = g // 4, g % 4
                mask_omega(g)
                if s == 0 and p + 1 < PAIRS:
                    ln0_c(p + 1)
                if s == 1 and p:
                    ln2_a(p - 1)
                    ln2_b(p - 1)
                if s == 2:
                    if p:
                        ln2_c(p - 1)
                    if p >= 2:
                        rotary(p - 2)
                if s == 3:
                    if p:
                        ln2_d(p - 1)
                    if p + 2 < PAIRS:
                        ln0_b(p + 2)
                    if p >= 2:
                        exact_parts(p - 2)

            def row_max(b):
                for u in range(3):
                    dve.wait_ge(S["p1_ps"], 3 * b + u + 1)
                    g, h0, nh = (2 * b, 0, 4) if u == 0 else (2 * b + 1, 2 * (u - 1), 2)
                    V_.tensor_reduce(nmx[:, g, h0:h0 + nh],
                                     bank[3 + (3 * b + u) % 2][:, :].rearrange("p (n s) -> p n s", n=nh),
                                     AX, ALU.max, negate=True).then_inc(S["max_ready"], 1)
                dve.wait_ge(S["max_ready"], 3 * b + 3)
                src, d_, r_ = nmx[:, 2 * b:2 * b + 2, :], nms[:, b % 2, :, :, :], nmr[:, b % 2, :, :]
                if b >= 2:
                    dve.wait_ge(S["nmT_ps"], b - 1)
                link(V_.tensor_copy(d_[:, :, :, 0], src))
                link(V_.tensor_tensor(r_, src, d_[:, :, :, 0], ALU.subtract))
                link(V_.tensor_copy(d_[:, :, :, 1], r_))
                V_.tensor_tensor(d_[:, :, :, 2], r_, d_[:, :, :, 1], ALU.subtract).then_inc(S["nms_ready"], 1)

            def max_out(b):
                dve.wait_ge(S["nmT_ps"], b + 1)
                if b >= 2:
                    dve.wait_ge(S["p2_ps"], 3 * b - 3)
                V_.tensor_copy(nmT[:, b % 2, :, :].rearrange("p a b -> p (a b)"),
                               bank[0][0:3 * NH, 0:P].bitcast(bf16)).then_inc(S["nmT_ready"], 1)

            def share(g):
                b = g // 2
                dve.wait_ge(S["wo_ps"], g + 1)
                if b >= 2:
                    dve.wait_ge(S["x2_ready"], b - 1)
                link(V_.reciprocal(rec[:, g, :], bank[2][:, NH * C:NWO]))
                V_.tensor_tensor(ym[:, b % 2, g % 2, :, :], bank[2][:, 0:NH * C].rearrange("p (n c) -> p n c", n=NH),
                                 rec[:, g, :].unsqueeze(2).to_broadcast([P, NH, C]), ALU.mult) \
                    .then_inc(S["ym_ready"], 1)

            def rms_square(p):
                g4 = slice(4 * p, 4 * p + 4)
                dve.wait_ge(S["x2_ready"], 2 * p + 2)
                link(V_.tensor_tensor(sqr[:, p % 2, :, :], x2[:, g4, :], x2[:, g4, :], ALU.mult))
                link(V_.tensor_reduce(stat[:, 10, g4], sqr[:, p % 2, :, :], AX, ALU.add))
                V_.tensor_scalar(stat[:, 7, g4], stat[:, 10, g4], 1.0 / C, 1e-6, ALU.mult, ALU.add) \
                    .then_inc(S["ss_ready"], 1)

            def rms_rows(p):
                g4 = slice(4 * p, 4 * p + 4)
                dve.wait_ge(S["r2_ready"], p + 1)
                if p >= 2:
                    dve.wait_ge(S["fsplit_ready"], p - 1)
                V_.tensor_tensor(s2[:, p % 2, :, 0, :], x2[:, g4, :], bc4(stat[:, 8, g4]), ALU.mult) \
                    .then_inc(S["fs_ready"], 1)

            def b8(ap):
                return ap.unsqueeze(2).to_broadcast([P, 4, NE])

            def router_in(p):
                g4 = slice(4 * p, 4 * p + 4)
                dve.wait_ge(S["rt_ps"], p + 1)
                l_ = lg[:, p % 2, :, :]
                ps = bank[1 if p < 2 else 7][:, 0:4 * NE].rearrange("p (a e) -> p a e", a=4)
                link(V_.tensor_reduce(stat[:, 10, g4], ps, AX, ALU.max))
                link(V_.tensor_tensor(l_, ps, b8(stat[:, 10, g4]), ALU.subtract))
                V_.tensor_scalar(l_, l_, 1.0 / FFN_SCALE, None, ALU.mult).then_inc(S["rexp_in"], 1)

            def gates(p):
                g4 = slice(4 * p, 4 * p + 4)
                dve.wait_ge(S["rexp_ready"], p + 1)
                l_ = lg[:, p % 2, :, :]
                e_i = l_.unsqueeze(3).to_broadcast([P, 4, NE, NE])
                e_j = l_.unsqueeze(2).to_broadcast([P, 4, NE, NE])
                low = lowidx[:, :, :].unsqueeze(1).to_broadcast([P, 4, NE, NE])
                link(V_.tensor_tensor(gt[:, :, :, :], e_j, e_i, ALU.is_gt))
                link(V_.tensor_tensor(ge[:, :, :, :], e_j, e_i, ALU.is_ge))
                link(V_.tensor_tensor(ge[:, :, :, :], ge[:, :, :, :], low, ALU.mult))
                link(V_.tensor_tensor(ge[:, :, :, :], ge[:, :, :, :], gt[:, :, :, :], ALU.max))
                link(V_.tensor_reduce(gate[:, g4, :], ge[:, :, :, :], AX, ALU.add))
                link(V_.scalar_tensor_tensor(gate[:, g4, :], gate[:, g4, :], 1.5, l_, ALU.is_lt, ALU.mult))
                link(V_.tensor_reduce(stat[:, 10, g4], l_, AX, ALU.add))
                link(V_.tensor_reduce(stat[:, 9, g4], gate[:, g4, :], AX, ALU.add))
                link(V_.scalar_tensor_tensor(stat[:, 9, g4], stat[:, 10, g4], 1e-9, stat[:, 9, g4], ALU.mult, ALU.add))
                link(V_.reciprocal(stat[:, 10, g4], stat[:, 9, g4]))
                V_.tensor_tensor(gate[:, g4, :], gate[:, g4, :], b8(stat[:, 10, g4]), ALU.mult) \
                    .then_inc(S["gate_ready"], 1)
                dve.wait_ge(S["gate_ready"], p + 1)

            row_max(0)
            ln2_a(3)
            ln2_b(3)
            max_out(0)
            for b in range(B + 1):
                if b + 1 < B:
                    row_max(b + 1)
                if b == 0:
                    rotary(2)
                if b == 1:
                    ln2_d(3)
                if b == 3:
                    exact_parts(3)
                if b in (4, 6, 8):
                    rms_rows((b - 4) // 2)
                if b in (7, 8):
                    router_in(b - 7)
                if b + 1 < B:
                    max_out(b + 1)
                if b == 0:
                    ln2_c(3)
                    exact_parts(2)
                if b >= 1:
                    share(2 * b - 2)
                if b == 2:
                    rotary(3)
                if b in (3, 5, 7):
                    rms_square((b - 3) // 2)
                if b >= 1:
                    share(2 * b - 1)
                if b in (7, 8):
                    gates(b - 7)

            def mix(g):
                dve.wait_ge(S["w2_ps"], g + 1)
                if g >= 2:
                    dve.wait_ge(S["fin_ready"], g - 1)
                V_.tensor_tensor(moe[:, g % 2, :, :], bank[4 + g % 2][:, :].rearrange("p (e c) -> p e c", e=NE),
                                 gate[:, g, :].unsqueeze(2).to_broadcast([P, NE, C]), ALU.mult) \
                    .then_inc(S["mix_ready"], 1)

            for n_ in range(PAIRS + 1):
                for j in range(CH):
                    u = CH * n_ + j
                    if n_ < PAIRS:
                        dve.wait_ge(S["sil_ready"], u + 1)
                        dve.wait_ge(S["b_ps"], u + 1)
                        if n_ >= 2:
                            dve.wait_ge(S["w2_ps"], 4 * (n_ - 1))
                        V_.scalar_tensor_tensor(hh[:, n_ % 2, j, :], bank[2 + u % 2][:, :], 1.0 / FFN_SCALE,
                                                sil[:, u % 2, :], ALU.mult, ALU.mult).then_inc(S["hh_ready"], 1)
                    if n_ == 0 and j == 1:
                        rms_square(PAIRS - 1)
                    if n_ == 0 and j == 4:
                        rms_rows(PAIRS - 1)
                    if n_ == 0 and j == 7:
                        router_in(2)
                    if n_ == 1 and j == 1:
                        router_in(3)
                    if n_ == 1 and j in (4, 7):
                        gates(2 + (j - 4) // 3)
                    if n_ and j % 3 == 2:
                        mix(4 * (n_ - 1) + j // 3)

        @block.tensor
        def _(pe):
            def mm(out_, l_, r_, a, z, skip=False):
                return nc.tensor.matmul(out_, l_, r_, start=a, stop=z, skip_group_check=skip)

            pe.wait_ge(S["embc_ready"], 1)
            mm(bank[4][:, 0:64], embc[:, :, :].rearrange("p a b -> p (a b)"), embp[:, V:2 * V], True, True)
            mm(bank[4][:, 64:65], inw2[:, :, :].rearrange("p a b -> p (a b)"), startc[:, :], True, True) \
                .then_inc(S["table_ps"], 1)
            pe.wait_ge(S["table_ready"], 1)
            for gm in range(2):
                pe.wait_ge(S["onehot_ready"], gm + 1)
                mm(bank[gm][:, :].rearrange("p (b t) -> p b t", b=2)[:, :, 1:T], table[:, :],
                   onehot[:, 2 * gm:2 * gm + 2, 1:T], True, True).then_inc(S["emb_ps"], 1)
            for l in range(LAYERS):
                d = 2 ** l
                if l == 0:
                    pe.wait_ge(S["ld_tcn0"], 64)
                    pe.wait_ge(S["wt_zero_low"], 1)
                    pe.wait_ge(S["wt_zero_high"], 1)
                if l == 1:
                    pe.wait_ge(S["ld_tcn1"], 48)
                for gm in range(2):
                    pe.wait_ge(S["x_ready"], 2 * l + gm + 1)
                    if l:
                        pe.wait_ge(S["hid_ready"], 2 * (l - 1) + gm + 1)
                    for k in range(TAPS):
                        at = PAD - (TAPS - 1 - k) * d
                        r = mm(bank[gm][:, :].rearrange("p (b t) -> p b t", b=2), Wt[:, (TAPS + 1) * l + k, :],
                               Xp[:, 2 * gm:2 * gm + 2, at:at + T], k == 0, k == TAPS - 1)
                    r.then_inc(S["conv_ps"], 1)
                for gm in range(2):
                    pe.wait_ge(S["hid_ready"], 2 * l + gm + 1)
                    if l:
                        pe.wait_ge(S["pw_gelu"], 2 * (l - 1) + gm + 1)
                    mm(bank[2 + gm][:, :], Wt[:, (TAPS + 1) * l + TAPS, :], hid1[:, gm, :], True, True) \
                        .then_inc(S["pw_ps"], 1)
            for gm in range(2):
                pe.wait_ge(S["x_ready"], 2 * LAYERS + gm + 1)
                mm(bank[gm][:, :].rearrange("p (b t) -> p b t", b=2), Wt[:, NBLK - 2, :],
                   Xp[:, 2 * gm:2 * gm + 2, PAD:PAD + T], True, True).then_inc(S["out1_ps"], 1)
            for p in range(PAIRS):
                pe.wait_ge(S["hid_ready"], 2 * LAYERS + p // 2 + 1)
                if p == 0:
                    pe.wait_ge(S["table_ready"], 1)
                for tt in range(2):
                    at = (p % 2) * T + tt * P
                    r = mm(bank[4 + p][:, P * tt:P * tt + P], hid1[:, p // 2, at:at + P], Wt[:, NBLK - 1, :],
                           True, True)
                r.then_inc(S["logits_ps"], 1)

            def prep(p):
                pe.wait_ge(S["s_ready"], p + 1)
                pe.wait_ge(S["consts"], 3)
                if p == 0:
                    pe.wait_ge(S["hid_ready"], 2 * LAYERS + 2)
                else:
                    pe.wait_ge(S["bdT_ready"], p)
                    pe.wait_ge(S["M_ready"], p)
                for a in range(4):
                    r = nc.tensor.transpose(bank[0][:, P * a:P * a + P],
                                            s2[:, p % 2, a, :, :].rearrange("p a b -> p (a b)"), identf[:, :])
                r.then_inc(S["tr32_ps"], 1)
                pe.wait_ge(S["shl_ready"], p + 1)
                for a in range(4):
                    r = nc.tensor.transpose(bank[1][:, 64 * a:64 * a + 64].bitcast(f16),
                                            shl[:, p % 2, a, :, :].rearrange("p a b -> p (a b)"), ident16[:, :])
                r.then_inc(S["tr16_ps"], 1)

            def outer_sums(p):
                pe.wait_ge(S["sTs_ready"], p + 1)
                for hf in range(2):
                    for k in range(3):
                        o = bank[1][:, 64 * (3 * hf + k):64 * (3 * hf + k) + 64]
                        parts = [(2 * hf, 64 if k == 0 else P)] + ([(2 * hf + 1, 64)] if k == 2 else [])
                        for i, (a, rows) in enumerate(parts):
                            r = mm(o, s2[0:rows, p % 2, a, :, :].rearrange("p a b -> p (a b)"),
                                   s2[0:rows, p % 2, a, 0, :], i == 0, i == len(parts) - 1)
                r.then_inc(S["M_ps"], 1)

            def queries(p):
                if p == 0:
                    pe.wait_ge(S["wts_ready"], 1)
                    pe.wait_ge(S["pw_gelu"], 2 * LAYERS)
                for a in range(4):
                    if 4 * p + a >= 2:
                        pe.wait_ge(S["q_ready"], 4 * p + a - 1)
                    rhs = sTs[:, 4 * p:4 * p + 4, :].rearrange("p a b -> p (a b)")
                    for w in range(2):
                        r = mm(bank[2 + a % 2][:, :], qwh[:, w, a, :], rhs, w == 0, w == 1)
                    r.then_inc(S["q_ps"], 1)

            def omega(g):
                p = g // 4
                pe.wait_ge(S["q_ready"], 4 * p + 4)
                pe.wait_ge(S["bdT_ready"], p + 1)
                if g == 0:
                    pe.wait_ge(S["logits_read"], 1)
                if g >= 1:
                    pe.wait_ge(S["om_ready"], g)
                for cc in range(2):
                    t0 = P * (g % 4) + 64 * cc
                    r = mm(bank[4][:, 256 * cc:256 * cc + 256].rearrange("p (a t) -> p a t", a=4),
                           bdT[:, 2 * g + cc, :], qT[:, p % 2, :, t0:t0 + 64], True, True)
                r.then_inc(S["om_ps"], 1)

            def attend(g):
                p = g // 4
                pe.wait_ge(S["om_ready"], g + 1)
                pe.wait_ge(S["bdS_ready"], p + 1)
                pe.wait_ge(S["M_ready"], p + 1)
                if g == 0:
                    pe.wait_ge(S["logits_read"], 3)
                if g >= 1:
                    pe.wait_ge(S["o_ready"], g)
                for cc in range(2):
                    k = 2 * (g % 2) + cc
                    o = bank[6][:, 256 * cc:256 * cc + 256]
                    t0 = P * (g % 4) + 64 * cc
                    r = mm(o, bdS[:, 2 * g + cc, :], om[:, g % 2, 256 * cc:256 * cc + 256], True, k == 0)
                    if k:
                        r = mm(o.rearrange("p (a t) -> p a t", a=4), bdM[:, g // 2, k - 1, :],
                               qT[:, p % 2, :, t0:t0 + 64], False, True)
                r.then_inc(S["o_ps"], 1)

            def project(g):
                pe.wait_ge(S["o_ready"], g + 1)
                if g == 0:
                    pe.wait_ge(S["logits_read"], 4)
                if g % 4 == 0 and g:
                    pe.wait_ge(S["h2_ready"], g // 4)
                for a in range(4):
                    r = mm(bank[7][:, 64 * (g % 4):64 * (g % 4) + 64], oT[:, g % 2, a, :], ew[:, a, :],
                           a == 0, a == 3)
                r.then_inc(S["e_ps"], 1)

            def rows(p):
                pe.wait_ge(S["hsplit_ready"], p + 1)
                before = (("logits_read", 2), ("v_ready", 1), ("q_ready", TILES), ("nmT_ready", 3))[p]
                pe.wait_ge(S[before[0]], before[1])
                b_ = bank[QKV_BANK[p]]
                for a in range(4):
                    r = nc.tensor.transpose(b_[:, 64 * a:64 * a + 64].bitcast(f16),
                                            shlB[:, a, :, :].rearrange("p a b -> p (a b)"), ident16[:, :])
                r.then_inc(S["trh_ps"], 1)

            def qkv(p):
                pe.wait_ge(S["hTs_ready"], p + 1)
                if p == 0:
                    pe.wait_ge(S["w1cast"], 1)
                if p == PAIRS - 1:
                    pe.wait_ge(S["nmT_ready"], 4)
                for a in range(4):
                    for w in range(2):
                        r = mm(bank[QKV_BANK[p]][:, P * a:P * a + P], hTs[:, 4 * p + a, :], qkvh[:, w, :], w == 0, w == 1)
                r.then_inc(S["qkv_ps"], 1)

            def stack(g):
                p = g // 4
                pe.wait_ge(S["split_ready"], p + 1)
                if g < 2:
                    pe.wait_ge(S[("bdT_ready", "M_ready")[g]], PAIRS)
                else:
                    pe.wait_ge(S["stk_ready"], g - 1 if g < 6 else g)
                for n_ in range(6):
                    r = nc.tensor.transpose(bank[stack_bank(g)][0:96, 64 * n_:64 * n_ + 64].bitcast(bf16),
                                            qst[:, p % 2, g % 4, n_, :, :].rearrange("p a b -> p (a b)"),
                                            identb[:, :])
                r.then_inc(S["stk_ps"], 1)

            def scores_for_max(b):
                pe.wait_ge(S["stk_ready"], 2 * b + 2)
                for u in range(3):
                    U = 3 * b + u
                    if U == 0:
                        pe.wait_ge(S["consts"], 14)
                        pe.wait_ge(S["q_ready"], TILES)
                    if U == 1:
                        pe.wait_ge(S["om_ready"], TILES)
                    if U >= 2:
                        pe.wait_ge(S["max_ready"], U - 1)
                    o = bank[3 + U % 2]
                    if u == 0:
                        mm(o[:, :], identb[:, :], mask_t[:, :, :].rearrange("p a b -> p (a b)"), True, False)
                        for n_ in range(NH):
                            r = mm(o[:, P * n_:P * n_ + P], qkT[:, 2 * b, n_, :], qkT[:, 2 * b, NH + n_ // 2, :],
                                   False, n_ == NH - 1)
                    else:
                        for i in range(2):
                            n_ = 2 * (u - 1) + i
                            mm(o[:, T * i:T * i + T].rearrange("p (a s) -> p a s", a=2),
                               qkT[:, 2 * b + 1, n_, :], qkT[:, 2 * b:2 * b + 2, NH + n_ // 2, :], True, False)
                            r = mm(o[:, T * i + P:T * i + T], identb[:, :], mask_t[:, 0, :], False, True)
                    r.then_inc(S["p1_ps"], 1)

            def max_rows(b):
                pe.wait_ge(S["nms_ready"], b + 1)
                if b:
                    pe.wait_ge(S["nmT_ready"], b)
                if b == 0:
                    pe.wait_ge(S["stk_ready"], 5)
                if b == 3:
                    pe.wait_ge(S["hTs_ready"], PAIRS)
                if b == 4:
                    pe.wait_ge(S["v_ready"], PAIRS)
                for a in range(2):
                    r = nc.tensor.transpose(bank[0][0:3 * NH, 64 * a:64 * a + 64].bitcast(bf16),
                                            nms[:, b % 2, a, :, :].rearrange("p a b -> p (a b)"), identb[:, :])
                r.then_inc(S["nmT_ps"], 1)

            def scores_shifted(b):
                pe.wait_ge(S["nmT_ready"], b + 1)
                for u in range(3):
                    U = 3 * b + u
                    if U == 0:
                        pe.wait_ge(S["v_ready"], 2)
                    if U == 1:
                        pe.wait_ge(S["o_ready"], TILES)
                    if U >= 2:
                        pe.wait_ge(S["exp2_ready"], U - 1)
                    o = bank[5 + U % 2]
                    if u < 2:
                        for i in range(2):
                            n_ = 2 * u + i
                            ov_ = o[:, T * i:T * i + T].rearrange("p (a s) -> p a s", a=2)
                            mm(ov_, qkT[:, 2 * b, NH + n_ // 2, :], qkT[:, 2 * b:2 * b + 2, n_, :], True, False)
                            mm(ov_, selh[:, n_, :], nmT[:, b % 2, :, :], False, False)
                            r = mm(o[:, T * i:T * i + P], identb[:, :], mask_s[:, 0, :], False, True)
                    else:
                        mm(o[:, :], identb[:, :], mask_s[:, :, :].rearrange("p a b -> p (a b)"), True, False)
                        for n_ in range(NH):
                            ov_ = o[:, P * n_:P * n_ + P]
                            mm(ov_, selh[:, n_, :], nmT[:, b % 2, 1, :], False, False)
                            r = mm(ov_, qkT[:, 2 * b + 1, NH + n_ // 2, :], qkT[:, 2 * b + 1, n_, :],
                                   False, n_ == NH - 1)
                    r.then_inc(S["p2_ps"], 1)

            def values(b):
                pe.wait_ge(S["exp2_ready"], 3 * b + 3)
                pe.wait_ge(S["v_ready"], b // 2 + 1)
                if b == 0:
                    pe.wait_ge(S["h2_ready"], PAIRS)
                else:
                    pe.wait_ge(S["yT_ready"], b)
                for n_ in range(NH):
                    o = bank[7][32 * n_:32 * n_ + 32, 0:T]
                    c0 = T * (n_ % 2)
                    mm(o, vaug[:, 2 * b, n_ // 2, :], pT[:, b % 2, n_ // 2, c0:c0 + T], True, False)
                    r = mm(bank[7][32 * n_:32 * n_ + 32, P:T], vaug[:, 2 * b + 1, n_ // 2, :],
                           pT[:, b % 2, 2, P * n_:P * n_ + P], False, True)
                r.then_inc(S["y_ps"], 1)

            def out_rows(b, a):
                pe.wait_ge(S["yT_ready"], b + 1)
                g = 2 * b + a
                if g:
                    pe.wait_ge(S["ym_ready"], g)
                else:
                    pe.wait_ge(S["v_ready"], 3)
                    pe.wait_ge(S["ld_ffn"], 16 * 16)
                mm(bank[2][:, 0:NWO], yT[:, b % 2, P * a:P * a + P], wo_sb[:, :], True, True) \
                    .then_inc(S["wo_ps"], 1)

            def f_transposed(p, b_):
                pe.wait_ge(S["fsplit_ready"], p + 1)
                if p == 0:
                    pe.wait_ge(S["stk_ready"], TILES)
                elif p == 1:
                    pe.wait_ge(S["rexp_in"], 1)
                elif p == 2:
                    pe.wait_ge(S["exp2_ready"], 3 * B)
                else:
                    pe.wait_ge(S["fTs_ready"], 3)
                for a in range(4):
                    r = nc.tensor.transpose(bank[b_][:, 64 * a:64 * a + 64].bitcast(f16),
                                            shl[:, p % 2, a, :, :].rearrange("p a b -> p (a b)"), ident16[:, :])
                r.then_inc(S["trf_ps"], 1)

            def routed(p, b_):
                pe.wait_ge(S["fTs_ready"], p + 1)
                if p == 2:
                    pe.wait_ge(S["yT_ready"], B)
                if p == 3:
                    pe.wait_ge(S["rexp_in"], p)
                for a in range(4):
                    for w in range(2):
                        r = mm(bank[b_][:, NE * a:NE * a + NE], fTs[:, 4 * p + a, :], rwh[:, w, :], w == 0, w == 1)
                r.then_inc(S["rt_ps"], 1)

            prep(0)
            outer_sums(0)
            queries(0)
            omega(0)
            pe.wait_ge(S["ld_attn"], 48)
            for g in range(TILES):
                p, s = g // 4, g % 4
                if g + 1 < TILES:
                    omega(g + 1)
                attend(g)
                if g:
                    project(g - 1)
                if s == 1 and p + 1 < PAIRS:
                    prep(p + 1)
                if s == 2 and p + 1 < PAIRS:
                    outer_sums(p + 1)
                    queries(p + 1)
                if s == 0 and p >= 2:
                    rows(p - 2)
                if s == 1 and p >= 2:
                    qkv(p - 2)
                if p == PAIRS - 1:
                    stack(s)
            project(TILES - 1)
            scores_for_max(0)
            rows(2)
            stack(4)
            stack(5)
            max_rows(0)
            qkv(2)
            for b in range(B + 1):
                if b + 1 < B:
                    scores_for_max(b + 1)
                if b >= 1:
                    values(b - 1)
                if b in STACK_B:
                    stack(STACK_B[b][0])
                if b in (6, 7):
                    f_transposed(b - 6, 1)
                if b + 1 < B:
                    max_rows(b + 1)
                if b >= 1:
                    out_rows(b - 1, 0)
                if b in (6, 7):
                    routed(b - 6, 1)
                if b < B:
                    scores_shifted(b)
                if b in STACK_B:
                    stack(STACK_B[b][1])
                if b >= 1:
                    out_rows(b - 1, 1)
                if b == 1:
                    rows(3)
                if b == 2:
                    qkv(3)

            def down(g):
                n_ = g // 4
                if g % 4 == 0:
                    pe.wait_ge(S["hh_ready"], CH * (n_ + 1))
                if g == 0:
                    pe.wait_ge(S["ld_w2"], 48)
                if g >= 2:
                    pe.wait_ge(S["mix_ready"], g - 1)
                o = bank[4 + g % 2]
                c = slice(P * (g % 4), P * (g % 4) + P)
                for k in range(NE // 2):
                    mm(o[:, P * k:P * k + P], hh[:, n_ % 2, NE + k, c], w2x[:, k, :], True, False)
                    for i in range(2):
                        e = 2 * k + i
                        r = mm(o[:, C * e:C * e + C], hh[:, n_ % 2, e, c], w2s[:, e, :], False, i == 1)
                r.then_inc(S["w2_ps"], 1)

            for n_ in range(PAIRS + 1):
                for j in range(CH):
                    u = CH * n_ + j
                    if n_ < PAIRS:
                        rhs = fTs[:, 4 * n_:4 * n_ + 4, :].rearrange("p a b -> p (a b)")
                        for w_, b0, read, done in ((w1h, 0, "sil_ready", "a_ps"), (w3h, 2, "hh_ready", "b_ps")):
                            if u == 0:
                                pe.wait_ge(S[("nmT_ready", "", "ym_ready")[b0]], B if b0 == 0 else TILES)
                                pe.wait_ge(S["w1cast"], 2)
                            if u == 1:
                                pe.wait_ge(S[("rexp_in", "", "max_ready")[b0]], 2 if b0 == 0 else 3 * B)
                            if u == 0 or u == CH * n_:
                                pe.wait_ge(S["fTs_ready"], n_ + 1)
                            if u >= 2:
                                pe.wait_ge(S[read], u - 1)
                            for w in range(2):
                                r = mm(bank[b0 + u % 2][:, :], w_[:, w, j, :], rhs, w == 0, w == 1)
                            r.then_inc(S[done], 1)
                    if n_ == 0 and j == 1:
                        f_transposed(2, 6)
                    if n_ == 0 and j == 4:
                        routed(2, 7)
                    if n_ == 0 and j == 8:
                        f_transposed(3, 6)
                    if n_ == 0 and j == 11:
                        routed(3, 7)
                    if n_ and j % 3 == 1:
                        down(4 * (n_ - 1) + j // 3)


def kernel(**inputs):
    import numpy as _np
    import concourse.bacc as _bacc
    from concourse import mybir as _mybir
    from concourse.bass_utils import run_bass_kernel_spmd as _run

    a = {k: _np.asarray(v) for k, v in inputs.items()}
    t = {k[3:]: v for k, v in a.items() if k != "x"}

    def cat(*xs):
        return _np.concatenate(xs, axis=1)

    layers = _np.concatenate([t["tok_conv_w"].transpose(2, 0, 3, 1), t["tok_pw_w"].transpose(2, 0, 1)[:, :, None]],
                             axis=2)
    tcn_w = cat(layers.reshape(C, -1), t["tok_out1_w"].T, t["tok_out2_w"].T)
    tcn_b = cat(t["tok_conv_b"].T, t["tok_pw_b"].T, t["tok_out1_b"][:, None])
    emb = cat(t["tok_byte_embed"].T, t["tok_in_w"].T, t["tok_channel_embed"][0][:, None],
              t["tok_start_token"][:, None])
    inv = 1.0 / 10000.0 ** (_np.arange(0, HD, 2, dtype=_np.float32) / HD)
    ang = _np.outer(_np.arange(T, dtype=_np.float32), inv)
    ang = _np.concatenate([ang, ang], axis=-1)
    sign = _np.repeat(_np.array([-1.0, 1.0], _np.float32), HD // 2)
    scale = _np.repeat(_np.array([0.25] * NH + [1.0] * NKV, _np.float32), HD)[None] / FFN_SCALE
    cos_t = (_np.tile(_np.cos(ang), (1, NH + NKV)) * scale).astype(_np.float32)
    sin_t = (_np.tile(_np.sin(ang) * sign, (1, NH + NKV)) * scale).astype(_np.float32)
    arrs = {
        "x": a["x"], "tcn_w": tcn_w, "tcn_b": tcn_b, "out2_b": t["tok_out2_b"][None, :], "emb": emb,
        "in_b": t["tok_in_b"][None, :],
        "attn_q": t["attn_Q"].transpose(1, 0, 2).reshape(C, HEADS * C),
        "attn_e": t["attn_E"].transpose(0, 2, 1),
        "qkv_w": cat(t["ffn_wq"].T, t["ffn_wk"].T, t["ffn_wv"].T),
        "wo_t": t["ffn_wo"].T, "ln1": t["ffn_ln1_w"][:, None], "ln2": t["ffn_ln2_w"][:, None],
        "router": t["ffn_router_w"].T,
        "w1m": t["ffn_w1"][:, :MAIN].transpose(2, 0, 1), "w1r": t["ffn_w1"][:, MAIN:].transpose(2, 0, 1),
        "w3m": t["ffn_w3"][:, :MAIN].transpose(2, 0, 1), "w3r": t["ffn_w3"][:, MAIN:].transpose(2, 0, 1),
        "w2m": t["ffn_w2"][:, :, :MAIN].transpose(2, 0, 1), "w2r": t["ffn_w2"][:, :, MAIN:].transpose(2, 0, 1),
        "cos_t": cos_t, "sin_t": sin_t,
    }
    nc = _bacc.Bacc("TRN2", target_bir_lowering=False, num_devices=1)
    arrays, args = {}, []
    for name, v in arrs.items():
        v = _np.ascontiguousarray(v)
        arrays[f"in_{name}_dram"] = v
        args.append(nc.dram_tensor(f"in_{name}_dram", v.shape, _mybir.dt.from_np(v.dtype), kind="ExternalInput").ap())
    args.append(nc.dram_tensor("out_0_dram", (B, T, C), _mybir.dt.float32, kind="ExternalOutput").ap())
    tower(nc, *args)
    r = _run(nc, [arrays], core_ids=[0])
    return r.results[0]["out_0_dram"]
```

```python
import concourse.bass as bass
from concourse import mybir
from contextlib import ExitStack
import numpy as np

B, T, C, V, EMB = 8, 256, 64, 64, 32
LAYERS, TAPS, PAD = 6, 3, 64
HEADS = 8
NH, NKV, HD = 4, 2, 16
NE, HID, MAIN = 8, 170, 128
REM = HID - MAIN
PAIRS, TILES, P = 4, 16, 128
CH = NE + NE // 2
NEG = -1e30
ATT_SCALE, FFN_SCALE, HH_SCALE = 64.0, 16.0, 4.0


def tower(nc, x, tcn_w, tcn_b, out2_b, emb, in_b, attn_q, attn_e, qkv_w, wo_t, ln1, ln2, router,
          w1m, w1r, w3m, w3r, w2m, w2r, cos_t, sin_t, out):
    f32, f16, bf16, i32 = mybir.dt.float32, mybir.dt.float16, mybir.dt.bfloat16, mybir.dt.int32
    ALU = mybir.AluOpType
    ACT = mybir.ActivationFunctionType
    AX = mybir.AxisListType.X
    NBLK = 3 * LAYERS + LAYERS + 2

    ctx = ExitStack()
    with ctx:
        def sb(name, shape, dt=f32):
            return ctx.enter_context(nc.sbuf_tensor(name, shape, dt))

        def sem(name):
            return ctx.enter_context(nc.semaphore(name))

        bank = [ctx.enter_context(nc.psum_tensor(f"bank{i}", [P, 512], f32)) for i in range(8)]

        NW, NX = NBLK * P, 4 * (PAD + T)
        early = sb("early", [P, NW + NX + 2048])
        Wt = early[:, 0:NW].rearrange("p (n o) -> p n o", o=P)
        Xp = early[:, NW:NW + NX].rearrange("p (b t) -> p b t", b=4)
        hid1 = early[:, NW + NX:NW + NX + 1024].rearrange("p (a c) -> p a c", a=PAIRS)
        hid2 = early[:, NW + NX + 1024:NW + NX + 2048].rearrange("p (a c) -> p a c", a=PAIRS)
        qkT = early[0:96, 0:TILES * 6 * P // 2].bitcast(bf16).rearrange("p (g n t) -> p g n t", n=6, t=P)
        bt = sb("bt", [P, 2 * LAYERS + 1])
        b2bc = sb("b2bc", [P, V])
        idx = sb("idx", [P, 4, T], i32)
        onehot = sb("onehot", [P, 4, T])
        vcol_i = sb("vcol_i", [P, 1], i32)
        vcol = sb("vcol", [P, 1])
        embp = sb("embp", [EMB + 1, 2 * V + 2])
        embc = sb("embc", [EMB + 1, 2, V])
        inw2 = sb("inw2", [EMB + 1, 2, C])
        startc = sb("startc", [EMB + 1, 1])
        table = sb("table", [P, P])
        identf = sb("identf", [P, P])
        ident16 = sb("ident16", [P, P], f16)
        identb = sb("identb", [P, P], bf16)
        trimul = sb("trimul", [P, 64])
        mask_t = sb("mask_t", [P, 4, P], bf16)
        mask_s = sb("mask_s", [P, 4, P], bf16)
        selh = sb("selh", [3 * NH, NH, P], bf16)
        neghalf = sb("neghalf", [P, 4])
        L = sb("L", [P, TILES, V])
        h = sb("h", [P, TILES, V])
        cen = sb("cen", [P, 2, 4, V])
        sqr = sb("sqr", [P, 2, 4, V])
        ex = sb("ex", [P, 2, 4, V])
        stat = sb("stat", [P, 16, TILES])
        s2 = sb("s2", [P, 2, 4, 2, V])
        shl = sb("shl", [P, 2, 4, 4, V], f16)
        qw = sb("qw", [P, 4, P])
        qwh = sb("qwh", [P, 2, 4, P], f16)
        ew = sb("ew", [P, 4, C])
        sTs = sb("sTs", [P, TILES, P], f16)
        shared = sb("shared", [P, 12288])
        bdT = shared[:, 0:4096].rearrange("p (n u) -> p n u", u=P)
        bdS = shared[:, 4096:8192].rearrange("p (n u) -> p n u", u=P)
        bdM = shared[:, 8192:11264].rearrange("p (b k u) -> p b k u", k=3, u=P)
        om = shared[:, 11264:12288].rearrange("p (a c) -> p a c", a=2)
        RING = 6
        hh = shared[:, 0:RING * 512].rearrange("p (j c) -> p j c", j=RING)
        hhx = shared[:, RING * 512:RING * 512 + 3 * 3 * 512].bitcast(f16) \
            .rearrange("p (a w j c) -> p a w j c", a=3, w=2, j=3)
        qT = sb("qT", [P, 2, 4, 512])
        oT = sb("oT", [P, 2, 4, P])
        oTx = sb("oTx", [P, 2, 2, 4, P], f16)
        ewx = sb("ewx", [P, 2, 4, C], f16)
        xf = sb("xf", [P, TILES, C])
        hx = sb("hx", [P, TILES, C])
        qkvw = sb("qkvw", [P, P])
        qkvh = sb("qkvh", [P, 2, P], f16)
        lns = sb("lns", [P, 2])
        NWO = NH * C + NH
        wo_sb = sb("wo_sb", [P, NWO])
        cos4 = sb("cos4", [P, 4, 96])
        sin4 = sb("sin4", [P, 4, 96])
        hTs = sb("hTs", [P, TILES, P], f16)
        rope = sb("rope", [P, 4, 96])
        rot = sb("rot", [P, 4, 96])
        qst = sb("qst", [P, 2, 4, 6, 6, HD], bf16)
        vaug = sb("vaug", [P, TILES, NKV, 32])
        nmx = sb("nmx", [P, TILES, NH])
        nmr = sb("nmr", [P, 2, 2, NH])
        nms = sb("nms", [P, 2, 2, NH, 3], bf16)
        nmT = sb("nmT", [3 * NH, 2, 2, P], bf16)
        pT = qT[:, :, 0:3, :]
        rec = sb("rec", [P, TILES, NH])
        yT = sb("yT", [P, 2, T])
        ym = oT[:, :, :, :].rearrange("p a b c -> p (a b c)").rearrange("p (u a n c) -> p u a n c", u=2, a=2, n=NH)
        cenB = qw[:, 0:2, :].rearrange("p a (b v) -> p (a b) v", v=V)
        sqrB = sb("sqrB", [P, 4, V])
        hrB = qw[:, 2:4, :].rearrange("p a (b v) -> p (a b) v", v=V)
        shlB = sb("shlB", [P, 4, 2, V], f16)
        rw = sb("rw", [P, NE])
        rwh = sb("rwh", [P, 2, NE], f16)
        w1s = sb("w1s", [P, CH, P])
        w1h = sb("w1h", [P, 2, CH, P], f16)
        w3h = sb("w3h", [P, 2, CH, P], f16)
        w2h = sb("w2h", [P, 2, NE, C], f16)
        w2xh = sb("w2xh", [P, 2, NE // 2, P], f16)
        w2in = hTs[:, :, :].rearrange("p a b -> p (a b)").bitcast(f32)
        w2s = w2in[:, 0:NE * C].rearrange("p (e c) -> p e c", c=C)
        w2x = w2in[:, NE * C:2 * NE * C].rearrange("p (k c) -> p k c", c=P)
        x2 = idx[:, :, :].rearrange("p a b -> p (a b)").bitcast(f32).rearrange("p (g c) -> p g c", c=C)
        fTs = onehot[:, :, :].rearrange("p a b -> p (a b)").bitcast(f16).rearrange("p (g c) -> p g c", c=P)
        lg = sb("lg", [P, 4, 4, NE])
        ge = sqr[:, 0, :, :].rearrange("p a (i j) -> p a i j", j=NE)
        gt = sqr[:, 1, :, :].rearrange("p a (i j) -> p a i j", j=NE)
        lowidx = sb("lowidx", [P, NE, NE])
        gate = sb("gate", [P, TILES, NE])
        sil = qT[:, :, 3, :]
        moe = qst[:, :, :, :, :, :].rearrange("p a b c d e -> p (a b c d e)")[:, 0:4 * 2 * NE * C].bitcast(f32) \
            .rearrange("p (a e c) -> p a e c", a=4, e=NE)
        fin = L

        names = ["ld_tok", "ld_emb", "ld_tcn0", "ld_tcn1", "ld_attn", "ld_ffn", "ld_w1", "ld_w3", "ld_w2", "stored",
                 "gchain", "consts", "memz", "bd_zero", "vchain", "embc_ready", "table_ps", "table_ready",
                 "onehot_ready", "emb_ps", "x_ready", "conv_ps", "hid_ready", "out_gelu", "pw_ps", "pw_gelu",
                 "out1_ps", "logits_ps", "logits_read", "lsub_ready", "exp_ready", "lsum_ready", "ln_ready",
                 "var_ready", "rstd_ready", "s_ready", "shl0_ready", "shl_ready", "h_ready", "tr32_ps", "tr16_ps",
                 "sTs_ready", "twice_ready", "bdT_ready", "bdS_ready", "M_ps", "M_ready", "q_ps", "q_ready", "om_ps",
                 "om_ready", "o_ps", "o_ready", "o_high", "o_low", "e_ps", "h2_ready", "var2_ready", "rstd2_ready",
                 "q1_ready", "rinv_ready", "hr_ready", "hsplit_ready", "hsplit3_ready", "trh_ps", "hTs_ready",
                 "qkv_ps", "rope_ready", "parts2_ready", "v_ready", "split_ready", "stk_ps", "stk_ready", "p1_ps",
                 "max_ready", "nms_ready", "nmT_ps", "nmT_ready", "p2_ps", "exp2_ready", "y_ps", "yT_ready", "wo_ps",
                 "x2_ready", "ym_ready", "ss_ready", "r2_ready", "fs_ready", "fsplit_ready", "trf_ps", "fTs_ready",
                 "rt_ps", "rexp_in", "rexp_ready", "gate_ready", "a_ps", "b_ps", "sil_ready", "hh_ready", "w2_ps",
                 "mix_ready", "fin_ready", "wts_ready", "w1cast", "w2_scaled", "w2_cast", "hx_ready", "hi_ready",
                 "lo_ready", "wt_zero_low", "wt_zero_high"]
        S = {n: sem(n) for n in names}

        QKV_BANK = (5, 5, 2, 0)

        STACK_B = {(0, 0): 6, (0, 1): 7, (2, 1): 8, (2, 2): 9, (3, 0): 10, (3, 1): 11, (4, 1): 12, (4, 2): 13,
                   (5, 0): 14, (5, 1): 15}

        RMS_SQUARE, RMS_ROWS = {4: 0, 5: 1, 7: 2}, {5: 0, 6: 1, 8: 2}

        GATE_STEPS = ((7, 9, 11), (13, 15, 24), (36, 37, 38), (39, 41, 47))

        def stack_bank(g):
            return g % 2 if g < 6 else 1

        block = ctx.enter_context(nc.Block())

        def xrows(half):
            return x[4 * half:4 * half + 4, 0:T - 1]

        @block.sync
        def _(sp):
            sp.dma_start(embp[0:EMB, :], emb[:, :]).then_inc(S["ld_emb"], 16)
            sp.dma_start(embp[EMB:EMB + 1, V:2 * V], in_b[:, :]).then_inc(S["ld_emb"], 16)
            for half in range(2):
                sp.dma_start(idx[64 * half:64 * half + 64, :, 1:T],
                             xrows(half).unsqueeze(0).to_broadcast([64, 4, T - 1])).then_inc(S["ld_tok"], 16)
            tw = tcn_w.rearrange("c (n o) -> c n o", o=C)
            for lo, hi, s in ((0, TAPS + 1, "ld_tcn0"), (TAPS + 1, NBLK, "ld_tcn1")):
                for half in range(2):
                    q = slice(64 * half, 64 * half + 64)
                    sp.dma_start(Wt[q, lo:hi, q], tw[:, lo:hi, :]).then_inc(S[s], 16)
                if lo == 0:
                    for half in range(2):
                        sp.dma_start(bt[64 * half:64 * half + 64, :], tcn_b[:, :]).then_inc(S[s], 16)
            sp.dma_start(b2bc[:, :], out2_b[:, :].to_broadcast([P, V])).then_inc(S["ld_tcn1"], 16)
            for half in range(2):
                q = slice(64 * half, 64 * half + 64)
                sp.dma_start(qw[q, :, :], attn_q.rearrange("c (a m) -> c a m", m=P)).then_inc(S["ld_attn"], 16)
            sp.dma_start(ew[:, :, :], attn_e.rearrange("(a two) j i -> (two j) a i", two=2)).then_inc(S["ld_attn"], 16)
            for half in range(2):
                q = slice(64 * half, 64 * half + 64)
                sp.dma_start(qkvw[q, :], qkv_w[:, :]).then_inc(S["ld_ffn"], 16)
                sp.dma_start(lns[q, 0:1], ln1[:, :]).then_inc(S["ld_ffn"], 16)
                sp.dma_start(lns[q, 1:2], ln2[:, :]).then_inc(S["ld_ffn"], 16)
                sp.dma_start(rw[q, :], router[:, :]).then_inc(S["ld_ffn"], 16)
                tt = cos_t.rearrange("(a p) c -> p a c", a=2)
                sp.dma_start(cos4[:, 2 * half:2 * half + 2, :], tt).then_inc(S["ld_ffn"], 16)
                tt = sin_t.rearrange("(a p) c -> p a c", a=2)
                sp.dma_start(sin4[:, 2 * half:2 * half + 2, :], tt).then_inc(S["ld_ffn"], 16)
            sp.wait_ge(S["bd_zero"], 2)
            for n_ in range(NH):
                sp.dma_start(wo_sb[32 * n_:32 * n_ + HD, C * n_:C * n_ + C],
                             wo_t[HD * n_:HD * n_ + HD, :]).then_inc(S["ld_ffn"], 16)
            sp.dma_start(w2s[:, :, :], w2m[:, :, :]).then_inc(S["ld_w2"], 16)
            w2v = w2r.rearrange("r (k two) c -> r k two c", two=2)
            for half in range(2):
                sp.dma_start(w2x[64 * half:64 * half + REM, :, 64 * half:64 * half + 64],
                             w2v[:, :, half, :]).then_inc(S["ld_w2"], 16)
            for n, (wm, wr, s) in enumerate(((w1m, w1r, "ld_w1"), (w3m, w3r, "ld_w3"))):
                if n:
                    sp.wait_ge(S["w1cast"], 1)
                for half in range(2):
                    q = slice(64 * half, 64 * half + 64)
                    sp.dma_start(w1s[q, 0:NE, :], wm[:, :, :]).then_inc(S[s], 16)
                    sp.dma_start(w1s[q, NE:CH, :].rearrange("c k (two r) -> c (k two) r", two=2)[:, :, 0:REM],
                                 wr[:, :, :]).then_inc(S[s], 16)
            ov = out.rearrange("(hf p) (tt q) c -> q p hf tt c", hf=2, tt=2)
            for g in range(TILES):
                p_, hf, tt = g // 4, (g // 2) % 2, g % 2
                sp.wait_ge(S["fin_ready"], g + 1)
                sp.dma_start(ov[:, p_, hf, tt, :], fin[:, g, :]).then_inc(S["stored"], 16)
            sp.wait_ge(S["stored"], 16 * TILES)

        @block.gpsimd
        def _(pool):
            n = [0]

            def link(ins):
                n[0] += 1
                ins.then_inc(S["gchain"], 1)
                pool.wait_ge(S["gchain"], n[0])

            made = [0]

            def const(ins):
                made[0] += 1
                ins.then_inc(S["consts"], 1)
                pool.wait_ge(S["consts"], made[0])

            nc.gpsimd.iota(vcol_i[0:64, :], [[0, 1]], base=0, channel_multiplier=1).then_inc(S["bd_zero"], 1)
            link(nc.gpsimd.iota(vcol_i[64:P, :], [[0, 1]], base=0, channel_multiplier=1))
            pool.wait_ge(S["bd_zero"], 1)
            const(nc.gpsimd.tensor_copy(vcol[:, :], vcol_i[:, :]))
            nc.gpsimd.memset(Wt[64:P, :, 0:64], 0.0).then_inc(S["wt_zero_low"], 1)
            pool.wait_ge(S["wt_zero_low"], 1)
            nc.gpsimd.memset(w2x[:, :, :], 0.0).then_inc(S["memz"], 1)
            nc.gpsimd.memset(w1s[:, NE:CH, :], 0.0).then_inc(S["memz"], 1)
            pool.wait_ge(S["memz"], 2)
            link(nc.gpsimd.memset(wo_sb[:, :], 0.0))
            nc.gpsimd.affine_select(out=wo_sb[:, NH * C:NWO], in_=wo_sb[:, NH * C:NWO],
                                    compare_op=ALU.not_equal, fill=1.0, base=-HD, pattern=[[-32, NH]],
                                    channel_multiplier=1).then_inc(S["bd_zero"], 1)
            pool.wait_ge(S["bd_zero"], 2)
            link(nc.gpsimd.memset(identf[:, :], 0.0))
            link(nc.gpsimd.affine_select(out=identf[:, :], in_=identf[:, :], compare_op=ALU.not_equal, fill=1.0,
                                         base=0, pattern=[[-1, P]], channel_multiplier=1))
            const(nc.gpsimd.tensor_copy(ident16[:, :], identf[:, :]))
            const(nc.gpsimd.tensor_copy(identb[:, :], identf[:, :]))
            link(nc.gpsimd.memset(trimul[:, :], 1.0))
            for half in range(2):
                q = slice(64 * half, 64 * half + 64)
                const(nc.gpsimd.affine_select(out=trimul[q, :], in_=trimul[q, :], compare_op=ALU.is_ge, fill=0.0,
                                              base=0,
                                        pattern=[[1, 64]], channel_multiplier=-1))
            const(nc.gpsimd.memset(neghalf[:, :], -0.5))
            const(nc.gpsimd.memset(bdT[:, :, :], 0.0))
            const(nc.gpsimd.memset(bdS[:, :, :], 0.0))
            const(nc.gpsimd.memset(bdM[:, :, :, :], 0.0))
            for m in (mask_t, mask_s):
                link(nc.gpsimd.memset(m[:, :, :], 0.0))
            for m, sgn in ((mask_t, -1), (mask_s, 1)):
                const(nc.gpsimd.affine_select(out=m[:, :, :], in_=m[:, :, :], compare_op=ALU.is_ge, fill=NEG, base=0,
                                              pattern=[[0, NH], [sgn, P]], channel_multiplier=-sgn))
            link(nc.gpsimd.memset(selh[:, :, :], 1.0))
            link(nc.gpsimd.affine_select(out=selh[:, :, :], in_=selh[:, :, :], compare_op=ALU.is_ge, fill=0.0, base=0,
                                         pattern=[[-3, NH], [0, P]], channel_multiplier=1))
            const(nc.gpsimd.affine_select(out=selh[:, :, :], in_=selh[:, :, :], compare_op=ALU.is_ge, fill=0.0, base=2,
                                    pattern=[[3, NH], [0, P]], channel_multiplier=-1))
            const(nc.gpsimd.memset(vaug[:, :, :, :], 1.0))
            link(nc.gpsimd.memset(lowidx[:, :, :], 1.0))
            const(nc.gpsimd.affine_select(out=lowidx[:, :, :], in_=lowidx[:, :, :], compare_op=ALU.is_gt, fill=0.0,
                                    base=0, pattern=[[1, NE], [-1, NE]], channel_multiplier=0))

            def split(dst, src, ready):
                link(nc.gpsimd.tensor_copy(dst[:, :, 0, :], src))
                nc.gpsimd.tensor_tensor(dst[:, :, 1, :], src, dst[:, :, 0, :], ALU.subtract).then_inc(S[ready], 1)

            def inverse_root(dst, src, p, before, ready):
                g4 = slice(4 * p, 4 * p + 4)
                pool.wait_ge(S[before], p + 1)
                nc.gpsimd.tensor_tensor(stat[:, dst, g4], stat[:, src, g4], neghalf[:, 0:4], ALU.pow) \
                    .then_inc(S[ready], 1)

            def variance_root(p):
                inverse_root(4, 3, p, "var_ready", "rstd_ready")

            def first_split(p):
                pool.wait_ge(S["s_ready"], p + 1)
                if p >= 2:
                    pool.wait_ge(S["M_ps"], p - 1)
                split(shl[:, p % 2, :, 1:3, :], s2[:, p % 2, :, 0, :], "shl_ready")

            def first_h(p):
                g4 = slice(4 * p, 4 * p + 4)
                pool.wait_ge(S["ln_ready"], 1)
                nc.gpsimd.tensor_tensor(h[:, g4, :], L[:, g4, :], stat[:, 1, g4].unsqueeze(2)
                                        .to_broadcast([P, 4, V]), ALU.subtract).then_inc(S["h_ready"], 1)

            def variance2_root(p):
                inverse_root(12, 11, p, "var2_ready", "rstd2_ready")

            def square2_root(p):
                inverse_root(6, 5, p, "q1_ready", "rinv_ready")

            def second_split(p):
                pool.wait_ge(S["hr_ready"], p + 1)
                if p:
                    pool.wait_ge(S["trh_ps"], p)
                split(shlB[:, :, :, :], hrB[:, :, :], "hsplit_ready")

            def third_root(p):
                inverse_root(8, 7, p, "ss_ready", "r2_ready")

            def third_split(p):
                pool.wait_ge(S["fs_ready"], p + 1)
                if p >= 2:
                    pool.wait_ge(S["trf_ps"], p - 1)
                split(shl[:, p % 2, :, 1:3, :], s2[:, p % 2, :, 0, :], "fsplit_ready")

            def head_sum(b):
                pool.wait_ge(S["ym_ready"], 2 * b + 2)
                m = ym[:, b % 2, :, :, :]
                link(nc.gpsimd.tensor_tensor(m[:, :, 0:2, :], m[:, :, 0:2, :], m[:, :, 2:4, :], ALU.add))
                link(nc.gpsimd.tensor_tensor(m[:, :, 0, :], m[:, :, 0, :], m[:, :, 1, :], ALU.add))
                nc.gpsimd.tensor_tensor(x2[:, 2 * b:2 * b + 2, :], m[:, :, 0, :], xf[:, 2 * b:2 * b + 2, :],
                                        ALU.add).then_inc(S["x2_ready"], 1)
                pool.wait_ge(S["x2_ready"], b + 1)

            def both_rows(p):
                g4 = slice(4 * p, 4 * p + 4)
                nc.gpsimd.tensor_tensor(hx[:, g4, :], h[:, g4, :], x2[:, g4, :], ALU.add).then_inc(S["hx_ready"], 1)
                pool.wait_ge(S["hx_ready"], p + 1)

            def low_part(u):
                v, i = u // 3, u % 3
                pool.wait_ge(S["hi_ready"], u + 1)
                if v >= 3:
                    pool.wait_ge(S["w2_ps"], 4 * (v - 2))
                nc.gpsimd.tensor_tensor(hhx[:, v % 3, 1, i, :], hh[:, u % RING, :], hhx[:, v % 3, 0, i, :],
                                        ALU.subtract).then_inc(S["lo_ready"], 1)
                pool.wait_ge(S["lo_ready"], u + 1)

            pool.wait_ge(S["w2_scaled"], 2)
            for i, (dst, src) in enumerate(((w2h, w2s), (w2xh, w2x))):
                link(nc.gpsimd.tensor_copy(dst[:, 0, :, :], src))
                nc.gpsimd.tensor_tensor(dst[:, 1, :, :], src, dst[:, 0, :, :], ALU.subtract).then_inc(S["w2_cast"], 1)
                pool.wait_ge(S["w2_cast"], i + 1)
            variance_root(0)
            variance_root(1)

            def pair_parts(p):
                pool.wait_ge(S["rope_ready"], 1)
                pool.wait_ge(S["stk_ps"], 4 * (p - 1))
                r6 = rope[:, :, :].rearrange("p a (n e) -> p a n e", e=HD)
                t6 = rot[:, :, :].rearrange("p a (n e) -> p a n e", e=HD)
                d_ = qst[:, p % 2, :, :, :, :]
                q_, k_ = slice(0, 4), slice(4, 6)
                link(nc.gpsimd.tensor_copy(d_[:, :, :, 0, :], r6))
                link(nc.gpsimd.tensor_tensor(t6, r6, d_[:, :, :, 0, :], ALU.subtract))
                link(nc.gpsimd.tensor_copy(d_[:, :, q_, 3, :], t6[:, :, q_, :]))
                link(nc.gpsimd.tensor_copy(d_[:, :, k_, 1, :], t6[:, :, k_, :]))
                link(nc.gpsimd.tensor_tensor(d_[:, :, q_, 5, :], t6[:, :, q_, :], d_[:, :, q_, 3, :], ALU.subtract))
                link(nc.gpsimd.tensor_tensor(d_[:, :, k_, 2, :], t6[:, :, k_, :], d_[:, :, k_, 1, :], ALU.subtract))
                for i, (heads, dst, src) in enumerate(((q_, 1, 0), (q_, 2, 0), (q_, 4, 3), (k_, 3, 0), (k_, 5, 0),
                                                       (k_, 4, 1))):
                    nc.gpsimd.tensor_copy(d_[:, :, heads, dst, :], d_[:, :, heads, src, :]) \
                        .then_inc(S["parts2_ready"], 1)
                    pool.wait_ge(S["parts2_ready"], i + 1)

            def low_rows(g):
                pool.wait_ge(S["o_high"], g + 1)
                nc.gpsimd.tensor_tensor(oTx[:, g % 2, 1, :, :], oT[:, g % 2, :, :], oTx[:, g % 2, 0, :, :],
                                        ALU.subtract).then_inc(S["o_low"], 1)
                pool.wait_ge(S["o_low"], g + 1)

            for g in range(TILES):
                p, s = g // 4, g % 4
                if g:
                    low_rows(g - 1)
                if s == 0 and p + 1 < PAIRS:
                    first_split(p + 1)
                if g == 4:
                    first_h(0)
                if s == 1 and p:
                    first_h(p)
                    if p:
                        variance2_root(p - 1)
                if s == 2 and p:
                    square2_root(p - 1)
                if s == 3:
                    if p:
                        second_split(p - 1)
                    if p + 2 < PAIRS:
                        variance_root(p + 2)
            low_rows(TILES - 1)
            pair_parts(2)
            for b in range(1, B + 1):
                if b == 1:
                    variance2_root(3)
                    square2_root(3)
                if b in RMS_ROWS:
                    third_split(RMS_ROWS[b])
                if b in RMS_SQUARE:
                    third_root(RMS_SQUARE[b])
                head_sum(b - 1)
                if b % 2 == 0:
                    both_rows(b // 2 - 1)
            for u in range(PAIRS * CH):
                low_part(u)
                if u == 2:
                    third_root(PAIRS - 1)
                if u == 6:
                    third_split(PAIRS - 1)

        @block.scalar
        def _(act):
            def conv_gelu(l, p):
                act.wait_ge(S["conv_ps"], PAIRS * l + p + 1)
                if l:
                    act.wait_ge(S["pw_ps"], PAIRS * (l - 1) + p + 1)
                nc.scalar.activation(hid1[:, p, :], bank[p][:, 0:T], ACT.Gelu,
                                     bias=bt[:, l:l + 1]).then_inc(S["hid_ready"], 1)

            def pw_gelu(l, p):
                act.wait_ge(S["pw_ps"], PAIRS * l + p + 1)
                if l:
                    act.wait_ge(S["x_ready"], PAIRS * l + p + 1)
                nc.scalar.activation(hid2[:, p, :], bank[4 + p][:, 0:T], ACT.Gelu,
                                     bias=bt[:, LAYERS + l:LAYERS + l + 1]).then_inc(S["pw_gelu"], 1)

            def out_gelu(p):
                act.wait_ge(S["out1_ps"], p + 1)
                nc.scalar.activation(hid1[:, p, :], bank[p][:, 0:T], ACT.Gelu,
                                     bias=bt[:, 2 * LAYERS:2 * LAYERS + 1]).then_inc(S["out_gelu"], 1)

            act.wait_ge(S["ld_tcn0"], 64)
            for l in range(LAYERS - 1):
                for p in range(PAIRS):
                    conv_gelu(l, p)
                for p in range(PAIRS):
                    pw_gelu(l, p)
            l = LAYERS - 1
            conv_gelu(l, 0)
            conv_gelu(l, 1)
            pw_gelu(l, 0)
            pw_gelu(l, 1)
            conv_gelu(l, 2)
            out_gelu(0)
            pw_gelu(l, 2)
            conv_gelu(l, 3)
            out_gelu(1)
            out_gelu(2)
            pw_gelu(l, 3)
            out_gelu(3)

            def exponentials(p):
                act.wait_ge(S["lsub_ready"], p + 1)
                if p >= 2:
                    act.wait_ge(S["lsum_ready"], p - 1)
                nc.scalar.activation(ex[:, p % 2, :, :], L[:, 4 * p:4 * p + 4, :], ACT.Exp) \
                    .then_inc(S["exp_ready"], 1)

            def chunk_rows(p):
                act.wait_ge(S["s_ready"], p + 1)
                act.wait_ge(S["consts"], 9)
                for src in range(2):
                    for dst in range(2):
                        sq = slice(64 * src, 64 * src + 64)
                        dq = slice(64 * dst, 64 * dst + 64)
                        o = bdS[dq, 8 * p:8 * p + 8, dq].rearrange("p (a cc) i -> p a cc i", cc=2)[:, :, src, :]
                        r = nc.scalar.copy(o, s2[sq, p % 2, :, dst, :])
                r.then_inc(S["bdS_ready"], 1)

            def rows_twice(p):
                act.wait_ge(S["shl_ready" if p else "shl0_ready"], max(p, 1))
                nc.scalar.copy(shl[:, p % 2, :, 0:4:3, :], shl[:, p % 2, :, 1:3, :]) \
                    .then_inc(S["twice_ready"], 1)

            def turned_rows(p):
                act.wait_ge(S["tr32_ps"], p + 1)
                for hf in range(2):
                    q = slice(64 * hf, 64 * hf + 64)
                    r = nc.scalar.copy(bdT[q, 8 * p:8 * p + 8, q], bank[0][q, :].rearrange("p (a u) -> p a u", u=64))
                r.then_inc(S["bdT_ready"], 1)
                act.wait_ge(S["tr16_ps"], p + 1)
                nc.scalar.copy(sTs[:, 4 * p:4 * p + 4, :].rearrange("p a b -> p (a b)"),
                               bank[1][:, 0:256].bitcast(f16)).then_inc(S["sTs_ready"], 1)

            def outer_out(p):
                act.wait_ge(S["M_ps"], p + 1)
                for hf in range(2):
                    q = slice(64 * hf, 64 * hf + 64)
                    r = nc.scalar.copy(bdM[q, 2 * p:2 * p + 2, :, q],
                                       bank[1][q, 0:384].rearrange("p (b k j) -> p b k j", b=2, k=3))
                r.then_inc(S["M_ready"], 1)

            def q_out(p, a):
                act.wait_ge(S["q_ps"], 4 * p + a + 1)
                if p >= 2:
                    act.wait_ge(S["o_ps"], 4 * (p - 1))
                nc.scalar.mul(qT[:, p % 2, a, :], bank[2 + a % 2][:, :], 1.0 / ATT_SCALE).then_inc(S["q_ready"], 1)

            def o_out(g):
                act.wait_ge(S["o_ps"], g + 1)
                if g >= 2:
                    act.wait_ge(S["o_low"], g - 1)
                nc.scalar.mul(oT[:, g % 2, :, :].rearrange("p a (cc t) -> p cc a t", cc=2),
                              bank[6][:, :].rearrange("p (cc a t) -> p cc a t", cc=2, a=4), 1.0 / ATT_SCALE) \
                    .then_inc(S["o_ready"], 1)
                act.wait_ge(S["o_ready"], g + 1)
                if g >= 2:
                    act.wait_ge(S["e_ps"], g - 1)
                nc.scalar.copy(oTx[:, g % 2, 0, :, :], oT[:, g % 2, :, :]).then_inc(S["o_high"], 1)

            def h_rows(p):
                act.wait_ge(S["trh_ps"], p + 1)
                nc.scalar.copy(hTs[:, 4 * p:4 * p + 4, :].rearrange("p a b -> p (a b)"),
                               bank[QKV_BANK[p]][:, 0:256].bitcast(f16)).then_inc(S["hTs_ready"], 1)

            def stacked(g):
                act.wait_ge(S["stk_ps"], g + 1)
                nc.scalar.copy(qkT[:, g, :, :].rearrange("p a b -> p (a b)"),
                               bank[stack_bank(g)][0:96, 0:384].bitcast(bf16)).then_inc(S["stk_ready"], 1)

            chunk_rows(0)
            turned_rows(0)
            rows_twice(0)
            q_out(0, 0)
            q_out(0, 1)
            q_out(0, 2)
            q_out(0, 3)
            outer_out(0)
            exponentials(0)
            exponentials(1)
            for g in range(TILES):
                p, s = g // 4, g % 4
                if s == 3 and p + 1 < PAIRS:
                    q_out(p + 1, 3)
                o_out(g)
                if g == 2:
                    exponentials(2)
                    exponentials(3)
                if g == 3:
                    act.wait_ge(S["lsum_ready"], PAIRS)
                    nc.scalar.activation(stat[:, 1, :], stat[:, 0, :], ACT.Ln).then_inc(S["ln_ready"], 1)
                if s == 0 and p + 1 < PAIRS:
                    chunk_rows(p + 1)
                if s == 0 and p >= 2:
                    h_rows(p - 2)
                if s == 1 and p + 1 < PAIRS:
                    rows_twice(p + 1)
                    turned_rows(p + 1)
                if s == 2 and p + 1 < PAIRS:
                    q_out(p + 1, 0)
                    q_out(p + 1, 1)
                    outer_out(p + 1)
                    q_out(p + 1, 2)
                if p == PAIRS - 1:
                    stacked(s)

            def probs(b, u):
                act.wait_ge(S["p2_ps"], 3 * b + u + 1)
                if b >= 2:
                    act.wait_ge(S["y_ps"], b - 1)
                nc.scalar.activation(pT[:, b % 2, u, :], bank[5 + (3 * b + u) % 2][:, :],
                                     ACT.Exp).then_inc(S["exp2_ready"], 1)

            def y_rows(b):
                act.wait_ge(S["y_ps"], b + 1)
                if b >= 2:
                    act.wait_ge(S["wo_ps"], 2 * b - 2)
                nc.scalar.copy(yT[:, b % 2, :], bank[7][:, 0:T]).then_inc(S["yT_ready"], 1)

            def f_rows(p, b_):
                act.wait_ge(S["trf_ps"], p + 1)
                nc.scalar.copy(fTs[:, 4 * p:4 * p + 4, :].rearrange("p a b -> p (a b)"),
                               bank[b_][:, 0:256].bitcast(f16)).then_inc(S["fTs_ready"], 1)

            def router_exp(p):
                act.wait_ge(S["rexp_in"], p + 1)
                nc.scalar.activation(lg[:, p, :, :], lg[:, p, :, :], ACT.Exp).then_inc(S["rexp_ready"], 1)

            h_rows(2)
            stacked(4)
            stacked(5)
            for b in range(B + 1):
                if b >= 1:
                    y_rows(b - 1)
                if b == 3:
                    h_rows(3)
                if (b, 0) in STACK_B:
                    stacked(STACK_B[b, 0])
                if b in (6, 7):
                    f_rows(b - 6, 1)
                if b in (7, 8):
                    router_exp(b - 7)
                for u in range(3):
                    if u == 2 and (b, 1) in STACK_B:
                        stacked(STACK_B[b, 1])
                    if b < B:
                        probs(b, u)
                if (b, 2) in STACK_B:
                    stacked(STACK_B[b, 2])
            def high_part(u):
                v, i = u // 3, u % 3
                act.wait_ge(S["hh_ready"], u + 1)
                if v >= 3:
                    act.wait_ge(S["w2_ps"], 4 * (v - 2))
                nc.scalar.copy(hhx[:, v % 3, 0, i, :], hh[:, u % RING, :]).then_inc(S["hi_ready"], 1)

            for n in range(PAIRS):
                for k in range(NE // 2):
                    for i in range(3):
                        u = CH * n + 3 * k + i
                        if (n, k, i) == (0, 1, 1):
                            f_rows(2, 6)
                        if (n, k, i) == (1, 2, 1):
                            f_rows(3, 4)
                        if (n, k, i) == (2, 2, 2):
                            router_exp(2)
                            router_exp(3)
                        act.wait_ge(S["a_ps"], u + 1)
                        if u >= 2:
                            act.wait_ge(S["hh_ready"], u - 1)
                        nc.scalar.activation(sil[:, u % 2, :], bank[u % 2][:, :], ACT.Silu,
                                             scale=1.0 / FFN_SCALE).then_inc(S["sil_ready"], 1)
                        if u:
                            high_part(u - 1)
            high_part(PAIRS * CH - 1)

        @block.vector
        def _(dve):
            n = [0]

            def link(ins):
                n[0] += 1
                ins.then_inc(S["vchain"], 1)
                dve.wait_ge(S["vchain"], n[0])

            V_ = nc.vector

            link(V_.memset(embc[:, :, :], 1.0))
            link(V_.memset(startc[:, :], 1.0))
            link(V_.memset(table[:, :], 0.0))
            link(V_.memset(Xp[:, :, 0:PAD], 0.0))
            dve.wait_ge(S["ld_emb"], 32)
            for d in range(2):
                link(V_.tensor_scalar(embc[0:EMB, d, :], embp[0:EMB, 0:V], embp[0:EMB, 2 * V:2 * V + 1], None,
                                      ALU.add))
                link(V_.tensor_copy(inw2[:, d, :], embp[:, V:2 * V]))
            V_.tensor_tensor(startc[0:EMB, :], embp[0:EMB, 2 * V + 1:2 * V + 2], embp[0:EMB, 2 * V:2 * V + 1],
                             ALU.add).then_inc(S["embc_ready"], 1)
            dve.wait_ge(S["consts"], 1)
            dve.wait_ge(S["ld_tok"], 32)
            for gm in range(2):
                V_.tensor_scalar(onehot[:, 2 * gm:2 * gm + 2, 1:T], idx[:, 2 * gm:2 * gm + 2, 1:T], vcol[:, 0:1],
                                 None, ALU.is_equal).then_inc(S["onehot_ready"], 1)
            dve.wait_ge(S["table_ps"], 1)
            link(V_.tensor_copy(table[0:64, 0:64], bank[4][0:64, 0:64]))
            link(V_.tensor_copy(Xp[:, :, PAD:PAD + 1], bank[4][:, 64:65].unsqueeze(1).to_broadcast([P, 4, 1])))
            V_.tensor_copy(table[64:P, 64:P], bank[4][64:P, 0:64]).then_inc(S["table_ready"], 1)
            V_.memset(Wt[0:64, :, 64:P], 0.0).then_inc(S["wt_zero_high"], 1)
            for p in range(PAIRS):
                dve.wait_ge(S["emb_ps"], p + 1)
                V_.tensor_copy(Xp[:, p, PAD + 1:PAD + T], bank[p][:, 1:T]).then_inc(S["x_ready"], 1)

            def residual(l, p):
                dve.wait_ge(S["pw_gelu"], PAIRS * l + p + 1)
                dve.wait_ge(S["conv_ps"], PAIRS * l + p + 1)
                V_.tensor_tensor(Xp[:, p, PAD:PAD + T], Xp[:, p, PAD:PAD + T], hid2[:, p, :], ALU.add) \
                    .then_inc(S["x_ready"], 1)

            def split16(hi, lo, src, scale, scratch):
                link(V_.tensor_scalar(scratch, src, scale, None, ALU.mult))
                link(V_.tensor_copy(hi, scratch))
                link(V_.tensor_tensor(lo, scratch, hi, ALU.subtract))

            def weights_setup(stage):
                if stage == 0:
                    dve.wait_ge(S["ld_attn"], 48)
                    split16(qwh[:, 0, :, :], qwh[:, 1, :, :], qw[:, :, :], ATT_SCALE, qw[:, :, :])
                    link(V_.tensor_scalar(ew[:, :, :], ew[:, :, :], ATT_SCALE, None, ALU.mult))
                    link(V_.tensor_copy(ewx[:, 0, :, :], ew[:, :, :]))
                    V_.tensor_tensor(ewx[:, 1, :, :], ew[:, :, :], ewx[:, 0, :, :], ALU.subtract) \
                        .then_inc(S["wts_ready"], 1)
                    dve.wait_ge(S["wts_ready"], 1)
                elif stage == 1:
                    dve.wait_ge(S["ld_ffn"], 16 * 16)
                    link(V_.tensor_scalar(qkvw[:, :], qkvw[:, :], lns[:, 0:1], None, ALU.mult))
                    split16(qkvh[:, 0, :], qkvh[:, 1, :], qkvw[:, :], FFN_SCALE, qkvw[:, :])
                    link(V_.tensor_scalar(rw[:, :], rw[:, :], lns[:, 1:2], None, ALU.mult))
                    split16(rwh[:, 0, :], rwh[:, 1, :], rw[:, :], FFN_SCALE, rw[:, :])
                elif stage in (2, 3):
                    dve.wait_ge(S["ld_w1" if stage == 2 else "ld_w3"], 64)
                    dst = w1h if stage == 2 else w3h
                    link(V_.tensor_scalar(w1s[:, :, :], w1s[:, :, :], lns[:, 1:2], FFN_SCALE, ALU.mult, ALU.mult))
                    link(V_.tensor_copy(dst[:, 0, :, :], w1s[:, :, :]))
                    V_.tensor_tensor(dst[:, 1, :, :], w1s[:, :, :], dst[:, 0, :, :], ALU.subtract) \
                        .then_inc(S["w1cast"], 1)
                    dve.wait_ge(S["w1cast"], stage - 1)

            for l in range(LAYERS - 1):
                for p in range(PAIRS):
                    residual(l, p)
                if l < 4:
                    weights_setup(l)

            dve.wait_ge(S["ld_w2"], 48)
            for w in (w2s, w2x):
                V_.tensor_scalar(w, w, FFN_SCALE, None, ALU.mult).then_inc(S["w2_scaled"], 1)

            def bc4(ap):
                return ap.unsqueeze(2).to_broadcast([P, 4, V])

            def logits_out(p):
                g4 = slice(4 * p, 4 * p + 4)
                dve.wait_ge(S["logits_ps"], p + 1)
                (V_.tensor_tensor(L[:, g4, :].rearrange("p (hf tt) v -> p tt hf v", hf=2),
                                      bank[4 + p][:, 0:256].rearrange("p (tt hf v) -> p tt hf v", tt=2, hf=2),
                                      b2bc[:, :].unsqueeze(1).unsqueeze(1).to_broadcast([P, 2, 2, V]), ALU.add)
                 .then_inc(S["logits_read"], 1))

            def ln0_a(p):
                g4 = slice(4 * p, 4 * p + 4)
                dve.wait_ge(S["logits_read"], p + 1)
                link(V_.tensor_reduce(stat[:, 2, g4], L[:, g4, :], AX, ALU.max))
                V_.tensor_tensor(L[:, g4, :], L[:, g4, :], bc4(stat[:, 2, g4]), ALU.subtract) \
                    .then_inc(S["lsub_ready"], 1)
                dve.wait_ge(S["lsub_ready"], p + 1)

            def centre(p, src, c_, q_, at, ready):
                g4 = slice(4 * p, 4 * p + 4)
                link(V_.tensor_reduce(stat[:, 2, g4], src, AX, ALU.add))
                link(V_.scalar_tensor_tensor(c_, bc4(stat[:, 2, g4]), -1.0 / V, src, ALU.mult, ALU.add))
                link(V_.tensor_tensor(q_, c_, c_, ALU.mult))
                link(V_.tensor_reduce(stat[:, 9, g4], q_, AX, ALU.add))
                V_.tensor_scalar(stat[:, at, g4], stat[:, 9, g4], 1.0 / V, 1e-5, ALU.mult, ALU.add) \
                    .then_inc(S[ready], 1)

            def ln0_b(p):
                centre(p, L[:, 4 * p:4 * p + 4, :], cen[:, p % 2], sqr[:, p % 2], 3, "var_ready")

            def exp_sum(p):
                dve.wait_ge(S["exp_ready"], p + 1)
                V_.tensor_reduce(stat[:, 0, 4 * p:4 * p + 4], ex[:, p % 2, :, :], AX, ALU.add) \
                    .then_inc(S["lsum_ready"], 1)

            def ln0_c(p):
                g4 = slice(4 * p, 4 * p + 4)
                dve.wait_ge(S["rstd_ready"], p + 1)
                if p >= 2:
                    dve.wait_ge(S["shl_ready"], max(p - 2, 1))
                    dve.wait_ge(S["M_ps"], p - 1)
                    dve.wait_ge(S["bdS_ready"], p - 1)
                V_.tensor_tensor(s2[:, p % 2, :, :, :], cen[:, p % 2, :, :].unsqueeze(2).to_broadcast([P, 4, 2, V]),
                                 stat[:, 4, g4].unsqueeze(2).unsqueeze(2).to_broadcast([P, 4, 2, V]), ALU.mult) \
                    .then_inc(S["s_ready"], 1)

            def mask_omega(g):
                dve.wait_ge(S["om_ps"], g + 1)
                if g >= 2:
                    dve.wait_ge(S["o_ps"], g - 1)
                V_.tensor_tensor(om[:, g % 2, :].rearrange("p (a t) -> p a t", t=64),
                                 bank[4][:, :].rearrange("p (a t) -> p a t", t=64),
                                 trimul[:, :].unsqueeze(1).to_broadcast([P, 8, 64]), ALU.mult) \
                    .then_inc(S["om_ready"], 1)

            def ln2_a(p):
                g4 = slice(4 * p, 4 * p + 4)
                dve.wait_ge(S["e_ps"], 4 * p + 4)
                dve.wait_ge(S["h_ready"], p + 1)
                V_.tensor_tensor(h[:, g4, :], h[:, g4, :], bank[7][:, 0:256].rearrange("p (a c) -> p a c", a=4),
                                 ALU.add).then_inc(S["h2_ready"], 1)
                dve.wait_ge(S["h2_ready"], p + 1)

            def ln2_b(p):
                if p:
                    dve.wait_ge(S["hr_ready"], p)
                centre(p, h[:, 4 * p:4 * p + 4, :], cenB[:, :, :], sqrB[:, :, :], 11, "var2_ready")

            def ln2_c(p):
                g4 = slice(4 * p, 4 * p + 4)
                dve.wait_ge(S["rstd2_ready"], p + 1)
                link(V_.tensor_tensor(xf[:, g4, :], cenB[:, :, :], bc4(stat[:, 12, g4]), ALU.mult))
                link(V_.tensor_tensor(stat[:, 10, g4], stat[:, 12, g4], stat[:, 12, g4], ALU.mult))
                link(V_.tensor_tensor(stat[:, 10, g4], stat[:, 10, g4], stat[:, 9, g4], ALU.mult))
                V_.tensor_scalar(stat[:, 5, g4], stat[:, 10, g4], 1.0 / V, 1e-6, ALU.mult, ALU.add) \
                    .then_inc(S["q1_ready"], 1)

            def ln2_d(p):
                g4 = slice(4 * p, 4 * p + 4)
                dve.wait_ge(S["rinv_ready"], p + 1)
                if p:
                    dve.wait_ge(S["hsplit_ready"], p)
                V_.tensor_tensor(hrB[:, :, :], xf[:, g4, :], bc4(stat[:, 6, g4]), ALU.mult) \
                    .then_inc(S["hr_ready"], 1)

            def rotary(p):
                dve.wait_ge(S["qkv_ps"], p + 1)
                if p == 3:
                    dve.wait_ge(S["parts2_ready"], 6)
                src = bank[QKV_BANK[p]][:, :].rearrange("p (a c) -> p a c", a=4)
                qk = src[:, :, 0:96]
                link(V_.tensor_tensor(rope[:, :, :], qk, cos4[:, :, :], ALU.mult))
                for d in range(2):
                    def half(ap, k):
                        return ap.rearrange("p a (n two e) -> p a n two e", two=2, e=8)[:, :, :, k, :]
                    link(V_.tensor_tensor(half(rot[:, :, :], d), half(qk, 1 - d), half(sin4[:, :, :], d), ALU.mult))
                dve.wait_ge(S["consts"], 13)
                V_.tensor_scalar(vaug[:, 4 * p:4 * p + 4, :, 0:HD],
                                 src[:, :, 96:128].rearrange("p a (n e) -> p a n e", e=HD), 1.0 / FFN_SCALE, None,
                                 ALU.mult).then_inc(S["v_ready"], 1)
                ins = V_.tensor_tensor(rope[:, :, :], rope[:, :, :], rot[:, :, :], ALU.add)
                if p == 2:
                    ins.then_inc(S["rope_ready"], 1)
                else:
                    link(ins)

            def three_parts(p):
                if p >= 2:
                    dve.wait_ge(S["stk_ps"], 4 * (p - 1))
                r6 = rope[:, :, :].rearrange("p a (n e) -> p a n e", e=HD)
                t6 = rot[:, :, :].rearrange("p a (n e) -> p a n e", e=HD)
                d_ = qst[:, p % 2, :, :, :, :]
                link(V_.tensor_copy(d_[:, :, :, 0, :], r6))
                link(V_.tensor_tensor(t6, r6, d_[:, :, :, 0, :], ALU.subtract))
                link(V_.tensor_copy(d_[:, :, 0:4, 3, :], t6[:, :, 0:4, :]))
                link(V_.tensor_copy(d_[:, :, 4:6, 1, :], t6[:, :, 4:6, :]))

            def three_parts_end(p):
                t6 = rot[:, :, :].rearrange("p a (n e) -> p a n e", e=HD)
                d_ = qst[:, p % 2, :, :, :, :]
                V_.tensor_tensor(d_[:, :, 0:4, 5, :], t6[:, :, 0:4, :], d_[:, :, 0:4, 3, :], ALU.subtract)
                V_.tensor_tensor(d_[:, :, 4:6, 2, :], t6[:, :, 4:6, :], d_[:, :, 4:6, 1, :], ALU.subtract)
                V_.tensor_copy(d_[:, :, 0:4, 1, :], d_[:, :, 0:4, 0, :])
                V_.tensor_copy(d_[:, :, 0:4, 2, :], d_[:, :, 0:4, 0, :])
                V_.tensor_copy(d_[:, :, 0:4, 4, :], d_[:, :, 0:4, 3, :])
                V_.tensor_copy(d_[:, :, 4:6, 3, :], d_[:, :, 4:6, 0, :])
                V_.tensor_copy(d_[:, :, 4:6, 5, :], d_[:, :, 4:6, 0, :])
                V_.tensor_copy(d_[:, :, 4:6, 4, :], d_[:, :, 4:6, 1, :]).then_inc(S["split_ready"], 1)
                dve.wait_ge(S["split_ready"], min(p, 2) + 1)

            dve.wait_ge(S["ld_tcn1"], 48)
            residual(LAYERS - 1, 0)
            residual(LAYERS - 1, 1)
            residual(LAYERS - 1, 2)
            logits_out(0)
            dve.wait_ge(S["logits_read"], 1)
            ln0_b(0)
            residual(LAYERS - 1, 3)
            ln0_a(0)
            logits_out(1)
            ln0_c(0)
            dve.wait_ge(S["s_ready"], 1)
            link(V_.tensor_copy(shl[:, 0, :, 1, :], s2[:, 0, :, 0, :]))
            V_.tensor_tensor(shl[:, 0, :, 2, :], s2[:, 0, :, 0, :], shl[:, 0, :, 1, :], ALU.subtract) \
                .then_inc(S["shl0_ready"], 1)
            logits_out(2)
            logits_out(3)
            ln0_a(1)
            ln0_b(1)
            ln0_a(2)
            ln0_a(3)
            dve.wait_ge(S["consts"], 6)
            for g in range(TILES):
                p, s = g // 4, g % 4
                mask_omega(g)
                if g == 0:
                    exp_sum(0)
                    exp_sum(1)
                if g == 3:
                    exp_sum(2)
                    exp_sum(3)
                if s == 0 and p + 1 < PAIRS:
                    ln0_c(p + 1)
                if s == 1 and p:
                    ln2_a(p - 1)
                    ln2_b(p - 1)
                if s == 2:
                    if p:
                        ln2_c(p - 1)
                    if p >= 2:
                        rotary(p - 2)
                if s == 3:
                    if p:
                        ln2_d(p - 1)
                    if p + 2 < PAIRS:
                        ln0_b(p + 2)
                    if p >= 2:
                        three_parts(p - 2)
                        three_parts_end(p - 2)

            def row_max(b):
                for u in range(3):
                    dve.wait_ge(S["p1_ps"], 3 * b + u + 1)
                    g, h0, nh = (2 * b, 0, 4) if u == 0 else (2 * b + 1, 2 * (u - 1), 2)
                    V_.tensor_reduce(nmx[:, g, h0:h0 + nh],
                                     bank[3 + (3 * b + u) % 2][:, :].rearrange("p (n s) -> p n s", n=nh),
                                     AX, ALU.max, negate=True).then_inc(S["max_ready"], 1)
                dve.wait_ge(S["max_ready"], 3 * b + 3)
                src, d_, r_ = nmx[:, 2 * b:2 * b + 2, :], nms[:, b % 2, :, :, :], nmr[:, b % 2, :, :]
                if b >= 2:
                    dve.wait_ge(S["nmT_ps"], b - 1)
                link(V_.tensor_copy(d_[:, :, :, 0], src))
                link(V_.tensor_tensor(r_, src, d_[:, :, :, 0], ALU.subtract))
                link(V_.tensor_copy(d_[:, :, :, 1], r_))
                V_.tensor_tensor(d_[:, :, :, 2], r_, d_[:, :, :, 1], ALU.subtract).then_inc(S["nms_ready"], 1)

            def max_out(b):
                dve.wait_ge(S["nmT_ps"], b + 1)
                if b >= 2:
                    dve.wait_ge(S["p2_ps"], 3 * b - 3)
                V_.tensor_copy(nmT[:, b % 2, :, :].rearrange("p a b -> p (a b)"),
                               bank[0][0:3 * NH, 0:P].bitcast(bf16)).then_inc(S["nmT_ready"], 1)

            def share(g):
                b = g // 2
                dve.wait_ge(S["wo_ps"], g + 1)
                if b >= 2:
                    dve.wait_ge(S["x2_ready"], b - 1)
                link(V_.reciprocal(rec[:, g, :], bank[2][:, NH * C:NWO]))
                V_.tensor_tensor(ym[:, b % 2, g % 2, :, :], bank[2][:, 0:NH * C].rearrange("p (n c) -> p n c", n=NH),
                                 rec[:, g, :].unsqueeze(2).to_broadcast([P, NH, C]), ALU.mult) \
                    .then_inc(S["ym_ready"], 1)

            def rms_square(p):
                g4 = slice(4 * p, 4 * p + 4)
                dve.wait_ge(S["x2_ready"], 2 * p + 2)
                link(V_.tensor_tensor(sqr[:, p % 2, :, :], x2[:, g4, :], x2[:, g4, :], ALU.mult))
                link(V_.tensor_reduce(stat[:, 10, g4], sqr[:, p % 2, :, :], AX, ALU.add))
                V_.tensor_scalar(stat[:, 7, g4], stat[:, 10, g4], 1.0 / C, 1e-6, ALU.mult, ALU.add) \
                    .then_inc(S["ss_ready"], 1)

            def rms_rows(p):
                g4 = slice(4 * p, 4 * p + 4)
                dve.wait_ge(S["r2_ready"], p + 1)
                if p >= 2:
                    dve.wait_ge(S["fsplit_ready"], p - 1)
                V_.tensor_tensor(s2[:, p % 2, :, 0, :], x2[:, g4, :], bc4(stat[:, 8, g4]), ALU.mult) \
                    .then_inc(S["fs_ready"], 1)

            def b8(ap):
                return ap.unsqueeze(2).to_broadcast([P, 4, NE])

            def router_in(p):
                g4 = slice(4 * p, 4 * p + 4)
                dve.wait_ge(S["rt_ps"], p + 1)
                l_ = lg[:, p, :, :]
                ps = bank[(1, 1, 7, 4)[p]][:, 0:4 * NE].rearrange("p (a e) -> p a e", a=4)
                link(V_.tensor_reduce(stat[:, 10, g4], ps, AX, ALU.max))
                link(V_.tensor_tensor(l_, ps, b8(stat[:, 10, g4]), ALU.subtract))
                V_.tensor_scalar(l_, l_, 1.0 / FFN_SCALE, None, ALU.mult).then_inc(S["rexp_in"], 1)

            def ranks(p):
                dve.wait_ge(S["rexp_ready"], p + 1)
                l_ = lg[:, p, :, :]
                e_i = l_.unsqueeze(3).to_broadcast([P, 4, NE, NE])
                e_j = l_.unsqueeze(2).to_broadcast([P, 4, NE, NE])
                low = lowidx[:, :, :].unsqueeze(1).to_broadcast([P, 4, NE, NE])
                link(V_.tensor_tensor(gt[:, :, :, :], e_j, e_i, ALU.is_gt))
                link(V_.tensor_tensor(ge[:, :, :, :], e_j, e_i, ALU.is_ge))
                link(V_.tensor_tensor(ge[:, :, :, :], ge[:, :, :, :], low, ALU.mult))

            def ranks_end(p):
                g4 = slice(4 * p, 4 * p + 4)
                link(V_.tensor_tensor(ge[:, :, :, :], ge[:, :, :, :], gt[:, :, :, :], ALU.max))
                link(V_.tensor_reduce(gate[:, g4, :], ge[:, :, :, :], AX, ALU.add))

            def gates(p):
                g4 = slice(4 * p, 4 * p + 4)
                l_ = lg[:, p, :, :]
                link(V_.scalar_tensor_tensor(gate[:, g4, :], gate[:, g4, :], 1.5, l_, ALU.is_lt, ALU.mult))
                link(V_.tensor_reduce(stat[:, 10, g4], l_, AX, ALU.add))
                link(V_.tensor_reduce(stat[:, 9, g4], gate[:, g4, :], AX, ALU.add))
                link(V_.scalar_tensor_tensor(stat[:, 9, g4], stat[:, 10, g4], 1e-9, stat[:, 9, g4], ALU.mult, ALU.add))
                link(V_.reciprocal(stat[:, 10, g4], stat[:, 9, g4]))
                V_.scalar_tensor_tensor(gate[:, g4, :], gate[:, g4, :], 1.0 / (HH_SCALE * FFN_SCALE),
                                        b8(stat[:, 10, g4]), ALU.mult, ALU.mult) \
                    .then_inc(S["gate_ready"], 1)
                dve.wait_ge(S["gate_ready"], p + 1)

            row_max(0)
            max_out(0)
            for b in range(B + 1):
                if b + 1 < B:
                    row_max(b + 1)
                if b == 0:
                    rotary(2)
                    ln2_a(3)
                if b == 3:
                    rotary(3)
                if b == 4:
                    three_parts_end(3)
                if b in RMS_ROWS:
                    rms_rows(RMS_ROWS[b])
                if b in (7, 8):
                    router_in(b - 7)
                if b >= 1:
                    share(2 * b - 2)
                if b + 1 < B:
                    max_out(b + 1)
                if b == 1:
                    ln2_b(3)
                if b == 2:
                    ln2_c(3)
                if b == 3:
                    three_parts(3)
                if b in RMS_SQUARE:
                    rms_square(RMS_SQUARE[b])
                if b >= 1:
                    share(2 * b - 1)
                if b == 2:
                    ln2_d(3)
                    dve.wait_ge(S["hr_ready"], PAIRS)
                    dve.wait_ge(S["trh_ps"], PAIRS - 1)
                    link(V_.tensor_copy(shlB[:, :, 0, :], hrB[:, :, :]))
                    V_.tensor_tensor(shlB[:, :, 1, :], hrB[:, :, :], shlB[:, :, 0, :], ALU.subtract) \
                        .then_inc(S["hsplit3_ready"], 1)

            def mix(g):
                dve.wait_ge(S["w2_ps"], 16 * (g // 4) + 12 + g % 4 + 1)
                V_.tensor_tensor(moe[:, g % 4, :, :], bank[4 + g % 4][:, :].rearrange("p (e c) -> p e c", e=NE),
                                 gate[:, g, :].unsqueeze(2).to_broadcast([P, NE, C]), ALU.mult) \
                    .then_inc(S["mix_ready"], 1)

            def reduce_rows(g):
                dve.wait_ge(S["mix_ready"], g + 1)
                dve.wait_ge(S["hx_ready"], PAIRS)
                link(V_.tensor_reduce(fin[:, g, :], moe[:, g % 4, :, :].rearrange("p e c -> p c e"), AX, ALU.add))
                V_.tensor_tensor(fin[:, g, :], fin[:, g, :], hx[:, g, :], ALU.add).then_inc(S["fin_ready"], 1)

            for n_ in range(PAIRS):
                for k in range(NE // 2):
                    for i in range(3):
                        u = CH * n_ + 3 * k + i
                        dve.wait_ge(S["sil_ready"], u + 1)
                        dve.wait_ge(S["b_ps"], u + 1)
                        if u >= RING:
                            dve.wait_ge(S["lo_ready"], u - RING + 1)
                        V_.scalar_tensor_tensor(hh[:, u % RING, :], bank[2 + u % 2][:, :], HH_SCALE / FFN_SCALE,
                                                sil[:, u % 2, :], ALU.mult, ALU.mult).then_inc(S["hh_ready"], 1)
                        if (n_, k, i) == (2, 2, 0):
                            router_in(3)
                        if n_ and 3 * k + i in (4, 5, 6, 7):
                            mix(4 * (n_ - 1) + 3 * k + i - 4)
                        if n_ and 3 * k + i >= 8:
                            reduce_rows(4 * (n_ - 1) + 3 * k + i - 8)
                        if (n_, k, i) == (0, 1, 2):
                            router_in(2)
                        if (n_, k, i) == (0, 0, 2):
                            rms_square(3)
                        if (n_, k, i) == (0, 2, 0):
                            rms_rows(3)
                        for p_, (first, second, third) in enumerate(GATE_STEPS):
                            if u == first:
                                ranks(p_)
                            if u == second:
                                ranks_end(p_)
                            if u == third:
                                gates(p_)
            for g in range(TILES - 4, TILES):
                mix(g)
                reduce_rows(g)

        @block.tensor
        def _(pe):
            def mm(out_, l_, r_, a, z, skip=False):
                return nc.tensor.matmul(out_, l_, r_, start=a, stop=z, skip_group_check=skip)

            pe.wait_ge(S["embc_ready"], 1)
            mm(bank[4][:, 0:64], embc[:, :, :].rearrange("p a b -> p (a b)"), embp[:, V:2 * V], True, True)
            mm(bank[4][:, 64:65], inw2[:, :, :].rearrange("p a b -> p (a b)"), startc[:, :], True, True) \
                .then_inc(S["table_ps"], 1)
            pe.wait_ge(S["table_ready"], 1)
            for p in range(PAIRS):
                pe.wait_ge(S["onehot_ready"], p // 2 + 1)
                mm(bank[p][:, 1:T], table[:, :], onehot[:, p, 1:T], True, True).then_inc(S["emb_ps"], 1)

            def conv(l, p):
                pe.wait_ge(S["x_ready"], PAIRS * l + p + 1)
                if l:
                    pe.wait_ge(S["hid_ready"], PAIRS * (l - 1) + p + 1)
                for k in range(TAPS):
                    at = PAD - (TAPS - 1 - k) * 2 ** l
                    r = mm(bank[p][:, 0:T], Wt[:, (TAPS + 1) * l + k, :], Xp[:, p, at:at + T], k == 0, k == TAPS - 1)
                r.then_inc(S["conv_ps"], 1)

            def pointwise(l, p):
                pe.wait_ge(S["hid_ready"], PAIRS * l + p + 1)
                if l:
                    pe.wait_ge(S["pw_gelu"], PAIRS * (l - 1) + p + 1)
                mm(bank[4 + p][:, 0:T], Wt[:, (TAPS + 1) * l + TAPS, :], hid1[:, p, :], True, True) \
                    .then_inc(S["pw_ps"], 1)

            def out1(p):
                pe.wait_ge(S["x_ready"], PAIRS * LAYERS + p + 1)
                mm(bank[p][:, 0:T], Wt[:, NBLK - 2, :], Xp[:, p, PAD:PAD + T], True, True) \
                    .then_inc(S["out1_ps"], 1)

            def logits(p):
                pe.wait_ge(S["out_gelu"], p + 1)
                for tt in range(2):
                    r = mm(bank[4 + p][:, P * tt:P * tt + P], hid1[:, p, P * tt:P * tt + P], Wt[:, NBLK - 1, :],
                           True, True)
                r.then_inc(S["logits_ps"], 1)

            for l in range(LAYERS - 1):
                if l == 0:
                    pe.wait_ge(S["ld_tcn0"], 64)
                    pe.wait_ge(S["wt_zero_low"], 1)
                    pe.wait_ge(S["wt_zero_high"], 1)
                if l == 1:
                    pe.wait_ge(S["ld_tcn1"], 48)
                for p in range(PAIRS):
                    conv(l, p)
                for p in range(PAIRS):
                    pointwise(l, p)
            l = LAYERS - 1
            conv(l, 0)
            conv(l, 1)
            pointwise(l, 0)
            pointwise(l, 1)
            conv(l, 2)
            out1(0)
            pointwise(l, 2)
            conv(l, 3)
            out1(1)
            logits(0)
            out1(2)
            pointwise(l, 3)
            logits(1)
            logits(2)
            out1(3)
            logits(3)

            def prep(p):
                pe.wait_ge(S["s_ready"], p + 1)
                pe.wait_ge(S["consts"], 3)
                if p == 0:
                    pe.wait_ge(S["out_gelu"], 2)
                else:
                    pe.wait_ge(S["bdT_ready"], p)
                    pe.wait_ge(S["M_ready"], p)
                for a in range(4):
                    r = nc.tensor.transpose(bank[0][:, P * a:P * a + P],
                                            s2[:, p % 2, a, :, :].rearrange("p a b -> p (a b)"), identf[:, :])
                r.then_inc(S["tr32_ps"], 1)
                pe.wait_ge(S["shl_ready" if p else "shl0_ready"], max(p, 1))
                for a in range(4):
                    r = nc.tensor.transpose(bank[1][:, 64 * a:64 * a + 64].bitcast(f16),
                                            shl[:, p % 2, a, 1:3, :].rearrange("p a b -> p (a b)"), ident16[:, :])
                r.then_inc(S["tr16_ps"], 1)

            def outer_sums(p):
                pe.wait_ge(S["sTs_ready"], p + 1)
                pe.wait_ge(S["twice_ready"], p + 1)
                for hf in range(2):
                    for k in range(3):
                        o = bank[1][:, 64 * (3 * hf + k):64 * (3 * hf + k) + 64]
                        parts = [(2 * hf, 64 if k == 0 else P)] + ([(2 * hf + 1, 64)] if k == 2 else [])
                        prods = [(a, rows, x_, w_) for a, rows in parts for x_, w_ in ((0, 0), (0, 1), (1, 0))]
                        for i, (a, rows, x_, w_) in enumerate(prods):
                            r = mm(o, shl[0:rows, p % 2, a, 2 * x_:2 * x_ + 2, :].rearrange("p a b -> p (a b)"),
                                   shl[0:rows, p % 2, a, 1 + w_, :], i == 0, i == len(prods) - 1)
                r.then_inc(S["M_ps"], 1)

            def query(p, a):
                pe.wait_ge(S["sTs_ready"], p + 1)
                if p == 0 and a == 0:
                    pe.wait_ge(S["wts_ready"], 1)
                    pe.wait_ge(S["out_gelu"], PAIRS)
                if 4 * p + a >= 2:
                    pe.wait_ge(S["q_ready"], 4 * p + a - 1)
                rhs = sTs[:, 4 * p:4 * p + 4, :].rearrange("p a b -> p (a b)")
                for w in range(2):
                    r = mm(bank[2 + a % 2][:, :], qwh[:, w, a, :], rhs, w == 0, w == 1)
                r.then_inc(S["q_ps"], 1)

            def omega(g):
                p = g // 4
                pe.wait_ge(S["q_ready"], 4 * p + 4)
                pe.wait_ge(S["bdT_ready"], p + 1)
                if g == 0:
                    pe.wait_ge(S["logits_read"], 1)
                if g >= 1:
                    pe.wait_ge(S["om_ready"], g)
                for cc in range(2):
                    t0 = P * (g % 4) + 64 * cc
                    r = mm(bank[4][:, 256 * cc:256 * cc + 256].rearrange("p (a t) -> p a t", a=4),
                           bdT[:, 2 * g + cc, :], qT[:, p % 2, :, t0:t0 + 64], True, True)
                r.then_inc(S["om_ps"], 1)

            def attend(g):
                p = g // 4
                pe.wait_ge(S["om_ready"], g + 1)
                pe.wait_ge(S["bdS_ready"], p + 1)
                pe.wait_ge(S["M_ready"], p + 1)
                if g == 0:
                    pe.wait_ge(S["logits_read"], 3)
                if g >= 1:
                    pe.wait_ge(S["o_ready"], g)
                for cc in range(2):
                    k = 2 * (g % 2) + cc
                    o = bank[6][:, 256 * cc:256 * cc + 256]
                    t0 = P * (g % 4) + 64 * cc
                    r = mm(o, bdS[:, 2 * g + cc, :], om[:, g % 2, 256 * cc:256 * cc + 256], True, k == 0)
                    if k:
                        r = mm(o.rearrange("p (a t) -> p a t", a=4), bdM[:, g // 2, k - 1, :],
                               qT[:, p % 2, :, t0:t0 + 64], False, True)
                r.then_inc(S["o_ps"], 1)

            def project(g):
                pe.wait_ge(S["o_low"], g + 1)
                if g == 0:
                    pe.wait_ge(S["logits_read"], 4)
                if g % 4 == 0 and g:
                    pe.wait_ge(S["h2_ready"], g // 4)
                for a in range(4):
                    for n, (x_, w_) in enumerate(((0, 0), (0, 1), (1, 0))):
                        r = mm(bank[7][:, 64 * (g % 4):64 * (g % 4) + 64], oTx[:, g % 2, x_, a, :], ewx[:, w_, a, :],
                               a == 0 and n == 0, a == 3 and n == 2)
                r.then_inc(S["e_ps"], 1)

            def rows(p):
                if p < 3:
                    pe.wait_ge(S["hsplit_ready"], p + 1)
                else:
                    pe.wait_ge(S["hsplit3_ready"], 1)
                before = (("logits_read", 2), ("v_ready", 1), ("q_ready", TILES), ("nmT_ready", 4))[p]
                pe.wait_ge(S[before[0]], before[1])
                b_ = bank[QKV_BANK[p]]
                for a in range(4):
                    r = nc.tensor.transpose(b_[:, 64 * a:64 * a + 64].bitcast(f16),
                                            shlB[:, a, :, :].rearrange("p a b -> p (a b)"), ident16[:, :])
                r.then_inc(S["trh_ps"], 1)

            def qkv(p):
                pe.wait_ge(S["hTs_ready"], p + 1)
                if p == 0:
                    pe.wait_ge(S["w1cast"], 1)
                for a in range(4):
                    for w in range(2):
                        r = mm(bank[QKV_BANK[p]][:, P * a:P * a + P], hTs[:, 4 * p + a, :], qkvh[:, w, :],
                               w == 0, w == 1)
                r.then_inc(S["qkv_ps"], 1)

            def stack(g):
                p = g // 4
                if p == 2:
                    pe.wait_ge(S["parts2_ready"], 6)
                else:
                    pe.wait_ge(S["split_ready"], min(p, 2) + 1)
                if g < 2:
                    pe.wait_ge(S[("bdT_ready", "M_ready")[g]], PAIRS)
                else:
                    pe.wait_ge(S["stk_ready"], g - 1 if g < 6 else g)
                for n_ in range(6):
                    r = nc.tensor.transpose(bank[stack_bank(g)][0:96, 64 * n_:64 * n_ + 64].bitcast(bf16),
                                            qst[:, p % 2, g % 4, n_, :, :].rearrange("p a b -> p (a b)"),
                                            identb[:, :])
                r.then_inc(S["stk_ps"], 1)

            def scores_for_max(b, u):
                pe.wait_ge(S["stk_ready"], 2 * b + (1 if u == 0 else 2))
                U = 3 * b + u
                if U == 0:
                    pe.wait_ge(S["consts"], 14)
                    pe.wait_ge(S["q_ready"], TILES)
                if U == 1:
                    pe.wait_ge(S["om_ready"], TILES)
                if U >= 2:
                    pe.wait_ge(S["max_ready"], U - 1)
                o = bank[3 + U % 2]
                if u == 0:
                    mm(o[:, :], identb[:, :], mask_t[:, :, :].rearrange("p a b -> p (a b)"), True, False)
                    for n_ in range(NH):
                        r = mm(o[:, P * n_:P * n_ + P], qkT[:, 2 * b, n_, :], qkT[:, 2 * b, NH + n_ // 2, :],
                               False, n_ == NH - 1)
                else:
                    for i in range(2):
                        n_ = 2 * (u - 1) + i
                        mm(o[:, T * i:T * i + T].rearrange("p (a s) -> p a s", a=2),
                           qkT[:, 2 * b + 1, n_, :], qkT[:, 2 * b:2 * b + 2, NH + n_ // 2, :], True, False)
                        r = mm(o[:, T * i + P:T * i + T], identb[:, :], mask_t[:, 0, :], False, True)
                r.then_inc(S["p1_ps"], 1)

            def max_rows(b):
                pe.wait_ge(S["nms_ready"], b + 1)
                if b:
                    pe.wait_ge(S["nmT_ready"], b)
                if b == 0:
                    pe.wait_ge(S["stk_ready"], 5)
                if b == 4:
                    pe.wait_ge(S["v_ready"], PAIRS)
                for a in range(2):
                    r = nc.tensor.transpose(bank[0][0:3 * NH, 64 * a:64 * a + 64].bitcast(bf16),
                                            nms[:, b % 2, a, :, :].rearrange("p a b -> p (a b)"), identb[:, :])
                r.then_inc(S["nmT_ps"], 1)

            def scores_shifted(b, u):
                pe.wait_ge(S["nmT_ready"], b + 1)
                U = 3 * b + u
                if U == 0:
                    pe.wait_ge(S["v_ready"], 2)
                if U == 1:
                    pe.wait_ge(S["o_ready"], TILES)
                if U >= 2:
                    pe.wait_ge(S["exp2_ready"], U - 1)
                o = bank[5 + U % 2]
                if u < 2:
                    for i in range(2):
                        n_ = 2 * u + i
                        ov_ = o[:, T * i:T * i + T].rearrange("p (a s) -> p a s", a=2)
                        mm(ov_, qkT[:, 2 * b, NH + n_ // 2, :], qkT[:, 2 * b:2 * b + 2, n_, :], True, False)
                        mm(ov_, selh[:, n_, :], nmT[:, b % 2, :, :], False, False)
                        r = mm(o[:, T * i:T * i + P], identb[:, :], mask_s[:, 0, :], False, True)
                else:
                    mm(o[:, :], identb[:, :], mask_s[:, :, :].rearrange("p a b -> p (a b)"), True, False)
                    for n_ in range(NH):
                        ov_ = o[:, P * n_:P * n_ + P]
                        mm(ov_, selh[:, n_, :], nmT[:, b % 2, 1, :], False, False)
                        r = mm(ov_, qkT[:, 2 * b + 1, NH + n_ // 2, :], qkT[:, 2 * b + 1, n_, :],
                               False, n_ == NH - 1)
                r.then_inc(S["p2_ps"], 1)

            def values(b):
                pe.wait_ge(S["exp2_ready"], 3 * b + 3)
                pe.wait_ge(S["v_ready"], b // 2 + 1)
                if b == 0:
                    pe.wait_ge(S["h2_ready"], PAIRS)
                else:
                    pe.wait_ge(S["yT_ready"], b)
                for n_ in range(NH):
                    o = bank[7][32 * n_:32 * n_ + 32, 0:T]
                    c0 = T * (n_ % 2)
                    mm(o, vaug[:, 2 * b, n_ // 2, :], pT[:, b % 2, n_ // 2, c0:c0 + T], True, False)
                    r = mm(bank[7][32 * n_:32 * n_ + 32, P:T], vaug[:, 2 * b + 1, n_ // 2, :],
                           pT[:, b % 2, 2, P * n_:P * n_ + P], False, True)
                r.then_inc(S["y_ps"], 1)

            def out_rows(b, a):
                pe.wait_ge(S["yT_ready"], b + 1)
                g = 2 * b + a
                if g:
                    pe.wait_ge(S["ym_ready"], g)
                else:
                    pe.wait_ge(S["v_ready"], 3)
                    pe.wait_ge(S["ld_ffn"], 16 * 16)
                mm(bank[2][:, 0:NWO], yT[:, b % 2, P * a:P * a + P], wo_sb[:, :], True, True) \
                    .then_inc(S["wo_ps"], 1)

            def f_transposed(p, b_):
                pe.wait_ge(S["fsplit_ready"], p + 1)
                if p == 0:
                    pe.wait_ge(S["stk_ready"], TILES)
                elif p == 1:
                    pe.wait_ge(S["rexp_in"], 1)
                elif p == 2:
                    pe.wait_ge(S["exp2_ready"], 3 * B)
                else:
                    pe.wait_ge(S["mix_ready"], 1)
                for a in range(4):
                    r = nc.tensor.transpose(bank[b_][:, 64 * a:64 * a + 64].bitcast(f16),
                                            shl[:, p % 2, a, 1:3, :].rearrange("p a b -> p (a b)"), ident16[:, :])
                r.then_inc(S["trf_ps"], 1)

            def routed(p, b_):
                pe.wait_ge(S["fTs_ready"], p + 1)
                if p == 2:
                    pe.wait_ge(S["yT_ready"], B)
                if p == 3:
                    pe.wait_ge(S["mix_ready"], 5)
                for a in range(4):
                    for w in range(2):
                        r = mm(bank[b_][:, NE * a:NE * a + NE], fTs[:, 4 * p + a, :], rwh[:, w, :], w == 0, w == 1)
                r.then_inc(S["rt_ps"], 1)

            prep(0)
            query(0, 0)
            query(0, 1)
            outer_sums(0)
            query(0, 2)
            query(0, 3)
            omega(0)
            pe.wait_ge(S["ld_attn"], 48)
            for g in range(TILES):
                p, s = g // 4, g % 4
                if s == 0 and p >= 2:
                    rows(p - 2)
                if s == 3 and p + 1 < PAIRS:
                    query(p + 1, 3)
                    attend(g)
                    omega(g + 1)
                else:
                    if g + 1 < TILES:
                        omega(g + 1)
                    attend(g)
                if s == 2 and p + 1 < PAIRS:
                    query(p + 1, 0)
                    outer_sums(p + 1)
                if g:
                    project(g - 1)
                if s == 1 and p + 1 < PAIRS:
                    prep(p + 1)
                if s == 2 and p + 1 < PAIRS:
                    query(p + 1, 1)
                    query(p + 1, 2)
                if s == 1 and p >= 2:
                    qkv(p - 2)
                if p == PAIRS - 1:
                    stack(s)
            scores_for_max(0, 0)
            rows(2)
            scores_for_max(0, 1)
            qkv(2)
            project(TILES - 1)
            stack(4)
            scores_for_max(0, 2)
            stack(5)

            def stack_at(b, place):
                if (b, place) in STACK_B:
                    stack(STACK_B[b, place])

            for b in range(B + 1):
                if b + 1 < B:
                    scores_for_max(b + 1, 0)
                    if b == 0:
                        max_rows(0)
                    scores_for_max(b + 1, 1)
                if b >= 1:
                    values(b - 1)
                if b == 3:
                    rows(3)
                if b + 1 < B:
                    scores_for_max(b + 1, 2)
                stack_at(b, 0)
                if b == 3:
                    qkv(3)
                if b in (6, 7):
                    f_transposed(b - 6, 1)
                if b < B:
                    scores_shifted(b, 0)
                if b >= 1:
                    out_rows(b - 1, 0)
                if b < B:
                    scores_shifted(b, 1)
                if b in (6, 7):
                    routed(b - 6, 1)
                if b + 1 < B:
                    max_rows(b + 1)
                stack_at(b, 1)
                if b < B:
                    scores_shifted(b, 2)
                if b >= 1:
                    out_rows(b - 1, 1)
                stack_at(b, 2)

            def down(n_, k, t_):
                v = 4 * n_ + k
                pe.wait_ge(S["lo_ready"], 3 * (v + 1))
                if v == 0:
                    pe.wait_ge(S["w2_cast"], 2)
                if v == 0 and t_ >= 2:
                    pe.wait_ge(S["fTs_ready"] if t_ == 2 else S["rexp_in"], 3)
                if n_ and k == 0:
                    pe.wait_ge(S["mix_ready"], 4 * (n_ - 1) + t_ + 1)
                if t_ == 0 and n_ in (1, 2) and k == 0:
                    pe.wait_ge(S["fTs_ready"] if n_ == 1 else S["rexp_in"], PAIRS)
                o = bank[4 + t_]
                c = slice(P * t_, P * t_ + P)
                parts = ((0, 0), (0, 1), (1, 0))
                for n, (x_, w_) in enumerate(parts):
                    mm(o[:, P * k:P * k + P], hhx[:, v % 3, x_, 2, c], w2xh[:, w_, k, :], n == 0, False)
                for i in range(2):
                    e = 2 * k + i
                    for n, (x_, w_) in enumerate(parts):
                        r = mm(o[:, C * e:C * e + C], hhx[:, v % 3, x_, i, c], w2h[:, w_, e, :], False,
                               i == 1 and n == 2)
                r.then_inc(S["w2_ps"], 1)

            for n_ in range(PAIRS):
                rhs = fTs[:, 4 * n_:4 * n_ + 4, :].rearrange("p a b -> p (a b)")
                pe.wait_ge(S["fTs_ready"], n_ + 1)
                for k in range(NE // 2):
                    for i in range(3):
                        v = 4 * n_ + k
                        u = 3 * v + i
                        j = 2 * k + i if i < 2 else NE + k
                        for w_, b0, read, done in ((w1h, 0, "sil_ready", "a_ps"), (w3h, 2, "hh_ready", "b_ps")):
                            if u == 0:
                                pe.wait_ge(S["nmT_ready" if b0 == 0 else "ym_ready"], B if b0 == 0 else TILES)
                                pe.wait_ge(S["w1cast"], 2)
                            if u == 1:
                                pe.wait_ge(S["rexp_in" if b0 == 0 else "max_ready"], 2 if b0 == 0 else 3 * B)
                            if u >= 2:
                                pe.wait_ge(S[read], u - 1)
                            for w in range(2):
                                r = mm(bank[b0 + u % 2][:, :], w_[:, w, j, :], rhs, w == 0, w == 1)
                            r.then_inc(S[done], 1)
                        if u == 3:
                            f_transposed(2, 6)
                        if u == 5:
                            routed(2, 7)
                        if (n_, k, i) == (1, 2, 0):
                            f_transposed(3, 4)
                        if (n_, k, i) == (2, 2, 0):
                            routed(3, 4)
                        if v >= 2:
                            for t_ in ((0,), (1,), (2, 3))[i] if (v - 2) % 4 else ((), (0, 1), (2, 3))[i]:
                                down((v - 2) // 4, (v - 2) % 4, t_)
            for k in range(NE // 2 - 2, NE // 2):
                for t_ in range(4):
                    down(PAIRS - 1, k, t_)


def kernel(**inputs):
    import numpy as _np
    import concourse.bacc as _bacc
    from concourse import mybir as _mybir
    from concourse.bass_utils import run_bass_kernel_spmd as _run

    a = {k: _np.asarray(v) for k, v in inputs.items()}
    t = {k[3:]: v for k, v in a.items() if k != "x"}

    def cat(*xs):
        return _np.concatenate(xs, axis=1)

    layers = _np.concatenate([t["tok_conv_w"].transpose(2, 0, 3, 1), t["tok_pw_w"].transpose(2, 0, 1)[:, :, None]],
                             axis=2)
    tcn_w = cat(layers.reshape(C, -1), t["tok_out1_w"].T, t["tok_out2_w"].T)
    tcn_b = cat(t["tok_conv_b"].T, t["tok_pw_b"].T, t["tok_out1_b"][:, None])
    emb = cat(t["tok_byte_embed"].T, t["tok_in_w"].T, t["tok_channel_embed"][0][:, None],
              t["tok_start_token"][:, None])
    inv = 1.0 / 10000.0 ** (_np.arange(0, HD, 2, dtype=_np.float32) / HD)
    ang = _np.outer(_np.arange(T, dtype=_np.float32), inv)
    ang = _np.concatenate([ang, ang], axis=-1)
    sign = _np.repeat(_np.array([-1.0, 1.0], _np.float32), HD // 2)
    scale = _np.repeat(_np.array([0.25] * NH + [1.0] * NKV, _np.float32), HD)[None] / FFN_SCALE
    cos_t = (_np.tile(_np.cos(ang), (1, NH + NKV)) * scale).astype(_np.float32)
    sin_t = (_np.tile(_np.sin(ang) * sign, (1, NH + NKV)) * scale).astype(_np.float32)
    arrs = {
        "x": a["x"], "tcn_w": tcn_w, "tcn_b": tcn_b, "out2_b": t["tok_out2_b"][None, :], "emb": emb,
        "in_b": t["tok_in_b"][None, :],
        "attn_q": t["attn_Q"].transpose(1, 0, 2).reshape(C, HEADS * C),
        "attn_e": t["attn_E"].transpose(0, 2, 1),
        "qkv_w": cat(t["ffn_wq"].T, t["ffn_wk"].T, t["ffn_wv"].T),
        "wo_t": t["ffn_wo"].T, "ln1": t["ffn_ln1_w"][:, None], "ln2": t["ffn_ln2_w"][:, None],
        "router": t["ffn_router_w"].T,
        "w1m": t["ffn_w1"][:, :MAIN].transpose(2, 0, 1), "w1r": t["ffn_w1"][:, MAIN:].transpose(2, 0, 1),
        "w3m": t["ffn_w3"][:, :MAIN].transpose(2, 0, 1), "w3r": t["ffn_w3"][:, MAIN:].transpose(2, 0, 1),
        "w2m": t["ffn_w2"][:, :, :MAIN].transpose(2, 0, 1), "w2r": t["ffn_w2"][:, :, MAIN:].transpose(2, 0, 1),
        "cos_t": cos_t, "sin_t": sin_t,
    }
    nc = _bacc.Bacc("TRN2", target_bir_lowering=False, num_devices=1)
    arrays, args = {}, []
    for name, v in arrs.items():
        v = _np.ascontiguousarray(v)
        arrays[f"in_{name}_dram"] = v
        args.append(nc.dram_tensor(f"in_{name}_dram", v.shape, _mybir.dt.from_np(v.dtype), kind="ExternalInput").ap())
    args.append(nc.dram_tensor("out_0_dram", (B, T, C), _mybir.dt.float32, kind="ExternalOutput").ap())
    tower(nc, *args)
    r = _run(nc, [arrays], core_ids=[0])
    return r.results[0]["out_0_dram"]
```
